# Optimizing a Trainium2 kernel written in Bass

```python
import numpy as np
import jax
import jax.numpy as jnp

def _softmax(x, axis=-1):
    return jax.nn.softmax(x, axis=axis)

def _gelu(x):
    return jax.nn.gelu(x, approximate=True)

def _silu(x):
    return jax.nn.silu(x)

def _sigmoid(x):
    return jax.nn.sigmoid(x)

def _layernorm(x, axis=-1, eps=1e-05):
    m = jnp.mean(x, axis=axis, keepdims=True)
    v = jnp.var(x, axis=axis, keepdims=True)
    return (x - m) / jnp.sqrt(v + eps)

def _scatter_add(tgt, idx, src, axis=0):
    return tgt.at[idx].add(src)

def _segment_sum(src, seg, n):
    return jax.ops.segment_sum(src, seg, n)
kernel_name = 'mk_flamingo_gated_d2_seqx_r8_394162'

def setup_inputs(seed: int=0):
    np.random.seed(seed)
    _w = jnp.asarray

    def _rec_inputs():
        import jax
        import jax.numpy as jnp
        _rk = jax.random.key(seed)
        x = -1.394e-06 + 0.9999 * jax.random.normal(jax.random.fold_in(_rk, 1), (8, 256, 128), jnp.float32)
        _lenS = 256 - jax.random.randint(jax.random.fold_in(_rk, 7), (8,), 0, max(1, 256 // 4) + 1, jnp.int32)
        _lenS2 = 256 - jax.random.randint(jax.random.fold_in(_rk, 8), (8,), 0, max(1, 256 // 4) + 1, jnp.int32)
        _ctx_1024P = jax.random.normal(jax.random.fold_in(_rk, 11), (8, 16, 128), jnp.float32)
        _ctx_1024c = jax.random.dirichlet(jax.random.fold_in(_rk, 511), 0.3 * jnp.ones((16,), jnp.float32), (8, 256))
        _ctx_1024t = jnp.einsum('bsk,bkd->bsd', _ctx_1024c, _ctx_1024P)
        _ctx_1024t = _ctx_1024t * jax.lax.rsqrt(jnp.mean(jnp.square(_ctx_1024t)) + 1e-12) * 0.953939
        ctx_1024 = -0.000292821 + 1.00034 * (_ctx_1024t + 0.3 * jax.random.normal(jax.random.fold_in(_rk, 611), (8, 256, 128), jnp.float32))
        _g = jax.random.normal(jax.random.fold_in(_rk, 9001), (2, 2), jnp.float32)
        _g = jnp.sign(_g) * jnp.maximum(jnp.abs(_g), 1.0) + (_g == 0) * 1.0
        g_xattn = _g[0]
        g_ffn = _g[1]
        return (x, ctx_1024, g_xattn, g_ffn)
    x, ctx_1024, g_xattn, g_ffn = _rec_inputs()

    def _L0_xattn_setup():
        import jax, jax.numpy as jnp
        import numpy as np
        B, N, T = (2, 256, 256)
        ENC, DEC, HID = (128, 128, 128)
        HEADS = 16
        DH = HID // HEADS
        HALF = DH // 2
        LAMBDA_INIT = 0.8
        key = jax.random.key(seed)
        ks = jax.random.split(key, 9)
        s = 0.02
        return {'encoder_feature': jax.random.normal(ks[0], (B, N, ENC), jnp.float32), 'decoder_feature': jax.random.normal(ks[1], (B, T, DEC), jnp.float32), 'Wq': jax.random.normal(ks[2], (HID, DEC), jnp.float32) * s, 'Wk': jax.random.normal(ks[3], (HID, ENC), jnp.float32) * s, 'Wv': jax.random.normal(ks[4], (HID, ENC), jnp.float32) * s, 'lambda_q1': jax.random.normal(ks[5], (HALF,), jnp.float32) * 0.1, 'lambda_q2': jax.random.normal(ks[6], (HALF,), jnp.float32) * 0.1, 'lambda_k1': jax.random.normal(ks[7], (HALF,), jnp.float32) * 0.1, 'lambda_k2': jax.random.normal(ks[8], (HALF,), jnp.float32) * 0.1}
    _L0_xattn_all = _L0_xattn_setup()
    _L0_xattn_in = {k: v for k, v in _L0_xattn_all.items() if k in ('Wq', 'Wk', 'Wv', 'lambda_q1', 'lambda_q2', 'lambda_k1', 'lambda_k2')}
    del _L0_xattn_all

    def _L0_ffn_setup():
        import jax, jax.numpy as jnp
        import numpy as np
        NUM_EXPERTS = 8
        CAPACITY = 80
        key = jax.random.key(seed)
        ks = jax.random.split(key, 5)
        D, E, F = (128, NUM_EXPERTS, 512)
        inputs = jax.random.normal(ks[0], (2, 256, D), dtype=jnp.float32)
        gate_w = jax.random.normal(ks[1], (D, E), dtype=jnp.float32) * 0.02
        gate_b = jnp.zeros((E,), dtype=jnp.float32)
        w1 = jax.random.normal(ks[2], (E, D, F), dtype=jnp.float32) * 0.02
        b1 = jnp.zeros((E, F), dtype=jnp.float32)
        w2 = jax.random.normal(ks[3], (E, F, D), dtype=jnp.float32) * 0.02
        b2 = jnp.zeros((E, D), dtype=jnp.float32)
        return {'inputs': inputs, 'gate_w': gate_w, 'gate_b': gate_b, 'w1': w1, 'b1': b1, 'w2': w2, 'b2': b2}
    _L0_ffn_all = _L0_ffn_setup()
    _L0_ffn_in = {k: v for k, v in _L0_ffn_all.items() if k in ('gate_w', 'gate_b', 'w1', 'b1', 'w2', 'b2')}
    del _L0_ffn_all

    def _L1_xattn_setup():
        import jax, jax.numpy as jnp
        import numpy as np
        DIM = 128
        H = 16
        D = 64
        INNER = H * D
        EPS = 1e-05

        def layernorm(x, w, b):
            mu = jnp.mean(x, axis=-1, keepdims=True)
            var = jnp.var(x, axis=-1, keepdims=True)
            return (x - mu) * jax.lax.rsqrt(var + EPS) * w + b
        key = jax.random.key(seed)
        ks = jax.random.split(key, 8)
        B, N, S = (4, 32, 1024)
        s = 1.0 / np.sqrt(DIM)
        return {'latents': jax.random.normal(ks[0], (B, N, DIM), jnp.float32), 'context': jax.random.normal(ks[1], (B, S, DIM), jnp.float32), 'ln_l_w': jnp.ones((DIM,), jnp.float32), 'ln_l_b': jnp.zeros((DIM,), jnp.float32), 'ln_c_w': jnp.ones((DIM,), jnp.float32), 'ln_c_b': jnp.zeros((DIM,), jnp.float32), 'Wq': jax.random.normal(ks[2], (DIM, INNER), jnp.float32) * s, 'Wkv': jax.random.normal(ks[3], (DIM, 2 * INNER), jnp.float32) * s, 'Wo': jax.random.normal(ks[4], (INNER, DIM), jnp.float32) * (1.0 / np.sqrt(INNER)), 'bo': jnp.zeros((DIM,), jnp.float32)}
    _L1_xattn_all = _L1_xattn_setup()
    _L1_xattn_in = {k: v for k, v in _L1_xattn_all.items() if k in ('ln_l_w', 'ln_l_b', 'ln_c_w', 'ln_c_b', 'Wq', 'Wkv', 'Wo', 'bo')}
    del _L1_xattn_all

    def _L1_ffn_setup():
        import jax, jax.numpy as jnp
        import numpy as np
        B, S, D, O, E, R = (8, 256, 128, 128, 8, 4)
        TOP_K = 2
        SCALING = 4.0 / 4.0
        key = jax.random.key(seed)
        k0, k1, k2, k3, k4 = jax.random.split(key, 5)
        hidden_states = jax.random.normal(k0, (B, S, D), dtype=jnp.float32)
        W_lin = jax.random.normal(k1, (O, D), dtype=jnp.float32) * 0.02
        b_lin = jnp.zeros((O,), dtype=jnp.float32)
        gate_w = jax.random.normal(k2, (E, D), dtype=jnp.float32) * 0.02
        left = jax.random.normal(k3, (E, D, R), dtype=jnp.float32) * 0.02
        right = jax.random.normal(k4, (E, R, O), dtype=jnp.float32) * 0.02
        return {'hidden_states': hidden_states, 'W_lin': W_lin, 'b_lin': b_lin, 'gate_w': gate_w, 'left': left, 'right': right}
    _L1_ffn_all = _L1_ffn_setup()
    _L1_ffn_in = {k: v for k, v in _L1_ffn_all.items() if k in ('W_lin', 'b_lin', 'gate_w', 'left', 'right')}
    del _L1_ffn_all
    return {'x': x, 'ctx_1024': ctx_1024, 'g_xattn': g_xattn, 'g_ffn': g_ffn, 'L0_xattn_Wq': _L0_xattn_in['Wq'], 'L0_xattn_Wk': _L0_xattn_in['Wk'], 'L0_xattn_Wv': _L0_xattn_in['Wv'], 'L0_xattn_lambda_q1': _L0_xattn_in['lambda_q1'], 'L0_xattn_lambda_q2': _L0_xattn_in['lambda_q2'], 'L0_xattn_lambda_k1': _L0_xattn_in['lambda_k1'], 'L0_xattn_lambda_k2': _L0_xattn_in['lambda_k2'], 'L0_ffn_gate_w': _L0_ffn_in['gate_w'], 'L0_ffn_gate_b': _L0_ffn_in['gate_b'], 'L0_ffn_w1': _L0_ffn_in['w1'], 'L0_ffn_b1': _L0_ffn_in['b1'], 'L0_ffn_w2': _L0_ffn_in['w2'], 'L0_ffn_b2': _L0_ffn_in['b2'], 'L1_xattn_ln_l_w': _L1_xattn_in['ln_l_w'], 'L1_xattn_ln_l_b': _L1_xattn_in['ln_l_b'], 'L1_xattn_ln_c_w': _L1_xattn_in['ln_c_w'], 'L1_xattn_ln_c_b': _L1_xattn_in['ln_c_b'], 'L1_xattn_Wq': _L1_xattn_in['Wq'], 'L1_xattn_Wkv': _L1_xattn_in['Wkv'], 'L1_xattn_Wo': _L1_xattn_in['Wo'], 'L1_xattn_bo': _L1_xattn_in['bo'], 'L1_ffn_W_lin': _L1_ffn_in['W_lin'], 'L1_ffn_b_lin': _L1_ffn_in['b_lin'], 'L1_ffn_gate_w': _L1_ffn_in['gate_w'], 'L1_ffn_left': _L1_ffn_in['left'], 'L1_ffn_right': _L1_ffn_in['right']}

def reference(x, ctx_1024, g_xattn, g_ffn, L0_xattn_Wq, L0_xattn_Wk, L0_xattn_Wv, L0_xattn_lambda_q1, L0_xattn_lambda_q2, L0_xattn_lambda_k1, L0_xattn_lambda_k2, L0_ffn_gate_w, L0_ffn_gate_b, L0_ffn_w1, L0_ffn_b1, L0_ffn_w2, L0_ffn_b2, L1_xattn_ln_l_w, L1_xattn_ln_l_b, L1_xattn_ln_c_w, L1_xattn_ln_c_b, L1_xattn_Wq, L1_xattn_Wkv, L1_xattn_Wo, L1_xattn_bo, L1_ffn_W_lin, L1_ffn_b_lin, L1_ffn_gate_w, L1_ffn_left, L1_ffn_right):
    import jax
    import jax.numpy as jnp

    def _L0_xattn_ref(encoder_feature, decoder_feature, Wq, Wk, Wv, lambda_q1, lambda_q2, lambda_k1, lambda_k2):
        import jax, jax.numpy as jnp
        import numpy as np
        B, N, T = (2, 256, 256)
        ENC, DEC, HID = (128, 128, 128)
        HEADS = 16
        DH = HID // HEADS
        HALF = DH // 2
        LAMBDA_INIT = 0.8
        b, n, _ = encoder_feature.shape
        _, t, _ = decoder_feature.shape
        hid = Wq.shape[0]
        dh = hid // HEADS
        half = dh // 2
        q = decoder_feature @ Wq.T
        k = encoder_feature @ Wk.T
        v = encoder_feature @ Wv.T
        q = q.reshape(b, t, 2 * HEADS, half).transpose(0, 2, 1, 3)
        k = k.reshape(b, n, 2 * HEADS, half).transpose(0, 2, 1, 3)
        v = v.reshape(b, n, HEADS, dh).transpose(0, 2, 1, 3)
        lam = jnp.exp(jnp.sum(lambda_q1 * lambda_k1)) - jnp.exp(jnp.sum(lambda_q2 * lambda_k2)) + LAMBDA_INIT
        scale = 1.0 / jnp.sqrt(jnp.float32(half))
        att = jax.nn.softmax(jnp.einsum('bhtd,bhnd->bhtn', q, k) * scale, axis=-1)
        att = att.reshape(b, HEADS, 2, t, n)
        att = att[:, :, 0] - lam * att[:, :, 1]
        out = jnp.einsum('bhtn,bhnd->bhtd', att, v)
        return out.transpose(0, 2, 1, 3).reshape(b, t, hid)

    def _L0_ffn_ref(inputs, gate_w, gate_b, w1, b1, w2, b2):
        import jax, jax.numpy as jnp
        import numpy as np
        NUM_EXPERTS = 8
        CAPACITY = 80
        D = inputs.shape[-1]
        tokens = inputs.reshape(-1, D)
        logits = tokens @ gate_w + gate_b
        probs = jax.nn.softmax(logits, axis=-1)
        expert_idx = jnp.argmax(probs, axis=-1)
        mask1 = jax.nn.one_hot(expert_idx, NUM_EXPERTS, dtype=jnp.float32)
        pos = jnp.sum(jnp.cumsum(mask1, axis=0) * mask1, axis=-1) - 1.0
        pos = pos.astype(jnp.int32)
        keep = (pos < CAPACITY).astype(jnp.float32)
        gate_prob = jnp.sum(probs * mask1, axis=-1)
        pos_oh = jax.nn.one_hot(pos, CAPACITY, dtype=jnp.float32)
        sec_mask = mask1[:, :, None] * pos_oh[:, None, :] * keep[:, None, None]
        combine_weights = sec_mask * gate_prob[:, None, None]
        dispatch = jnp.einsum('nec,nd->ecd', sec_mask, tokens)
        h = jax.nn.gelu(jnp.einsum('ecd,edf->ecf', dispatch, w1) + b1[:, None, :])
        expert_out = jnp.einsum('ecf,efd->ecd', h, w2) + b2[:, None, :]
        out = jnp.einsum('nec,ecd->nd', combine_weights, expert_out)
        return out.reshape(inputs.shape)

    def _L1_xattn_ref(latents, context, ln_l_w, ln_l_b, ln_c_w, ln_c_b, Wq, Wkv, Wo, bo):
        import jax, jax.numpy as jnp
        import numpy as np
        DIM = 128
        H = 16
        D = 64
        INNER = H * D
        EPS = 1e-05

        def layernorm(x, w, b):
            mu = jnp.mean(x, axis=-1, keepdims=True)
            var = jnp.var(x, axis=-1, keepdims=True)
            return (x - mu) * jax.lax.rsqrt(var + EPS) * w + b
        b, n, _ = latents.shape
        s = context.shape[1]
        lat = layernorm(latents, ln_l_w, ln_l_b)
        ctx = layernorm(context, ln_c_w, ln_c_b)
        q = (lat @ Wq).reshape(b, n, H, D).transpose(0, 2, 1, 3)
        kv = ctx @ Wkv
        k, v = jnp.split(kv, 2, axis=-1)
        k = k.reshape(b, s, H, D).transpose(0, 2, 1, 3)
        v = v.reshape(b, s, H, D).transpose(0, 2, 1, 3)
        scale = D ** (-0.5)
        attn = jnp.einsum('bhnd,bhsd->bhns', q, k) * scale
        attn = jnp.clip(attn, -11.0, 11.0)
        attn = jax.nn.softmax(attn, axis=-1)
        out = jnp.einsum('bhns,bhsd->bhnd', attn, v)
        out = out.transpose(0, 2, 1, 3).reshape(b, n, INNER)
        return out @ Wo + bo

    def _L1_ffn_ref(hidden_states, W_lin, b_lin, gate_w, left, right):
        import jax, jax.numpy as jnp
        import numpy as np
        B, S, D, O, E, R = (8, 256, 128, 128, 8, 4)
        TOP_K = 2
        SCALING = 4.0 / 4.0
        bsz, seq, d_in = hidden_states.shape
        x = hidden_states.reshape(-1, d_in)
        logits = x @ gate_w.T
        scores = jax.nn.softmax(logits, axis=-1)
        weights, idx = jax.lax.top_k(scores, TOP_K)
        base = x @ W_lin.T + b_lin
        left_sel = left[idx]
        right_sel = right[idx]
        t = jnp.einsum('nd,nkdr->nkr', x, left_sel)
        out_k = jnp.einsum('nkr,nkro->nko', t, right_sel)
        lora = jnp.sum(weights[..., None] * out_k, axis=1) * SCALING
        return (base + lora).reshape(bsz, seq, -1)
    x = x + jnp.tanh(g_xattn[0]) * _L0_xattn_ref(ctx_1024, _layernorm(x, axis=-1), L0_xattn_Wq, L0_xattn_Wk, L0_xattn_Wv, L0_xattn_lambda_q1, L0_xattn_lambda_q2, L0_xattn_lambda_k1, L0_xattn_lambda_k2)
    x = x + jnp.tanh(g_ffn[0]) * _L0_ffn_ref(_layernorm(x, axis=-1), L0_ffn_gate_w, L0_ffn_gate_b, L0_ffn_w1, L0_ffn_b1, L0_ffn_w2, L0_ffn_b2)
    x = x + jnp.tanh(g_xattn[1]) * _L1_xattn_ref(_layernorm(x, axis=-1), ctx_1024, L1_xattn_ln_l_w, L1_xattn_ln_l_b, L1_xattn_ln_c_w, L1_xattn_ln_c_b, L1_xattn_Wq, L1_xattn_Wkv, L1_xattn_Wo, L1_xattn_bo)
    x = x + jnp.tanh(g_ffn[1]) * _L1_ffn_ref(_layernorm(x, axis=-1), L1_ffn_W_lin, L1_ffn_b_lin, L1_ffn_gate_w, L1_ffn_left, L1_ffn_right)
    return x

_drawn_inputs = setup_inputs


def setup_inputs(seed=0):
    import zlib

    import numpy as np

    out = dict(_drawn_inputs(seed))
    spreads = {'g_ffn': (-1.0, 0.6),
     'L0_ffn_gate_b': (0.0, 0.8),
     'L0_ffn_b1': (0.0, 0.8),
     'L0_ffn_b2': (0.0, 0.8),
     'L1_xattn_ln_l_w': (1.0, 0.6),
     'L1_xattn_ln_l_b': (0.0, 0.514),
     'L1_xattn_ln_c_w': (1.0, 0.2),
     'L1_xattn_ln_c_b': (0.0, 0.1),
     'L1_xattn_bo': (0.0, 0.1),
     'L1_ffn_b_lin': (0.0, 0.1)}
    factors = {'L0_xattn_Wq': 8.0,
     'L0_xattn_Wk': 8.0,
     'L0_xattn_Wv': 3.477,
     'L0_xattn_lambda_q1': 8.0,
     'L0_xattn_lambda_q2': 8.0,
     'L0_xattn_lambda_k1': 8.0,
     'L0_xattn_lambda_k2': 8.0,
     'L0_ffn_gate_w': 7.926,
     'L0_ffn_w1': 8.0,
     'L0_ffn_w2': 8.0,
     'L1_ffn_gate_w': 8.0,
     'L1_ffn_left': 8.0,
     'L1_ffn_right': 8.0}
    for name, (base, spread) in spreads.items():
        noise = np.random.default_rng([zlib.crc32(name.encode()), seed]).standard_normal(out[name].shape)
        drawn = base * np.exp(spread * noise) if base else spread * noise
        out[name] = jnp.asarray(drawn.astype(out[name].dtype))
    for name, factor in factors.items():
        out[name] = (out[name] * factor).astype(out[name].dtype)
    return out
```

```python
from contextlib import ExitStack

import concourse.bass as bass
from concourse import mybir

F32 = mybir.dt.float32
BF16 = mybir.dt.bfloat16
F16 = mybir.dt.float16
ALU = mybir.AluOpType
ACT = mybir.ActivationFunctionType
AX = mybir.AxisListType

P = 128
BATCH, SEQ, DIM = 8, 256, 128
TILES = BATCH * SEQ // P
TPB = SEQ // P
BANK = 512
TPK = BANK // P
CHUNKS = TILES // TPK
EPS = 1e-5

SUBW, HEADS_A, HEADW_A = 4, 16, 8
ROWT, GROUPS = 4, 8
Q_PARTS = (0, 0, 0, 1, 1, 2)
K_PARTS = (0, 1, 2, 0, 1, 0)
PAIRS = len(Q_PARTS)
KROWS = PAIRS * SUBW
MROWS = 2
SLOTS = 3
VPARTS = 3
VCOLS = VPARTS * HEADW_A + 1
LAMBDA_INIT = 0.8
SCALE_A = SUBW ** -0.5
PRING = 8
LAG = 4
A_TILES = ROWT * GROUPS
B_TILES = 2 * GROUPS
QUARTER = 4
HALF = GROUPS // 2
LOADS = 2 * ROWT + 1
COMBINE_LINKS = 7

EXPERTS, CAP, FF = 8, 80, 512
FCH = FF // P
EROWS = EXPERTS * CAP
ECH = EROWS // P
EHALF = EROWS // 2


def lo_on_vector(bt):
    return bt % 4 == 3


LO_V = sum(lo_on_vector(t) for t in range(B_TILES))
LO_G = B_TILES - LO_V

WIDE, HEADS_B, HEADW_B = 1024, 16, 64
PAIRS_B = HEADS_B // 2
SCALE_B = HEADW_B ** -0.5
CLIP = 11.0
RING_B = 4
JOBS_B = 12
JOBS_AT = (0, 2, 2, 2, 2, 2, 1, 1)
LINKS_B = 1

RANK = 4
ER = EXPERTS * RANK


class Chain:

    def __init__(self, eng, sem):
        self.eng, self.sem, self.n, self.base = eng, sem, 0, 0

    def link(self, ins):
        ins.then_inc(self.sem, 1)
        self.n += 1
        self.eng.wait_ge(self.sem, self.base + self.n)


def batches(eng, step, chain=None, links=0):
    step(0, 0, 0, True, False)
    turns = (BATCH - 2) // SLOTS
    with eng.Fori(0, turns) as i:
        if chain:
            start, chain.base = chain.n, i * (SLOTS * links)
        for j in range(1, SLOTS + 1):
            step(i * SLOTS + j, j % SLOTS, i + j // SLOTS, False, False)
    if chain:
        assert chain.n - start == SLOTS * links
        chain.n, chain.base = start + turns * SLOTS * links, 0
    step(BATCH - 1, (BATCH - 1) % SLOTS, (BATCH - 1) // SLOTS, False, True)


def batch_pairs(eng, step, chain=None, links=0):
    step(0, 0, True, False)
    turns = (BATCH - 2) // 2
    with eng.Fori(0, turns) as i:
        if chain:
            start, chain.base = chain.n, i * (2 * links)
        for j in (1, 2):
            step(i * 2 + j, j % 2, False, False)
    if chain:
        assert chain.n - start == 2 * links
        chain.n, chain.base = start + turns * 2 * links, 0
    step(BATCH - 1, (BATCH - 1) % 2, False, True)


def build(nc, I, out):
    with ExitStack() as ctx:
        def sb(name, shape, dt=F32, scope=ctx):
            return scope.enter_context(nc.sbuf_tensor(name, shape, dt))

        def sem(name):
            return ctx.enter_context(nc.semaphore(name))

        ps = ctx.enter_context(nc.psum_tensor("ps", [P, 8, BANK], F32))
        BANK_A, BANK_B, BANK_O, BANK_M = (0, 1), (2, 4), 6, 7

        ident = sb("ident", [P, P])
        identb = sb("identb", [P, P], BF16)
        x = sb("x", [P, TILES, DIM])
        cx = sb("cx", [P, TILES, DIM])
        eps = sb("eps", [P, 1])
        stat = sb("stat", [P, TILES, 6])
        mv = sb("mv", [P, TILES, 2])
        std = sb("std", [P, TILES])
        rstd = sb("rstd", [P, TILES])
        cT = sb("cT", [P, TILES, P])
        w3 = sb("w3", [P, 3, DIM])
        w3T = sb("w3T", [P, 3, DIM])
        lam_in = sb("lam_in", [P, 4, SUBW])
        lam_pr = sb("lam_pr", [P, 2, SUBW])
        lam_s = sb("lam_s", [P, 2])
        lam_e = sb("lam_e", [P, 2])
        gates = sb("gates", [P, 4])
        tg = sb("tg", [P, 4])
        lam = sb("lam", [P, 1])
        coef = sb("coef", [P, 2])

        wq1 = sb("wq1", [P, WIDE])
        wkv1 = sb("wkv1", [P, 2 * WIDE])
        wo1 = sb("wo1", [P, PAIRS_B, DIM])
        lnf = sb("lnf", [P, 4])
        bo1 = sb("bo1", [P, DIM])
        wl_in, gw_in = sb("wl_in", [P, DIM]), sb("gw_in", [EXPERTS, DIM])
        wlT = sb("wlT", [P, DIM])
        gl = sb("gl", [P, EXPERTS + ER])
        right_b = sb("right_b", [ER + 1, DIM])
        gate_w, gate_b = sb("gate_w", [P, EXPERTS]), sb("gate_b", [P, EXPERTS])
        b1_in, b1T = sb("b1_in", [EXPERTS * FCH, P]), sb("b1T", [P, EXPERTS * FCH])
        b2_in, b2T = sb("b2_in", [EXPERTS, P]), sb("b2T", [P, EXPERTS])
        w1 = sb("w1", [P, EXPERTS, FF])
        w2 = sb("w2", [P, EXPERTS * FCH, DIM])
        iota_e = sb("iota_e", [P, TILES, EXPERTS])
        place0 = sb("place0", [P, EXPERTS, TILES])
        keep_sum = sb("keep_sum", [P, EXPERTS, TILES])
        places = sb("places", [P, EROWS], F16)
        place_p = sb("place_p", [P, ECH])
        before = sb("before", [P, P], BF16)
        onesb = sb("onesb", [P, P], BF16)
        onesh = sb("onesh", [P, P], F16)
        attn0, ffn0 = ExitStack(), ExitStack()
        vp = sb("vp", [P, TILES, HEADS_A, VCOLS], BF16, attn0)
        qaug = [sb(f"qaug{i}", [P, GROUPS, SEQ], BF16, attn0) for i in range(SLOTS)]
        kaug = [sb(f"kaug{i}", [P, GROUPS, SEQ], BF16, attn0) for i in range(SLOTS)]
        vbuf = [sb(f"vbuf{i}", [P, TPB, HEADS_A, VCOLS], BF16, attn0) for i in range(SLOTS)]
        nmax = [sb(f"nmax{i}", [P, TPB, ROWT, HALF], F32, attn0) for i in range(2)]
        mpart = [sb(f"mpart{i}", [P, TPB, ROWT, MROWS, HALF], BF16, attn0) for i in range(2)]
        mT = [sb(f"mT{i}", [ROWT * MROWS * HALF, SEQ], BF16, attn0) for i in range(2)]

        ov = sb("ov", [P, TPB * ROWT * 4, 2, HEADW_A], F32, attn0)
        rs = sb("rs", [P, TPB * ROWT * 4, 2], F32, attn0)

        early, loop_a = ExitStack(), ExitStack()
        xn = sb("xn", [P, TILES, DIM], F32, early)
        xT = sb("xT", [P, TILES, P], F32, early)
        qk32 = sb("qk32", [P, 2, TILES * P], F32, early)
        parts = sb("parts", [P, 2, 3, TILES * P], BF16, early)
        res = sb("res", [P, 2, BANK], F32, early)
        v32 = sb("v32", [P, TILES, DIM], F32, early)
        vres = xn
        early.close()
        pexp = [sb(f"pexp{i}", [P, 2, TPB, SEQ], F32, loop_a) for i in range(PRING)]
        plo = [sb(f"plo{i}", [P, 2, TPB, SEQ], F16, loop_a) for i in range(PRING)]
        oraw = [sb(f"oraw{i}", [P, TPB * ROWT, 4, 2 * VCOLS], F32, loop_a) for i in range(SLOTS)]
        loop_a.close()
        attn0.close()
        xn1 = sb("xn1", [P, TILES, DIM], F32, ffn0)
        xT1 = sb("xT1", [P, TILES, P], F32, ffn0)
        lg = sb("lg", [P, TILES, EXPERTS], F32, ffn0)
        ne = sb("ne", [P, TILES, EXPERTS], F32, ffn0)
        t16 = sb("t16", [P, TILES], F32, ffn0)
        gprob = sb("gprob", [P, TILES], F32, ffn0)
        mask = sb("mask", [P, EXPERTS, TILES], BF16, ffn0)
        upto = sb("upto", [P, EXPERTS, TILES], F32, ffn0)
        prior = sb("prior", [P, EXPERTS, TILES], BF16, ffn0)
        over = sb("over", [P, EXPERTS, TILES], F32, ffn0)
        place = sb("place", [P, TILES], F32, ffn0)
        onehot = [sb(f"onehot{i}", [P, EROWS], F32, ffn0) for i in range(4)]
        diag = sb("diag", [P, TILES, P], F16, ffn0)
        place_row = sb("place_row", [P, TILES * P], F16, ffn0)
        onehotT = sb("onehotT", [P, ECH, TILES * P], BF16, ffn0)
        tokT = sb("tokT", [P, EROWS], F32, ffn0)
        hpre = sb("hpre", [P, EXPERTS * FCH, CAP], F32, ffn0)
        hact = sb("hact", [P, EXPERTS * FCH, CAP], F32, ffn0)
        yT = sb("yT", [P, EROWS], F32, ffn0)
        yrow = sb("yrow", [P, ECH, P], F32, ffn0)
        ypart = sb("ypart", [P, 3, ECH, P], BF16, ffn0)
        yres = sb("yres", [P, ECH, P], F32, ffn0)
        ffn0.close()
        attn1 = ExitStack()
        xn2 = sb("xn2", [P, TILES, DIM], F32, attn1)
        latT = sb("latT", [P, TILES, P], F32, attn1)
        lat_b = [sb(f"lat_b{i}", [P, SEQ], F32, attn1) for i in range(2)]
        ctx_b = [sb(f"ctx_b{i}", [P, SEQ], F32, attn1) for i in range(2)]
        qT = [sb(f"qT{i}", [P, PAIRS_B, SEQ], F32, attn1) for i in range(2)]
        kT = [sb(f"kT{i}", [P, PAIRS_B, SEQ], F32, attn1) for i in range(2)]
        v1 = [sb(f"v1_{i}", [P, TPB, HEADS_B, HEADW_B + 1], F32, attn1) for i in range(2)]
        pclip = [sb(f"pclip{i}", [P, 2, TPB, SEQ], F32, attn1) for i in range(RING_B)]
        rsum = [sb(f"rsum{i}", [P, TPB * 2], F32, attn1) for i in range(2)]
        on = [sb(f"on{i}", [P, TPB * 2, HEADW_B], F32, attn1) for i in range(2)]
        oT = [sb(f"oT{i}", [P, PAIRS_B, SEQ], F32, attn1) for i in range(2)]
        ysum = sb("ysum", [P, TPB, DIM], F32, attn1)
        attn1.close()
        ffn1 = ExitStack()
        xn3 = sb("xn3", [P, TILES, DIM], F32, ffn1)
        xT3 = sb("xT3", [P, TILES, P], F32, ffn1)
        lt = sb("lt", [P, TILES, EXPERTS + ER], F32, ffn1)
        sc = sb("sc", [P, TILES, EXPERTS], F32, ffn1)
        rest = sb("rest", [P, TILES, EXPERTS], F32, ffn1)
        cand = sb("cand", [P, TILES, EXPERTS], F32, ffn1)
        best = sb("best", [P, 2, TILES, EXPERTS], F32, ffn1)
        u16 = sb("u16", [P, TILES], F32, ffn1)
        tw = sb("tw", [P, TILES, ER], F32, ffn1)
        twT = sb("twT", [ER + 1, TILES * P], F32, ffn1)
        ffn1.close()
        qk_dram = nc.dram_tensor("qk_dram", [2, ROWT, PAIRS, SUBW * GROUPS, TILES * P], BF16).ap()

        ld_x, ld_c, ld_w, ld_small = sem("ld_x"), sem("ld_c"), sem("ld_w"), sem("ld_small")
        out_stored = sem("out_stored")
        dve_self, act_self, pool_self = sem("dve_self"), sem("act_self"), sem("pool_self")
        consts_ready = sem("consts_ready")
        ones_ready = sem("ones_ready")
        var_ready, std_ready, xn_ready = sem("var_ready"), sem("std_ready"), sem("xn_ready")
        job_full, job_out = sem("job_full"), sem("job_out")
        qk_split, qk_stored = sem("qk_split"), sem("qk_stored")
        v_cast, v_split = sem("v_cast"), sem("v_split")
        lam_sum, lam_exp, coef_ready = sem("lam_sum"), sem("lam_exp"), sem("coef_ready")
        aug_loaded = [sem(f"aug_loaded{i}") for i in range(SLOTS)]
        m_loaded = [[sem(f"m_loaded{i}_{h}") for h in range(2)] for i in range(SLOTS)]
        a_full, a_used = sem("a_full"), sem("a_used")
        b_full, exp_done = sem("b_full"), sem("exp_done")
        lo_pool, lo_dve = sem("lo_pool"), sem("lo_dve")
        pv_done, o_saved = sem("pv_done"), sem("o_saved")
        m_split, m_turned, m_copied = sem("m_split"), sem("m_turned"), sem("m_copied")
        ld_ffn = sem("ld_ffn")
        x1_ready = sem("x1_ready")
        ffn_consts = sem("ffn_consts")
        bT_full, bT_out = sem("bT_full"), sem("bT_out")
        xT_full, xT_out = sem("xT_full"), sem("xT_out")
        logits_full, logits_max, logits_exp = sem("logits_full"), sem("logits_max"), sem("logits_exp")
        mask_ready, rank_full, diag_ready = sem("mask_ready"), sem("rank_full"), sem("diag_ready")
        onehot_ready, onehot_used = sem("onehot_ready"), sem("onehot_used")
        row_full, row_out, onehotT_ready = sem("row_full"), sem("row_out"), sem("onehotT_ready")
        tok_full, tok_out = sem("tok_full"), sem("tok_out")
        h_full, h_biased, h_ready = sem("h_full"), sem("h_biased"), sem("h_ready")
        y_full, y_biased, yrow_full, yrow_out, y_split = sem("y_full"), sem("y_biased"), sem("yrow_full"), sem("yrow_out"), sem("y_split")
        moe_full, moe_used = sem("moe_full"), sem("moe_used")
        x2_ready = sem("x2_ready")
        ld_l1 = sem("ld_l1")
        ones1_ready = sem("ones1_ready")
        ctxT_full, ctxT_out = sem("ctxT_full"), sem("ctxT_out")
        batch_loaded = [sem(f"batch_loaded{i}") for i in range(2)]
        proj_full, proj_act, proj_dve = sem("proj_full"), sem("proj_act"), sem("proj_dve")
        s_full, s_exp, s_clip = sem("s_full"), sem("s_exp"), sem("s_clip")
        o_full, o_norm, oT_full, oT_out = sem("o_full"), sem("o_norm"), sem("oT_full"), sem("oT_out")
        out_full, out_used = sem("out_full"), sem("out_used")
        x3_ready = sem("x3_ready")
        ld_f1 = sem("ld_f1")
        w1T_full, w1T_out = sem("w1T_full"), sem("w1T_out")
        lt_full, lt_out = sem("lt_full"), sem("lt_out")
        sc_shifted, sc_exp, tw_ready = sem("sc_shifted"), sem("sc_exp"), sem("tw_ready")
        twT_full, twT_out, twT_ones = sem("twT_full"), sem("twT_out"), sem("twT_ones")
        lin_full, lin_used = sem("lin_full"), sem("lin_used")

        block = ctx.enter_context(nc.Block())

        JOBS = [("w", 0)] + [("xT", c) for c in range(CHUNKS)] + [("cT", c) for c in range(CHUNKS)]
        for c in range(CHUNKS):
            JOBS += [("q", c), ("k", c)]
        JOBS += [("v", c) for c in range(CHUNKS)]
        job_at = {job: n for n, job in enumerate(JOBS)}

        def hi_of(k):
            return pexp[k % PRING][:].bitcast(BF16).rearrange("p r n (t two) -> p r n t two", two=2)[:, :, :, :, 1]

        def proj_src(n):
            if n < 8:
                return ps[:, 7, :].rearrange("p (m t) -> p m t", m=2)
            return ps[:, 7, :].rearrange("p (h d) -> p h d", d=HEADW_B)

        def proj_dst(par, n):
            if n < 8:
                return (qT if n < 4 else kT)[par][:, 2 * (n % 4):2 * (n % 4) + 2, :]
            t, half = divmod(n - 8, 2)
            return v1[par][:, t, 8 * half:8 * half + 8, 0:HEADW_B]

        def head_bank(k):
            return BANK_B[k % 2]

        @block.sync
        def _(sp):
            tok = lambda ap: ap.rearrange("b (t p) d -> p (b t) d", p=P)
            for c in range(CHUNKS):
                sp.dma_start(x[:, TPK * c:TPK * c + TPK, :], tok(I["x"])[:, TPK * c:TPK * c + TPK, :]).then_inc(ld_x, 16)
            for k, n in enumerate(("Wq", "Wk", "Wv")):
                sp.dma_start(w3[:, k, :], I["L0_xattn_" + n]).then_inc(ld_w, 16)
            sp.dma_start(cx[:], tok(I["ctx_1024"])).then_inc(ld_c, 16)
            for k, n in enumerate(("lambda_q1", "lambda_k1", "lambda_q2", "lambda_k2")):
                sp.dma_start(lam_in[:, k, :], I["L0_xattn_" + n].partition_broadcast(P)).then_inc(ld_small, 16)
            for k, n in enumerate(("g_xattn", "g_ffn")):
                sp.dma_start(gates[:, 2 * k:2 * k + 2], I[n].partition_broadcast(P)).then_inc(ld_small, 16)
            sp.dma_start(gate_w[:], I["L0_ffn_gate_w"]).then_inc(ld_ffn, 16)
            sp.dma_start(gate_b[:], I["L0_ffn_gate_b"].partition_broadcast(P)).then_inc(ld_ffn, 16)
            sp.dma_start(b1_in[:], I["L0_ffn_b1"].rearrange("e (c f) -> (e c) f", f=P)).then_inc(ld_ffn, 16)
            sp.dma_start(b2_in[:], I["L0_ffn_b2"]).then_inc(ld_ffn, 16)
            sp.dma_start(w1[:], I["L0_ffn_w1"].rearrange("e d f -> d e f")).then_inc(ld_ffn, 16)
            sp.dma_start(w2[:], I["L0_ffn_w2"].rearrange("e (c f) d -> f (e c) d", f=P)).then_inc(ld_ffn, 16)
            sp.dma_start(wq1[:], I["L1_xattn_Wq"]).then_inc(ld_l1, 16)
            sp.dma_start(wkv1[:], I["L1_xattn_Wkv"]).then_inc(ld_l1, 16)
            sp.dma_start(wo1[:], I["L1_xattn_Wo"].rearrange("(m p) d -> p m d", p=P)).then_inc(ld_l1, 16)
            for k, n in enumerate(("ln_l_w", "ln_l_b", "ln_c_w", "ln_c_b")):
                sp.dma_start(lnf[:, k:k + 1], I["L1_xattn_" + n].rearrange("(d o) -> d o", o=1)).then_inc(ld_l1, 16)
            sp.dma_start(bo1[:], I["L1_xattn_bo"].partition_broadcast(P)).then_inc(ld_l1, 16)
            sp.dma_start(wl_in[:], I["L1_ffn_W_lin"]).then_inc(ld_f1, 16)
            sp.dma_start(gw_in[:], I["L1_ffn_gate_w"]).then_inc(ld_f1, 16)
            sp.dma_start(gl[:, EXPERTS:].rearrange("p (e r) -> p e r", r=RANK),
                         I["L1_ffn_left"].rearrange("e d r -> d e r")).then_inc(ld_f1, 16)
            sp.dma_start(right_b[0:ER, :], I["L1_ffn_right"].rearrange("e r o -> (e r) o")).then_inc(ld_f1, 16)
            sp.dma_start(right_b[ER:ER + 1, :], I["L1_ffn_b_lin"].rearrange("(a d) -> a d", a=1)).then_inc(ld_f1, 16)
            for c in range(CHUNKS):
                cols = slice(BANK * c, BANK * c + BANK)
                for side, which in enumerate((Q_PARTS, K_PARTS)):
                    sp.wait_ge(qk_split, 2 * c + side + 1)
                    for pair, part in enumerate(which):
                        sp.dma_start(qk_dram[side, :, pair, :, cols], parts[:, side, part, cols]).then_inc(qk_stored, 16)
            sp.wait_ge(qk_stored, 16 * 2 * PAIRS * CHUNKS)
            sp.wait_ge(v_split, 1)
            sp.wait_ge(ones_ready, 1)

            def load_batch(b, s):
                for side, aug in enumerate((qaug[s], kaug[s])):
                    for r in range(ROWT):
                        row = P // ROWT * r
                        src = qk_dram[side, r, :, :, bass.ds(b * SEQ, SEQ)].rearrange(
                            "c (d g) t -> (c d) g t", g=GROUPS)
                        sp.dma_start(aug[row:row + KROWS, :, :], src).then_inc(aug_loaded[s], 16)
                sp.dma_start(vbuf[s][:], vp[:, bass.ds(b * TPB, TPB), :, :]).then_inc(aug_loaded[s], 16)

            def m_rows(b, s, half):
                sp.wait_ge(m_copied, b * 2 + half + 1)
                for r in range(ROWT):
                    row = P // ROWT * r + KROWS
                    sp.dma_start(qaug[s][row:row + MROWS, HALF * half:HALF * half + HALF, :],
                                 mT[half][r * MROWS * HALF:(r + 1) * MROWS * HALF, :]).then_inc(m_loaded[s][half], 16)

            load_batch(0, 0)
            load_batch(1, 1)
            m_rows(0, 0, 0)
            m_rows(0, 0, 1)

            m_rows(1, 1, 0)
            load_batch(2, 2)
            with sp.Fori(0, (BATCH - 2) // SLOTS) as i:
                for j in range(1, SLOTS + 1):
                    b = i * SLOTS + j
                    m_rows(b, j % SLOTS, 1)
                    m_rows(b + 1, (j + 1) % SLOTS, 0)
                    sp.wait_ge(pv_done, b * B_TILES)
                    load_batch(b + 2 if j < SLOTS else i * 2 + 5, (j + 2) % SLOTS)
            m_rows(BATCH - 1, (BATCH - 1) % SLOTS, 1)

            def load_tokens(b, par):
                for src, dst in ((latT, lat_b), (cT, ctx_b)):
                    sp.dma_start(dst[par][:].rearrange("p (t n) -> p t n", n=P),
                                 src[:, bass.ds(b * TPB, TPB), :]).then_inc(batch_loaded[par], 16)

            sp.wait_ge(ctxT_out, CHUNKS)
            sp.wait_ge(xT_out, 2 * CHUNKS)
            load_tokens(0, 0)
            load_tokens(1, 1)
            with sp.Fori(0, (BATCH - 2) // 2) as i:
                for j in range(2):
                    sp.wait_ge(proj_full, i * (2 * JOBS_B) + (j + 1) * JOBS_B)
                    load_tokens(i * 2 + (j + 2), j)
            for c in range(CHUNKS):
                sp.wait_ge(lin_used, TPK * (c + 1))
                sp.dma_start(tok(out)[:, TPK * c:TPK * c + TPK, :], x[:, TPK * c:TPK * c + TPK, :]).then_inc(out_stored, 16)
            sp.wait_ge(out_stored, 16 * CHUNKS)

        @block.gpsimd
        def _(pool):
            c = Chain(pool, pool_self)
            c.link(nc.gpsimd.memset(ident[:], 0.0))
            c.link(nc.gpsimd.affine_select(out=ident[:], in_=ident[:], compare_op=ALU.not_equal, fill=1.0, base=0,
                                           pattern=[[-1, P]], channel_multiplier=1))
            nc.gpsimd.tensor_copy(identb[:], ident[:]).then_inc(consts_ready, 1)
            for s in range(SLOTS):
                nc.gpsimd.memset(qaug[s][:], 1.0)
                nc.gpsimd.memset(kaug[s][:], 1.0)
            nc.gpsimd.memset(vp[:, :, :, VCOLS - 1:VCOLS], 1.0).then_inc(ones_ready, 1)

            nc.gpsimd.iota(iota_e[:], [[0, TILES], [1, EXPERTS]], base=0, channel_multiplier=0, allow_small_or_imprecise_dtypes=True)
            nc.gpsimd.iota(place0[:], [[CAP, EXPERTS], [0, TILES]], base=0, channel_multiplier=0, allow_small_or_imprecise_dtypes=True)
            nc.gpsimd.iota(places[:], [[1, EROWS]], base=0, channel_multiplier=0, allow_small_or_imprecise_dtypes=True)
            nc.gpsimd.iota(place_p[:], [[P, ECH]], base=0, channel_multiplier=1, allow_small_or_imprecise_dtypes=True)
            nc.gpsimd.memset(onesh[:], 1.0)
            nc.gpsimd.memset(onesb[:], 1.0)
            c.link(nc.gpsimd.memset(keep_sum[:], 1.0))
            c.link(nc.gpsimd.memset(keep_sum[:, :, 0:1], 0.0))
            nc.gpsimd.affine_select(out=before[:], in_=onesb[:], compare_op=ALU.is_gt, fill=0.0, base=0,
                                    pattern=[[1, P]], channel_multiplier=-1).then_inc(ffn_consts, 1)

            def step(b, s, turn, first, last):
                for k in range(B_TILES):
                    if not lo_on_vector(k):
                        pool.wait_ge(exp_done, b * B_TILES + k + 1)
                        nc.gpsimd.tensor_tensor(plo[k % PRING][:], pexp[k % PRING][:], hi_of(k), ALU.subtract).then_inc(lo_pool, 1)

            batches(pool, step)
            pool.wait_ge(x2_ready, 1)
            for par in range(2):
                last = nc.gpsimd.memset(v1[par][:, :, :, HEADW_B:HEADW_B + 1], 1.0)
            last.then_inc(ones1_ready, 1)
            pool.wait_ge(x3_ready, 1)
            nc.gpsimd.memset(twT[ER:ER + 1, :], 1.0).then_inc(twT_ones, 1)

        @block.tensor
        def _(pe):
            pe.wait_ge(consts_ready, 1)
            for n, (what, c) in enumerate(JOBS):
                bank = ps[:, n % 8, :]
                if n >= 8:
                    pe.wait_ge(job_out, n - 7)
                if what == "w":
                    pe.wait_ge(ld_w, 48)
                    for k in range(3):
                        mm = nc.tensor.transpose(bank[:, P * k:P * k + P], w3[:, k, :], ident[:])
                elif what in ("xT", "cT"):
                    if what == "xT":
                        pe.wait_ge(xn_ready, c + 1)
                    else:
                        pe.wait_ge(ld_c, 16)
                    src = xn if what == "xT" else cx
                    for t in range(TPK):
                        mm = nc.tensor.transpose(bank[:, P * t:P * t + P], src[:, TPK * c + t, :], ident[:])
                else:
                    need = {"q": ("xT", c), "k": ("cT", c), "v": ("cT", c)}[what]
                    pe.wait_ge(job_out, job_at[need] + 1)
                    if what == "v":
                        for t in range(TPK):
                            mm = nc.tensor.matmul(bank[:, P * t:P * t + P], cT[:, TPK * c + t, :], w3T[:, 2, :],
                                                  start=True, stop=True)
                    else:
                        src = (xT if what == "q" else cT)[:, TPK * c:TPK * c + TPK, :]
                        mm = nc.tensor.matmul(bank, w3T[:, 0 if what == "q" else 1, :], src, start=True, stop=True)
                mm.then_inc(job_full, 1)

            def score_a(b, s, a):
                g, r = a // ROWT, a % ROWT
                if not (isinstance(b, int) and b * A_TILES + a < 2):
                    pe.wait_ge(a_used, b * A_TILES + (a - 1))
                rows = slice(P // ROWT * r, P // ROWT * r + KROWS)
                for t in range(TPB):
                    mm = nc.tensor.matmul(ps[:, BANK_A[a % 2], SEQ * t:SEQ * t + SEQ],
                                          qaug[s][rows, g, P * t:P * t + P], kaug[s][rows, g, :],
                                          start=True, stop=True)
                mm.then_inc(a_full, 1)

            def turn_max(b, half):
                pe.wait_ge(m_split, b * 2 + half + 1)
                if not (isinstance(b, int) and b * 2 + half < 1):
                    pe.wait_ge(m_copied, b * 2 + half)
                for t in range(TPB):
                    mm = nc.tensor.transpose(
                        ps[0:ROWT * MROWS * HALF, BANK_M, 0:SEQ // 2].bitcast(BF16)[:, P * t:P * t + P],
                        mpart[half][:, t, :, :, :], identb[:])
                mm.then_inc(m_turned, 1)

            def score_b(b, s, turn, k):
                g = k // 2
                if k == 0:
                    pe.wait_ge(aug_loaded[s], (turn + 1) * (16 * LOADS))
                    pe.wait_ge(m_loaded[s][0], (turn + 1) * (16 * ROWT))
                if k == B_TILES // 2:
                    pe.wait_ge(m_loaded[s][1], (turn + 1) * (16 * ROWT))
                if not (isinstance(b, int) and b * B_TILES + k < 2):
                    pe.wait_ge(exp_done, b * B_TILES + (k - 1))
                for t in range(TPB):
                    for r in range(2):
                        row = P // ROWT * (2 * (k % 2) + r)
                        rows = slice(row, row + KROWS + MROWS)
                        mm = nc.tensor.matmul(ps[:, head_bank(k) + r, SEQ * t:SEQ * t + SEQ],
                                              kaug[s][rows, g, P * t:P * t + P], qaug[s][rows, g, :],
                                              start=True, stop=True)
                mm.then_inc(b_full, 1)

            def times_v(b, s, k):
                idx = b * B_TILES
                pe.wait_ge(exp_done, idx + (k + 1))
                g, q = k // 2, k // QUARTER
                dve_lo = sum(lo_on_vector(t) for t in range(k + 1))
                if lo_on_vector(k):
                    pe.wait_ge(lo_dve, b * LO_V + dve_lo)
                else:
                    pe.wait_ge(lo_pool, b * LO_G + (k + 1 - dve_lo))
                if k % QUARTER == 0 and not (isinstance(b, int) and b * 4 + q < 1):
                    pe.wait_ge(o_saved, b * 4 + q)
                for r in range(2):
                    h4 = 2 * (k % 2) + r
                    v = vbuf[s][:, :, (GROUPS * h4 + g) // 2, :]
                    for t in range(TPB):
                        at = ((t * ROWT + h4) * 2 + g % 2) * VCOLS
                        for nt in range(TPB):
                            for lo in range(2):
                                src = plo[k % PRING][:, r, nt, :] if lo else hi_of(k)[:, r, nt, :]
                                mm = nc.tensor.matmul(ps[:, BANK_O, at:at + VCOLS], src[:, P * t:P * t + P],
                                                      v[:, nt, :], start=nt == 0 and lo == 0,
                                                      stop=nt == TPB - 1 and lo == 1)
                mm.then_inc(pv_done, 1)

            def turn_x(src, n):
                for i in range(CHUNKS):
                    pe.wait_ge(xn_ready, CHUNKS * n + i + 1)
                    for t in range(TPK):
                        mm = nc.tensor.transpose(ps[:, i, P * t:P * t + P], src[:, TPK * i + t, :], ident[:])
                    mm.then_inc(xT_full, 1)

            pe.wait_ge(job_out, len(JOBS))
            pe.wait_ge(aug_loaded[0], 16 * LOADS)
            for a in range(A_TILES):
                score_a(0, 0, a)
                if a == A_TILES // 2 + 3:
                    turn_max(0, 0)
            turn_max(0, 1)

            def step(b, s, turn, first, last):
                for k in range(B_TILES):
                    if k == 1 and not first:
                        turn_max(b, 1)
                    score_b(b, s, turn, k)
                    if not last:
                        if k == 0:
                            pe.wait_ge(aug_loaded[(s + 1) % SLOTS], (turn + (s + 1) // SLOTS + 1) * (16 * LOADS))
                        score_a(b + 1, (s + 1) % SLOTS, 2 * k)
                        score_a(b + 1, (s + 1) % SLOTS, 2 * k + 1)
                        if k == B_TILES // 2 + 1:
                            turn_max(b + 1, 0)
                    if k >= LAG:
                        times_v(b, s, k - LAG)
                    elif not first:
                        times_v(b - 1, (s - 1) % SLOTS, B_TILES - LAG + k)

            batches(pe, step)
            for k in range(B_TILES - LAG, B_TILES):
                times_v(BATCH - 1, (BATCH - 1) % SLOTS, k)

            pe.wait_ge(ld_ffn, 16 * 6)
            pe.wait_ge(x1_ready, 1)
            nc.tensor.transpose(ps[:, 4, 0:EXPERTS * FCH], b1_in[:], ident[0:EXPERTS * FCH, 0:EXPERTS * FCH])
            nc.tensor.transpose(ps[:, 4, EXPERTS * FCH:EXPERTS * FCH + EXPERTS], b2_in[:],
                                ident[0:EXPERTS, 0:EXPERTS]).then_inc(bT_full, 1)
            turn_x(xn1, 1)
            pe.wait_ge(xT_out, CHUNKS)
            for t in range(TILES):
                mm = nc.tensor.matmul(ps[:, 5, EXPERTS * t:EXPERTS * t + EXPERTS], xT1[:, t, :], gate_w[:], start=True, stop=True)
            mm.then_inc(logits_full, 1)
            pe.wait_ge(mask_ready, 1)
            pe.wait_ge(ffn_consts, 1)
            nc.tensor.matmul(ps[:, 6, 0:EXPERTS * TILES], before[:], mask[:], start=True, stop=False)
            nc.tensor.matmul(ps[:, 6, 0:EXPERTS * TILES], onesb[:], prior[:], start=False, stop=True).then_inc(rank_full, 1)
            pe.wait_ge(diag_ready, 1)
            for n in range(CHUNKS):
                nc.tensor.matmul(ps[:, n, :], onesh[:], diag[:, TPK * n:TPK * n + TPK, :], start=True, stop=True).then_inc(row_full, 1)
            for t in range(TILES):
                pe.wait_ge(onehot_ready, t + 1)
                if t == 0:
                    pe.wait_ge(bT_out, 1)
                for half in range(2):
                    mm = nc.tensor.matmul(ps[:, 4 + half, 0:EHALF], xn1[:, t, :], onehot[t % 4][:, EHALF * half:EHALF * half + EHALF],
                                          start=t == 0, stop=t == TILES - 1)
                mm.then_inc(onehot_used, 1)
            pe.wait_ge(tok_out, 1)
            pe.wait_ge(row_out, CHUNKS)
            for e in range(EXPERTS):
                if e >= 4:
                    pe.wait_ge(h_biased, e - 3)
                for f in range(FCH):
                    mm = nc.tensor.matmul(ps[:, e % 4, CAP * f:CAP * f + CAP], w1[:, e, P * f:P * f + P],
                                          tokT[:, CAP * e:CAP * e + CAP], start=True, stop=True)
                mm.then_inc(h_full, 1)
            for e in range(EXPERTS):
                pe.wait_ge(h_ready, e + 1)
                bank, at = 6 + e // 4, CAP * (e % 4)
                for f in range(FCH):
                    mm = nc.tensor.matmul(ps[:, bank, at:at + CAP], w2[:, FCH * e + f, :], hact[:, FCH * e + f, :],
                                          start=f == 0, stop=f == FCH - 1)
                if e % 4 == 3:
                    mm.then_inc(y_full, 1)
            pe.wait_ge(y_biased, 2)
            for j in range(ECH):
                mm = nc.tensor.transpose(ps[:, 4 + j // 4, P * (j % 4):P * (j % 4) + P], yT[:, P * j:P * j + P], ident[:])
            mm.then_inc(yrow_full, 1)
            pe.wait_ge(y_split, 1)
            pe.wait_ge(onehotT_ready, 1)
            for t in range(TILES):
                if t >= 4:
                    pe.wait_ge(moe_used, t - 3)
                for j in range(ECH):
                    for part in range(3):
                        mm = nc.tensor.matmul(ps[:, t % 4, 0:DIM], onehotT[:, j, P * t:P * t + P], ypart[:, part, j, :],
                                              start=j == 0 and part == 0, stop=j == ECH - 1 and part == 2)
                mm.then_inc(moe_full, 1)


            turn_x(xn2, 3)
            for i in range(CHUNKS):
                pe.wait_ge(xn_ready, CHUNKS * 4 + i + 1)
                for t in range(TPK):
                    mm = nc.tensor.transpose(ps[:, 4 + i, P * t:P * t + P], cx[:, TPK * i + t, :], ident[:])
                mm.then_inc(ctxT_full, 1)
            pe.wait_ge(ld_l1, 16 * 8)
            pe.wait_ge(xT_out, 2 * CHUNKS)
            pe.wait_ge(ctxT_out, CHUNKS)
            pe.wait_ge(ones1_ready, 1)

            def project(b, par, n):
                if n == 0:
                    turn = (b - par) * 16 if not isinstance(b, int) else (b - par) * 16
                    pe.wait_ge(batch_loaded[par], turn + 32)
                if n % 2:
                    pe.wait_ge(proj_act, b * (JOBS_B // 2) + (n + 1) // 2)
                elif not (isinstance(b, int) and b == 0 and n == 0):
                    pe.wait_ge(proj_dve, b * (JOBS_B // 2) + n // 2)
                if n < 8:
                    w, src = (wq1, lat_b) if n < 4 else (wkv1, ctx_b)
                    for i in range(2):
                        m = 2 * (n % 4) + i
                        mm = nc.tensor.matmul(ps[:, 7, SEQ * i:SEQ * i + SEQ], w[:, P * m:P * m + P], src[par][:],
                                              start=True, stop=True)
                else:
                    t, half = divmod(n - 8, 2)
                    at = WIDE + BANK * half
                    mm = nc.tensor.matmul(ps[:, 7, :], ctx_b[par][:, P * t:P * t + P], wkv1[:, at:at + BANK],
                                          start=True, stop=True)
                mm.then_inc(proj_full, 1)

            def scores(b, par, m):
                if m == 0:
                    pe.wait_ge(proj_act, (b + 1) * (JOBS_B // 2))
                    pe.wait_ge(proj_dve, (b + 1) * (JOBS_B // 2))
                if not (isinstance(b, int) and b * PAIRS_B + m < 2):
                    pe.wait_ge(s_exp, b * PAIRS_B + (m - 1))
                for t in range(TPB):
                    for r in range(2):
                        rows = slice(HEADW_B * r, HEADW_B * r + HEADW_B)
                        mm = nc.tensor.matmul(ps[:, 2 * (m % 2) + r, SEQ * t:SEQ * t + SEQ],
                                              kT[par][rows, m, P * t:P * t + P], qT[par][rows, m, :],
                                              start=True, stop=True)
                mm.then_inc(s_full, 1)

            def apply_v(b, par, m):
                pe.wait_ge(s_clip, b * PAIRS_B + (m + 1))
                if not (isinstance(b, int) and b * PAIRS_B + m < 2):
                    pe.wait_ge(o_norm, b * PAIRS_B + (m - 1))
                for t in range(TPB):
                    for r in range(2):
                        at = (2 * t + r) * (HEADW_B + 1)
                        for nt in range(TPB):
                            mm = nc.tensor.matmul(ps[:, 4 + m % 2, at:at + HEADW_B + 1],
                                                  pclip[m % RING_B][:, r, nt, P * t:P * t + P],
                                                  v1[par][:, nt, 2 * m + r, :], start=nt == 0, stop=nt == TPB - 1)
                mm.then_inc(o_full, 1)

            def turn_o(b, m):
                pe.wait_ge(o_norm, b * PAIRS_B + (m + 1))
                if not (isinstance(b, int) and b * PAIRS_B + m < 1):
                    pe.wait_ge(oT_out, b * PAIRS_B + m)
                if m == 0 and not (isinstance(b, int) and b == 0):
                    pe.wait_ge(out_used, b)
                for t in range(TPB):
                    mm = nc.tensor.transpose(ps[:, 6, P * t:P * t + P],
                                             on[m % 2][:, 2 * t:2 * t + 2, :].rearrange("p r d -> p (r d)"), ident[:])
                mm.then_inc(oT_full, 1)

            def output(b, par):
                pe.wait_ge(oT_out, (b + 1) * PAIRS_B)
                for t in range(TPB):
                    for m in range(PAIRS_B):
                        mm = nc.tensor.matmul(ps[:, 6, P * t:P * t + P], oT[par][:, m, P * t:P * t + P], wo1[:, m, :],
                                              start=m == 0, stop=m == PAIRS_B - 1)
                mm.then_inc(out_full, 1)

            for n in range(JOBS_B):
                project(0, 0, n)

            def step(b, par, first, last):
                n = 0
                for m in range(PAIRS_B):
                    if m == 2 and not first:
                        output(b - 1, 1 - par)
                    scores(b, par, m)
                    if m >= 1:
                        apply_v(b, par, m - 1)
                    elif not first:
                        apply_v(b - 1, 1 - par, PAIRS_B - 1)
                    if not last:
                        for _ in range(JOBS_AT[m]):
                            project(b + 1, 1 - par, n)
                            n += 1
                    if m >= 2:
                        turn_o(b, m - 2)
                    elif not first:
                        turn_o(b - 1, PAIRS_B - 2 + m)

            batch_pairs(pe, step)
            last_b, par = BATCH - 1, (BATCH - 1) % 2
            apply_v(last_b, par, PAIRS_B - 1)
            turn_o(last_b, PAIRS_B - 2)
            turn_o(last_b, PAIRS_B - 1)
            output(last_b, par)

            pe.wait_ge(ld_f1, 16 * 5)
            pe.wait_ge(x3_ready, 1)
            nc.tensor.transpose(ps[:, 4, 0:P], wl_in[:], ident[:])
            nc.tensor.transpose(ps[:, 4, P:P + EXPERTS], gw_in[:], ident[0:EXPERTS, 0:EXPERTS]).then_inc(w1T_full, 1)
            turn_x(xn3, 5)
            pe.wait_ge(w1T_out, 1)
            pe.wait_ge(xT_out, 3 * CHUNKS)
            for t in range(TILES):
                mm = nc.tensor.matmul(ps[:, 5 + t // 8, (EXPERTS + ER) * (t % 8):(EXPERTS + ER) * (t % 8 + 1)], xT3[:, t, :], gl[:],
                                      start=True, stop=True)
            mm.then_inc(lt_full, 1)
            pe.wait_ge(tw_ready, 1)
            for n in range(CHUNKS):
                for t in range(TPK):
                    mm = nc.tensor.transpose(ps[0:ER, n, P * t:P * t + P], tw[:, TPK * n + t, :], ident[:])
                mm.then_inc(twT_full, 1)
            pe.wait_ge(twT_ones, 1)
            for t in range(TILES):
                pe.wait_ge(twT_out, t // TPK + 1)
                if t >= 4:
                    pe.wait_ge(lin_used, t - 3)
                bank = ps[:, 4 + t % 4, 0:DIM]
                nc.tensor.matmul(bank, xT3[:, t, :], wlT[:], start=True, stop=False)
                nc.tensor.matmul(bank, twT[:, P * t:P * t + P], right_b[:], start=False, stop=True).then_inc(lin_full, 1)

        @block.scalar
        def _(act):
            c = Chain(act, act_self)

            def job(what, n):
                act.wait_ge(job_full, job_at[(what, n)] + 1)
                return ps[:, job_at[(what, n)] % 8, :]

            def root(n):
                act.wait_ge(var_ready, n + 1)
                nc.scalar.activation(std[:], mv[:, :, 1], ACT.Sqrt, bias=eps[:]).then_inc(std_ready, 1)

            root(0)
            src = job("w", 0)
            for k in range(2):
                nc.scalar.activation(w3T[:, k, :].rearrange("p (r d g) -> p r g d", r=ROWT, g=GROUPS),
                                     src[:, P * k:P * k + P].rearrange("p (r g d) -> p r g d", r=ROWT, g=GROUPS), ACT.Copy)
            nc.scalar.activation(w3T[:, 2, :], src[:, 2 * P:3 * P], ACT.Copy).then_inc(job_out, 1)
            for what, dst in (("xT", xT), ("cT", cT)):
                for n in range(CHUNKS):
                    nc.scalar.activation(dst[:, TPK * n:TPK * n + TPK, :], job(what, n), ACT.Copy).then_inc(job_out, 1)
            for n in range(CHUNKS):
                for side, what in enumerate("qk"):
                    nc.scalar.activation(qk32[:, side, BANK * n:BANK * n + BANK], job(what, n), ACT.Copy).then_inc(job_out, 1)
            for n in range(CHUNKS):
                nc.scalar.activation(v32[:, TPK * n:TPK * n + TPK, :], job("v", n), ACT.Copy).then_inc(job_out, 1)
            act.wait_ge(lam_sum, 1)
            nc.scalar.activation(tg[:], gates[:], ACT.Tanh)
            nc.scalar.activation(lam_e[:], lam_s[:], ACT.Exp).then_inc(lam_exp, 1)

            def save_o(b, s, q):
                act.wait_ge(pv_done, b * B_TILES + (q + 1) * QUARTER)
                nc.scalar.activation(oraw[s][:, :, q, :],
                                     ps[:, BANK_O, 0:TPB * ROWT * 2 * VCOLS].rearrange("p (a c) -> p a c", c=2 * VCOLS),
                                     ACT.Copy).then_inc(o_saved, 1)

            def step(b, s, turn, first, last):
                for k in range(B_TILES):
                    act.wait_ge(b_full, b * B_TILES + (k + 1))
                    if not (isinstance(b, int) and b * B_TILES + k < PRING):
                        act.wait_ge(pv_done, b * B_TILES + (k + 1 - PRING))
                    bank = head_bank(k)
                    nc.scalar.activation(pexp[k % PRING][:], ps[:, bank:bank + 2, :].rearrange("p r (n t) -> p r n t", n=TPB),
                                         ACT.Exp, scale=SCALE_A).then_inc(exp_done, 1)
                    if k % QUARTER == 0:
                        q = k // QUARTER - 2
                        if q >= 0:
                            save_o(b, s, q)
                        elif not first:
                            save_o(b - 1, (s - 1) % SLOTS, q + 4)

            batches(act, step)
            save_o(BATCH - 1, (BATCH - 1) % SLOTS, 2)
            save_o(BATCH - 1, (BATCH - 1) % SLOTS, 3)


            act.wait_ge(bT_full, 1)
            nc.scalar.activation(b1T[:], ps[:, 4, 0:EXPERTS * FCH], ACT.Copy)
            nc.scalar.activation(b2T[:], ps[:, 4, EXPERTS * FCH:EXPERTS * FCH + EXPERTS], ACT.Copy).then_inc(bT_out, 1)
            root(1)
            for n in range(CHUNKS):
                act.wait_ge(xT_full, n + 1)
                nc.scalar.activation(xT1[:, TPK * n:TPK * n + TPK, :], ps[:, n, :], ACT.Copy).then_inc(xT_out, 1)
            act.wait_ge(logits_max, 1)
            nc.scalar.activation(lg[:], lg[:], ACT.Exp).then_inc(logits_exp, 1)
            for n in range(CHUNKS):
                act.wait_ge(row_full, n + 1)
                nc.scalar.activation(place_row[:, BANK * n:BANK * n + BANK], ps[:, n, :], ACT.Copy).then_inc(row_out, 1)
            act.wait_ge(onehot_used, TILES)
            for half in range(2):
                last = nc.scalar.activation(tokT[:, EHALF * half:EHALF * half + EHALF], ps[:, 4 + half, 0:EHALF], ACT.Copy)
            last.then_inc(tok_out, 1)
            for e in range(EXPERTS):
                act.wait_ge(h_biased, e + 1)
                nc.scalar.activation(hact[:, FCH * e:FCH * e + FCH, :], hpre[:, FCH * e:FCH * e + FCH, :],
                                     ACT.Gelu_apprx_tanh).then_inc(h_ready, 1)
            act.wait_ge(yrow_full, 1)
            nc.scalar.activation(yrow[:, 0:4, :], ps[:, 4, :], ACT.Copy)
            nc.scalar.activation(yrow[:, 4:ECH, :], ps[:, 5, 0:P], ACT.Copy).then_inc(yrow_out, 1)


            act.wait_ge(ld_l1, 16 * 8)
            root(2)
            root(3)
            root(4)
            for n in range(CHUNKS):
                act.wait_ge(xT_full, CHUNKS + n + 1)
                nc.scalar.activation(latT[:, TPK * n:TPK * n + TPK, :], ps[:, n, :], ACT.Identity,
                                     bias=lnf[:, 1:2], scale=lnf[:, 0:1]).then_inc(xT_out, 1)
            for n in range(CHUNKS):
                act.wait_ge(ctxT_full, n + 1)
                nc.scalar.activation(cT[:, TPK * n:TPK * n + TPK, :], ps[:, 4 + n, :], ACT.Identity,
                                     bias=lnf[:, 3:4], scale=lnf[:, 2:3]).then_inc(ctxT_out, 1)

            def copy_proj(b, par, n):
                act.wait_ge(proj_full, b * JOBS_B + (n + 1))
                nc.scalar.activation(proj_dst(par, n), proj_src(n), ACT.Copy).then_inc(proj_act, 1)

            def copy_oT(b, par, m):
                act.wait_ge(oT_full, b * PAIRS_B + (m + 1))
                nc.scalar.activation(oT[par][:, m, :], ps[:, 6, 0:SEQ], ACT.Copy).then_inc(oT_out, 1)

            for n in range(0, JOBS_B, 2):
                copy_proj(0, 0, n)

            def step(b, par, first, last):
                n = 0
                for m in range(PAIRS_B):
                    act.wait_ge(s_full, b * PAIRS_B + (m + 1))
                    if not (isinstance(b, int) and b * PAIRS_B + m < RING_B):
                        act.wait_ge(o_full, b * PAIRS_B + (m + 1 - RING_B))
                    nc.scalar.activation(pclip[m % RING_B][:], ps[:, 2 * (m % 2):2 * (m % 2) + 2, :].rearrange("p r (n t) -> p r n t", n=TPB),
                                         ACT.Exp, scale=SCALE_B).then_inc(s_exp, 1)
                    if not last:
                        for _ in range(JOBS_AT[m]):
                            if n % 2 == 0:
                                copy_proj(b + 1, 1 - par, n)
                            n += 1
                    if m >= 2:
                        copy_oT(b, par, m - 2)
                    elif not first:
                        copy_oT(b - 1, 1 - par, PAIRS_B - 2 + m)

            batch_pairs(act, step)
            copy_oT(BATCH - 1, (BATCH - 1) % 2, PAIRS_B - 2)
            copy_oT(BATCH - 1, (BATCH - 1) % 2, PAIRS_B - 1)

            act.wait_ge(w1T_full, 1)
            nc.scalar.activation(wlT[:], ps[:, 4, 0:P], ACT.Copy)
            nc.scalar.activation(gl[:, 0:EXPERTS], ps[:, 4, P:P + EXPERTS], ACT.Copy).then_inc(w1T_out, 1)
            root(5)
            for n in range(CHUNKS):
                act.wait_ge(xT_full, 2 * CHUNKS + n + 1)
                nc.scalar.activation(xT3[:, TPK * n:TPK * n + TPK, :], ps[:, n, :], ACT.Copy).then_inc(xT_out, 1)
            act.wait_ge(sc_shifted, 1)
            nc.scalar.activation(sc[:], sc[:], ACT.Exp).then_inc(sc_exp, 1)
            for n in range(CHUNKS):
                act.wait_ge(twT_full, n + 1)
                nc.scalar.activation(twT[0:ER, BANK * n:BANK * n + BANK], ps[0:ER, n, :], ACT.Copy).then_inc(twT_out, 1)

        @block.vector
        def _(dve):
            c = Chain(dve, dve_self)
            nc.vector.memset(eps[:], EPS)

            def norm(n, src, dst):
                for t in range(TILES):
                    last = nc.vector.bn_stats(stat[:, t, :], src[:, t, :])
                c.link(last)
                for t in range(TILES):
                    last = nc.vector.bn_aggr(mv[:, t, :], stat[:, t, :])
                last.then_inc(var_ready, 1)
                dve.wait_ge(std_ready, n + 1)
                c.link(nc.vector.reciprocal(rstd[:], std[:]))
                for t in range(TILES):
                    last = nc.vector.tensor_scalar(dst[:, t, :], src[:, t, :], mv[:, t, 0:1], rstd[:, t:t + 1], ALU.subtract, ALU.mult)
                    if t % TPK == TPK - 1:
                        last.then_inc(xn_ready, 1)

            dve.wait_ge(ld_x, 16 * CHUNKS)
            norm(0, x, xn)
            dve.wait_ge(ld_small, 16 * 6)
            c.link(nc.vector.tensor_tensor(lam_pr[:], lam_in[:, 0:4:2, :], lam_in[:, 1:4:2, :], ALU.mult))
            nc.vector.tensor_reduce(lam_s[:], lam_pr[:], AX.X, ALU.add).then_inc(lam_sum, 1)

            for n in range(CHUNKS):
                cols = slice(BANK * n, BANK * n + BANK)
                for side, what in enumerate("qk"):
                    dve.wait_ge(job_out, job_at[(what, n)] + 1)
                    whole, r = qk32[:, side, cols], res[:, side, :]
                    c.link(nc.vector.tensor_copy(parts[:, side, 0, cols], whole))
                    c.link(nc.vector.tensor_tensor(r, whole, parts[:, side, 0, cols], ALU.subtract))
                    c.link(nc.vector.tensor_copy(parts[:, side, 1, cols], r))
                    nc.vector.tensor_tensor(parts[:, side, 2, cols], r, parts[:, side, 1, cols], ALU.subtract).then_inc(qk_split, 1)
            dve.wait_ge(job_out, len(JOBS))
            heads = lambda ap: ap.rearrange("p t (h w) -> p (t h) w", w=HEADW_A)
            vpart = [vp[:].rearrange("p t h c -> p (t h) c")[:, :, HEADW_A * i:HEADW_A * (i + 1)] for i in range(VPARTS)]
            c.link(nc.vector.tensor_copy(vpart[0], heads(v32[:])))
            c.link(nc.vector.tensor_tensor(heads(vres[:]), heads(v32[:]), vpart[0], ALU.subtract))
            c.link(nc.vector.tensor_copy(vpart[1], heads(vres[:])))
            nc.vector.tensor_tensor(vpart[2], heads(vres[:]), vpart[1], ALU.subtract).then_inc(v_split, 1)

            dve.wait_ge(lam_exp, 1)
            c.link(nc.vector.tensor_tensor(lam[:], lam_e[:, 0:1], lam_e[:, 1:2], ALU.subtract))
            c.link(nc.vector.tensor_scalar(lam[:], lam[:], LAMBDA_INIT, -1.0, ALU.add, ALU.mult))
            nc.vector.tensor_copy(coef[:, 0:1], tg[:, 0:1])
            c.link(nc.vector.tensor_tensor(coef[:, 1:2], lam[:], tg[:, 0:1], ALU.mult))

            def max_a(b, a):
                g, r = a // ROWT, a % ROWT
                dve.wait_ge(a_full, b * A_TILES + (a + 1))
                nc.vector.tensor_reduce(nmax[g // HALF][:, :, r, g % HALF],
                                        ps[:, BANK_A[a % 2], :].rearrange("p (t n) -> p t n", t=TPB),
                                        AX.X, ALU.max, negate=True).then_inc(a_used, 1)

            def split_max(b, half):
                dve.wait_ge(a_used, b * A_TILES + (half + 1) * (A_TILES // 2))
                for t in range(TPB):
                    last = nc.vector.tensor_copy(mpart[half][:, t, :, 0, :], nmax[half][:, t, :, :])
                c.link(last)
                for t in range(TPB):
                    last = nc.vector.tensor_tensor(mpart[half][:, t, :, 1, :], nmax[half][:, t, :, :],
                                                   mpart[half][:, t, :, 0, :], ALU.subtract)
                last.then_inc(m_split, 1)

            def copy_max(b, half):
                dve.wait_ge(m_turned, b * 2 + half + 1)
                nc.vector.tensor_copy(mT[half][:], ps[0:ROWT * MROWS * HALF, BANK_M, 0:SEQ // 2].bitcast(BF16)).then_inc(m_copied, 1)

            def combine(b, s):
                dve.wait_ge(o_saved, b * 4 + 4)
                raw = oraw[s][:].rearrange("p a q (two c) -> p (a q two) c", two=2)
                part = [raw[:, :, HEADW_A * i:HEADW_A * (i + 1)] for i in range(VPARTS)]
                o = ov[:].rearrange("p a two w -> p (a two) w")
                r = rs[:].rearrange("p a two -> p (a two)")
                c.link(nc.vector.tensor_tensor(o, part[1], part[2], ALU.add))
                c.link(nc.vector.tensor_tensor(o, o, part[0], ALU.add))
                c.link(nc.vector.reciprocal(r, raw[:, :, VCOLS - 1]))
                c.link(nc.vector.tensor_tensor(rs[:], rs[:], coef[:].unsqueeze(1).broadcast_to([P, TPB * ROWT * 4, 2]), ALU.mult))
                c.link(nc.vector.tensor_tensor(o, o, r.unsqueeze(2).broadcast_to([P, TPB * ROWT * 8, HEADW_A]), ALU.mult))
                c.link(nc.vector.tensor_tensor(ov[:, :, 0, :], ov[:, :, 0, :], ov[:, :, 1, :], ALU.add))
                xb = x[:, bass.ds(b * TPB, TPB), :].rearrange("p t (h w) -> p (t h) w", w=HEADW_A)
                c.link(nc.vector.tensor_tensor(xb, xb, ov[:, :, 0, :], ALU.add))

            for a in range(A_TILES):
                max_a(0, a)
                if a == A_TILES // 2 - 1:
                    split_max(0, 0)
                if a == A_TILES - 2:
                    copy_max(0, 0)
            split_max(0, 1)
            copy_max(0, 1)

            def step(b, s, turn, first, last):
                for k in range(B_TILES):
                    if k == 1 and not first:
                        copy_max(b, 1)
                    if not last:
                        max_a(b + 1, 2 * k)
                        max_a(b + 1, 2 * k + 1)
                        if k == B_TILES // 2 - 1:
                            split_max(b + 1, 0)
                        if k == B_TILES // 2 + 2:
                            copy_max(b + 1, 0)
                        if k == B_TILES - 1:
                            split_max(b + 1, 1)
                    if lo_on_vector(k):
                        dve.wait_ge(exp_done, b * B_TILES + (k + 1))
                        nc.vector.tensor_tensor(plo[k % PRING][:], pexp[k % PRING][:], hi_of(k), ALU.subtract).then_inc(lo_dve, 1)
                    if k == LAG + 3 and not first:
                        combine(b - 1, (s - 1) % SLOTS)

            batches(dve, step, c, COMBINE_LINKS + 2)
            combine(BATCH - 1, (BATCH - 1) % SLOTS)
            dve.wait_ge(dve_self, c.n)

            dve.wait_ge(aug_loaded[2], 3 * 16 * LOADS)
            nc.vector.tensor_copy(lam[:], lam[:]).then_inc(x1_ready, 1)
            norm(1, x, xn1)
            wide = [P, TILES, EXPERTS]
            over_e = lambda ap: ap.unsqueeze(2).broadcast_to(wide)
            dve.wait_ge(logits_full, 1)
            dve.wait_ge(ld_ffn, 16 * 6)
            c.link(nc.vector.tensor_tensor(lg[:], ps[:, 5, 0:TILES * EXPERTS].rearrange("p (t e) -> p t e", e=EXPERTS),
                                           gate_b[:].unsqueeze(1).broadcast_to(wide), ALU.add))
            c.link(nc.vector.tensor_reduce(t16[:], lg[:], AX.X, ALU.max))
            nc.vector.tensor_tensor(lg[:], lg[:], over_e(t16[:]), ALU.subtract).then_inc(logits_max, 1)
            dve.wait_ge(logits_exp, 1)
            c.link(nc.vector.tensor_reduce(t16[:], lg[:], AX.X, ALU.add))
            c.link(nc.vector.reciprocal(t16[:], t16[:]))
            c.link(nc.vector.tensor_tensor(lg[:], lg[:], over_e(t16[:]), ALU.mult))
            c.link(nc.vector.tensor_reduce(gprob[:], lg[:], AX.X, ALU.max))
            c.link(nc.vector.tensor_tensor(ne[:], lg[:], over_e(gprob[:]), ALU.is_lt))
            dve.wait_ge(ffn_consts, 1)
            c.link(nc.vector.scalar_tensor_tensor(ne[:], ne[:], float(EXPERTS), iota_e[:], ALU.mult, ALU.add))
            c.link(nc.vector.tensor_reduce(t16[:], ne[:], AX.X, ALU.min))
            c.link(nc.vector.tensor_tensor(mask[:].rearrange("p e t -> p t e"), iota_e[:], over_e(t16[:]), ALU.is_equal))
            c.link(nc.vector.tensor_tensor_scan(upto[:].rearrange("p e t -> p (e t)"), keep_sum[:].rearrange("p e t -> p (e t)"),
                                                mask[:].rearrange("p e t -> p (e t)"), 0.0, ALU.mult, ALU.add))
            nc.vector.tensor_tensor(prior[:], upto[:], mask[:], ALU.subtract).then_inc(mask_ready, 1)
            dve.wait_ge(rank_full, 1)
            rank = ps[:, 6, 0:EXPERTS * TILES].rearrange("p (e t) -> p e t", e=EXPERTS)
            c.link(nc.vector.tensor_scalar(over[:], rank, float(CAP), float(EROWS), ALU.is_ge, ALU.mult))
            c.link(nc.vector.tensor_tensor(over[:], over[:], rank, ALU.add))
            c.link(nc.vector.tensor_tensor(over[:], over[:], place0[:], ALU.add))
            c.link(nc.vector.tensor_tensor(over[:], over[:], mask[:], ALU.mult))
            c.link(nc.vector.tensor_reduce(place[:], over[:].rearrange("p e t -> p t e"), AX.X, ALU.add))
            nc.vector.tensor_tensor(diag[:], ident[:].unsqueeze(1).broadcast_to([P, TILES, P]),
                                    place[:].unsqueeze(2).broadcast_to([P, TILES, P]), ALU.mult).then_inc(diag_ready, 1)
            for t in range(TILES):
                if t >= 4:
                    dve.wait_ge(onehot_used, t - 3)
                nc.vector.tensor_scalar(onehot[t % 4][:], places[:], place[:, t:t + 1], None, ALU.is_equal).then_inc(onehot_ready, 1)
            dve.wait_ge(row_out, CHUNKS)
            for j in range(ECH):
                last = nc.vector.tensor_scalar(onehotT[:, j, :], place_row[:], place_p[:, j:j + 1], None, ALU.is_equal)
            last.then_inc(onehotT_ready, 1)
            c.link(nc.vector.tensor_scalar(gprob[:], gprob[:], tg[:, 2:3], None, ALU.mult))
            dve.wait_ge(bT_out, 1)
            for e in range(EXPERTS):
                dve.wait_ge(h_full, e + 1)
                nc.vector.tensor_tensor(hpre[:, FCH * e:FCH * e + FCH, :], ps[:, e % 4, 0:FCH * CAP].rearrange("p (f c) -> p f c", f=FCH),
                                        b1T[:, FCH * e:FCH * e + FCH].unsqueeze(2).broadcast_to([P, FCH, CAP]), ALU.add).then_inc(h_biased, 1)
            for half in range(2):
                dve.wait_ge(y_full, half + 1)
                nc.vector.tensor_tensor(yT[:, EHALF * half:EHALF * half + EHALF].rearrange("p (e c) -> p e c", c=CAP),
                                        ps[:, 6 + half, 0:EHALF].rearrange("p (e c) -> p e c", c=CAP),
                                        b2T[:, 4 * half:4 * half + 4].unsqueeze(2).broadcast_to([P, 4, CAP]), ALU.add).then_inc(y_biased, 1)
            dve.wait_ge(yrow_out, 1)
            c.link(nc.vector.tensor_copy(ypart[:, 0], yrow[:]))
            c.link(nc.vector.tensor_tensor(yres[:], yrow[:], ypart[:, 0], ALU.subtract))
            c.link(nc.vector.tensor_copy(ypart[:, 1], yres[:]))
            nc.vector.tensor_tensor(ypart[:, 2], yres[:], ypart[:, 1], ALU.subtract).then_inc(y_split, 1)
            for t in range(TILES):
                dve.wait_ge(moe_full, t + 1)
                nc.vector.scalar_tensor_tensor(x[:, t, :], ps[:, t % 4, 0:DIM], gprob[:, t:t + 1], x[:, t, :], ALU.mult, ALU.add).then_inc(moe_used, 1)
            dve.wait_ge(moe_used, TILES)
            nc.vector.tensor_copy(lam[:], lam[:]).then_inc(x2_ready, 1)

            norm(2, x, xn2)
            norm_self = c
            dve.wait_ge(xn_ready, CHUNKS * 3)
            norm(3, xn2, xn2)
            norm(4, cx, cx)
            import math
            low, high = math.exp(-CLIP), math.exp(CLIP)

            def copy_proj(b, par, n):
                dve.wait_ge(proj_full, b * JOBS_B + (n + 1))
                nc.vector.tensor_copy(proj_dst(par, n), proj_src(n)).then_inc(proj_dve, 1)

            def norm_o(b, m):
                dve.wait_ge(o_full, b * PAIRS_B + (m + 1))
                src = ps[:, 4 + m % 2, 0:2 * TPB * (HEADW_B + 1)].rearrange("p (a c) -> p a c", c=HEADW_B + 1)
                c.link(nc.vector.reciprocal(rsum[m % 2][:], src[:, :, HEADW_B]))
                nc.vector.tensor_tensor(on[m % 2][:], src[:, :, 0:HEADW_B],
                                        rsum[m % 2][:].unsqueeze(2).broadcast_to([P, 2 * TPB, HEADW_B]), ALU.mult).then_inc(o_norm, 1)

            def add_output(b):
                dve.wait_ge(out_full, b + 1)
                c.link(nc.vector.tensor_tensor(ysum[:], ps[:, 6, 0:SEQ].rearrange("p (t d) -> p t d", t=TPB),
                                               bo1[:].unsqueeze(1).broadcast_to([P, TPB, DIM]), ALU.add))
                xb = x[:, bass.ds(b * TPB, TPB), :]
                nc.vector.scalar_tensor_tensor(xb, ysum[:], tg[:, 1:2], xb, ALU.mult, ALU.add).then_inc(out_used, 1)

            for n in range(1, JOBS_B, 2):
                copy_proj(0, 0, n)

            def step(b, par, first, last):
                n = 0
                for m in range(PAIRS_B):
                    dve.wait_ge(s_exp, b * PAIRS_B + (m + 1))
                    nc.vector.tensor_scalar(pclip[m % RING_B][:], pclip[m % RING_B][:], low, high, ALU.max, ALU.min).then_inc(s_clip, 1)
                    if m >= 1:
                        norm_o(b, m - 1)
                    elif not first:
                        norm_o(b - 1, PAIRS_B - 1)
                    if m == 2 and not first:
                        add_output(b - 1)
                    if not last:
                        for _ in range(JOBS_AT[m]):
                            if n % 2:
                                copy_proj(b + 1, 1 - par, n)
                            n += 1

            batch_pairs(dve, step, c, PAIRS_B + 1)
            norm_o(BATCH - 1, PAIRS_B - 1)
            add_output(BATCH - 1)
            dve.wait_ge(out_used, BATCH)
            nc.vector.tensor_copy(lam[:], lam[:]).then_inc(x3_ready, 1)

            norm(5, x, xn3)
            dve.wait_ge(lt_full, 1)
            for half in range(2):
                last = nc.vector.tensor_copy(lt[:, 8 * half:8 * half + 8, :],
                                             ps[:, 5 + half, 0:8 * (EXPERTS + ER)].rearrange("p (t n) -> p t n", t=8))
            c.link(last)
            logits = lt[:, :, 0:EXPERTS]
            c.link(nc.vector.tensor_reduce(u16[:], logits, AX.X, ALU.max))
            nc.vector.tensor_tensor(sc[:], logits, over_e(u16[:]), ALU.subtract).then_inc(sc_shifted, 1)
            dve.wait_ge(sc_exp, 1)
            c.link(nc.vector.tensor_reduce(u16[:], sc[:], AX.X, ALU.add))
            c.link(nc.vector.reciprocal(u16[:], u16[:]))
            c.link(nc.vector.tensor_tensor(sc[:], sc[:], over_e(u16[:]), ALU.mult))
            left = sc
            for n in range(2):
                c.link(nc.vector.tensor_reduce(u16[:], left[:], AX.X, ALU.max))
                c.link(nc.vector.tensor_tensor(cand[:], left[:], over_e(u16[:]), ALU.is_lt))
                c.link(nc.vector.scalar_tensor_tensor(cand[:], cand[:], float(EXPERTS), iota_e[:], ALU.mult, ALU.add))
                c.link(nc.vector.tensor_reduce(u16[:], cand[:], AX.X, ALU.min))
                c.link(nc.vector.tensor_tensor(best[:, n], iota_e[:], over_e(u16[:]), ALU.is_equal))
                if n == 0:
                    c.link(nc.vector.scalar_tensor_tensor(rest[:], best[:, 0], -2.0, sc[:], ALU.mult, ALU.add))
                    left = rest
            c.link(nc.vector.tensor_tensor(cand[:], best[:, 0], best[:, 1], ALU.add))
            c.link(nc.vector.tensor_tensor(cand[:], cand[:], sc[:], ALU.mult))
            nc.vector.tensor_tensor(tw[:].rearrange("p t (e r) -> p t e r", r=RANK),
                                    lt[:, :, EXPERTS:].rearrange("p t (e r) -> p t e r", r=RANK),
                                    cand[:].unsqueeze(3).broadcast_to([P, TILES, EXPERTS, RANK]), ALU.mult).then_inc(tw_ready, 1)
            for t in range(TILES):
                dve.wait_ge(lin_full, t + 1)
                nc.vector.scalar_tensor_tensor(x[:, t, :], ps[:, 4 + t % 4, 0:DIM], tg[:, 3:4], x[:, t, :], ALU.mult, ALU.add).then_inc(lin_used, 1)


INPUTS = ['x', 'ctx_1024', 'g_xattn', 'g_ffn', 'L0_xattn_Wq', 'L0_xattn_Wk', 'L0_xattn_Wv', 'L0_xattn_lambda_q1',
          'L0_xattn_lambda_q2', 'L0_xattn_lambda_k1', 'L0_xattn_lambda_k2', 'L0_ffn_gate_w', 'L0_ffn_gate_b',
          'L0_ffn_w1', 'L0_ffn_b1', 'L0_ffn_w2', 'L0_ffn_b2', 'L1_xattn_ln_l_w', 'L1_xattn_ln_l_b',
          'L1_xattn_ln_c_w', 'L1_xattn_ln_c_b', 'L1_xattn_Wq', 'L1_xattn_Wkv', 'L1_xattn_Wo', 'L1_xattn_bo',
          'L1_ffn_W_lin', 'L1_ffn_b_lin', 'L1_ffn_gate_w', 'L1_ffn_left', 'L1_ffn_right']


def kernel(**inputs):
    import numpy as np
    import concourse.bacc as bacc
    from concourse.bass_utils import run_bass_kernel_spmd

    nc = bacc.Bacc("TRN2", target_bir_lowering=False, num_devices=1)
    arrays, args = {}, {}
    for name in INPUTS:
        a = np.ascontiguousarray(inputs[name])
        arrays["in_" + name] = a
        args[name] = nc.dram_tensor("in_" + name, a.shape, mybir.dt.from_np(a.dtype), kind="ExternalInput").ap()
    out = nc.dram_tensor("out", (BATCH, SEQ, DIM), F32, kind="ExternalOutput").ap()
    build(nc, args, out)
    r = run_bass_kernel_spmd(nc, [arrays], core_ids=[0])
    return r.results[0]["out"]
```

```python
from contextlib import ExitStack
from math import exp

import concourse.bass as bass
from concourse import mybir

F32 = mybir.dt.float32
BF16 = mybir.dt.bfloat16
F16 = mybir.dt.float16
F32R = mybir.dt.float32r
ALU = mybir.AluOpType
ACT = mybir.ActivationFunctionType
AX = mybir.AxisListType

P = 128
BATCH, SEQ, DIM = 8, 256, 128
TILES = BATCH * SEQ // P
TPB = SEQ // P
BANK = 512
TPK = BANK // P
CHUNKS = TILES // TPK
EPS = 1e-5

SUBW, HEADS_A, HEADW_A = 4, 16, 8
ROWT, GROUPS = 4, 8
Q_PARTS = (0, 0, 0, 1, 1, 2)
K_PARTS = (0, 1, 2, 0, 1, 0)
PAIRS = len(Q_PARTS)
KROWS = PAIRS * SUBW
MROWS = 2
SLOTS = 3
VPARTS = 3
VCOLS = VPARTS * HEADW_A + 1
LAMBDA_INIT = 0.8
SCALE_A = SUBW ** -0.5
PRING = 8
LAG = 5
A_TILES = ROWT * GROUPS
B_TILES = 2 * GROUPS
QUARTER = 4
HALF = GROUPS // 2
LOADS = 2 * ROWT + 1
COMBINE_LINKS = 7

EXPERTS, CAP, FF = 8, 80, 512
FCH = FF // P
EROWS = EXPERTS * CAP
ECH = EROWS // P
EHALF = EROWS // 2


def lo_on_vector(bt):
    return bt % 4 == 3


LO_V = sum(lo_on_vector(t) for t in range(B_TILES))
LO_G = B_TILES - LO_V

WIDE, HEADS_B, HEADW_B = 1024, 16, 64
PAIRS_B = HEADS_B // 2
SCALE_B = HEADW_B ** -0.5
CLIP = 11.0
RING_B = 4
LAG_B = 2
HEADC_B = HEADW_B + 1
VMID_B, VLOW_B = HEADC_B, HEADC_B + HEADW_B
VCOLS_B = VLOW_B + HEADW_B
AHEAD_B = 2
JOBS_V = 4
V_AT = 2
RING_QK = 4
JOBS_FIRST = [("qk", 0)] + [("v", j) for j in range(JOBS_V)] + [("qk", 1)]


def jobs_with(m, last):
    jobs = [] if last and m + AHEAD_B >= PAIRS_B else [("qk", (m + AHEAD_B) % PAIRS_B, (m + AHEAD_B) // PAIRS_B)]
    if not last and 0 <= m - V_AT < JOBS_V:
        jobs.append(("v", m - V_AT, 1))
    return jobs


JOBS_B = sum(len(jobs_with(m, False)) for m in range(PAIRS_B))
assert JOBS_B % 2 == 0 and len(JOBS_FIRST) % 2 == 0


def job_count(b, m, last=False):
    return b * JOBS_B + (len(JOBS_FIRST) + sum(len(jobs_with(i, last)) for i in range(m)))


def jobs_for_pair(b, m, last=False):
    if m >= AHEAD_B:
        return job_count(b, m - AHEAD_B, last) + 1
    if isinstance(b, int) and b == 0:
        return JOBS_FIRST.index(("qk", m)) + 1
    return job_count(b - 1, PAIRS_B - AHEAD_B + m) + 1


RANK = 4
ER = EXPERTS * RANK


class Chain:

    def __init__(self, eng, sem):
        self.eng, self.sem, self.n, self.base = eng, sem, 0, 0

    def link(self, ins):
        ins.then_inc(self.sem, 1)
        self.n += 1
        self.eng.wait_ge(self.sem, self.base + self.n)


def batches(eng, step, chain=None, links=0):
    step(0, 0, 0, True, False)
    turns = (BATCH - 2) // SLOTS
    with eng.Fori(0, turns) as i:
        if chain:
            start, chain.base = chain.n, i * (SLOTS * links)
        for j in range(1, SLOTS + 1):
            step(i * SLOTS + j, j % SLOTS, i + j // SLOTS, False, False)
    if chain:
        assert chain.n - start == SLOTS * links
        chain.n, chain.base = start + turns * SLOTS * links, 0
    step(BATCH - 1, (BATCH - 1) % SLOTS, (BATCH - 1) // SLOTS, False, True)


def batch_pairs(eng, step, chain=None, links=0):
    step(0, 0, True, False)
    turns = (BATCH - 2) // 2
    with eng.Fori(0, turns) as i:
        if chain:
            start, chain.base = chain.n, i * (2 * links)
        for j in (1, 2):
            step(i * 2 + j, j % 2, False, False)
    if chain:
        assert chain.n - start == 2 * links
        chain.n, chain.base = start + turns * 2 * links, 0
    step(BATCH - 1, (BATCH - 1) % 2, False, True)


def build(nc, I, out):
    with ExitStack() as ctx:
        def sb(name, shape, dt=F32, scope=ctx):
            return scope.enter_context(nc.sbuf_tensor(name, shape, dt))

        def sem(name):
            return ctx.enter_context(nc.semaphore(name))

        ps = ctx.enter_context(nc.psum_tensor("ps", [P, 8, BANK], F32))
        BANK_A, BANK_B, BANK_O, BANK_M = (0, 1), (2, 4), 6, 7

        ident = sb("ident", [P, P])
        identb = sb("identb", [P, P], BF16)
        x = sb("x", [P, TILES, DIM])
        cx = sb("cx", [P, TILES, DIM])
        eps = sb("eps", [P, 2])
        stat = sb("stat", [P, TILES, 6])
        mv = sb("mv", [P, TILES, 2])
        std = sb("std", [P, TILES])
        rstd = sb("rstd", [P, TILES])
        cT = sb("cT", [P, TILES, P])
        w3 = sb("w3", [P, 3, DIM])
        w3T = sb("w3T", [P, 3, DIM])
        lam_in = sb("lam_in", [P, 4, SUBW])
        lam_pr = sb("lam_pr", [P, 2, SUBW])
        lam_s = sb("lam_s", [P, 2])
        lam_e = sb("lam_e", [P, 2])
        gates = sb("gates", [P, 4])
        tg = sb("tg", [P, 4])
        lam = sb("lam", [P, 1])
        coef = sb("coef", [P, 2])

        wq1 = sb("wq1", [P, WIDE])
        wkv1 = sb("wkv1", [P, 2 * WIDE])
        wo1 = sb("wo1", [P, PAIRS_B, DIM])
        lnf = sb("lnf", [P, 4])
        bo1 = sb("bo1", [P, DIM])
        wl_in, gw_in = sb("wl_in", [P, DIM]), sb("gw_in", [EXPERTS, DIM])
        wlT = sb("wlT", [P, DIM])
        gl = sb("gl", [P, EXPERTS + ER])
        right_b = sb("right_b", [ER + 1, DIM])
        gate_w, gate_b = sb("gate_w", [P, EXPERTS]), sb("gate_b", [P, EXPERTS])
        b1_in, b1T = sb("b1_in", [EXPERTS * FCH, P]), sb("b1T", [P, EXPERTS * FCH])
        b2_in, b2T = sb("b2_in", [EXPERTS, P]), sb("b2T", [P, EXPERTS])
        iota_e = sb("iota_e", [P, TILES, EXPERTS])
        place0 = sb("place0", [P, EXPERTS, TILES])
        keep_sum = sb("keep_sum", [P, EXPERTS, TILES])
        places = sb("places", [P, EROWS], F16)
        place_p = sb("place_p", [P, ECH])
        before = sb("before", [P, P], BF16)
        onesb = sb("onesb", [P, P], BF16)
        onesh = sb("onesh", [P, P], F16)
        attn0, ffn0 = ExitStack(), ExitStack()
        vp = sb("vp", [P, TILES, HEADS_A, VCOLS], BF16, attn0)
        qaug = [sb(f"qaug{i}", [P, GROUPS, SEQ], BF16, attn0) for i in range(SLOTS)]
        kaug = [sb(f"kaug{i}", [P, GROUPS, ROWT, SEQ], BF16, attn0) for i in range(SLOTS)]
        vbuf = [sb(f"vbuf{i}", [P, TPB, HEADS_A, VCOLS], BF16, attn0) for i in range(SLOTS)]
        nmax = [sb(f"nmax{i}", [P, TPB, ROWT, HALF], F32, attn0) for i in range(2)]
        mpart = [sb(f"mpart{i}", [P, TPB, ROWT, MROWS, HALF], BF16, attn0) for i in range(2)]
        mT = [sb(f"mT{i}", [ROWT * MROWS * HALF, SEQ], BF16, attn0) for i in range(2)]

        ov = sb("ov", [P, TPB * ROWT * 4, 2, HEADW_A], F32, attn0)
        rs = sb("rs", [P, TPB * ROWT * 4, 2], F32, attn0)

        early, loop_a = ExitStack(), ExitStack()
        xn = sb("xn", [P, TILES, DIM], F32, early)
        xT = sb("xT", [P, TILES, P], F32, early)
        qk32 = sb("qk32", [P, 2, TILES * P], F32, early)
        parts = sb("parts", [P, 2, 3, TILES * P], BF16, early)
        res = sb("res", [P, 2, BANK], F32, early)
        mfill = sb("mfill", [ROWT * MROWS * GROUPS, 2, BANK], BF16, early)
        v32 = sb("v32", [P, TILES, DIM], F32, early)
        vres = xn
        early.close()
        pexp = [sb(f"pexp{i}", [P, 2, TPB, SEQ], F32, loop_a) for i in range(PRING)]
        plo = [sb(f"plo{i}", [P, 2, TPB, SEQ], F16, loop_a) for i in range(PRING)]
        oraw = [sb(f"oraw{i}", [P, TPB * ROWT, 4, 2 * VCOLS], F32, loop_a) for i in range(SLOTS)]
        loop_a.close()
        attn0.close()
        w1 = sb("w1", [P, EXPERTS, FF], F32, ffn0)
        w2 = sb("w2", [P, EXPERTS * FCH, DIM], F32, ffn0)
        xn1 = sb("xn1", [P, TILES, DIM], F32, ffn0)
        xT1 = sb("xT1", [P, TILES, P], F32, ffn0)
        lg = sb("lg", [P, TILES, EXPERTS], F32, ffn0)
        ne = sb("ne", [P, TILES, EXPERTS], F32, ffn0)
        t16 = sb("t16", [P, TILES], F32, ffn0)
        gprob = sb("gprob", [P, TILES], F32, ffn0)
        mask = sb("mask", [P, EXPERTS, TILES], BF16, ffn0)
        upto = sb("upto", [P, EXPERTS, TILES], F32, ffn0)
        prior = sb("prior", [P, EXPERTS, TILES], BF16, ffn0)
        over = sb("over", [P, EXPERTS, TILES], F32, ffn0)
        place = sb("place", [P, TILES], F32, ffn0)
        onehot = [sb(f"onehot{i}", [P, EROWS], F32, ffn0) for i in range(4)]
        diag = sb("diag", [P, TILES, P], F16, ffn0)
        place_row = sb("place_row", [P, TILES * P], F16, ffn0)
        onehotT = sb("onehotT", [P, ECH, TILES * P], BF16, ffn0)
        tokT = sb("tokT", [P, EROWS], F32, ffn0)
        hpre = sb("hpre", [P, EXPERTS * FCH, CAP], F32, ffn0)
        hact = sb("hact", [P, EXPERTS * FCH, CAP], F32, ffn0)
        yT = sb("yT", [P, EROWS], F32, ffn0)
        yrow = sb("yrow", [P, ECH, P], F32, ffn0)
        ypart = sb("ypart", [P, 3, ECH, P], BF16, ffn0)
        yres = sb("yres", [P, ECH, P], F32, ffn0)
        ffn0.close()
        attn1 = ExitStack()
        xn2 = sb("xn2", [P, TILES, DIM], F32, attn1)
        latT = sb("latT", [P, TILES, P], F32, attn1)
        tok_b = [sb(f"tok_b{i}", [P, 2, SEQ], F32, attn1) for i in range(2)]
        tok_parts = [[sb(f"tok_parts{i}_{p}", [P, 2, SEQ], F32R, attn1) for p in range(2)] for i in range(2)]
        q_parts = [[sb(f"q_parts{i}_{p}", [P, 2, SEQ], F32R, attn1) for p in range(2)] for i in range(RING_QK)]
        k_parts = [[sb(f"k_parts{i}_{p}", [P, SEQ], F32R, attn1) for p in range(2)] for i in range(RING_QK)]
        v1 = [sb(f"v1_{i}", [P, TPB, HEADS_B, VCOLS_B], BF16, attn1) for i in range(2)]
        v1res = [sb(f"v1res{i}", [P, BANK], F32, attn1) for i in range(2)]
        pclip = [sb(f"pclip{i}", [P, TPB, 2, SEQ], F32, attn1) for i in range(RING_B)]
        pclo = [sb(f"pclo{i}", [P, TPB, 2, SEQ], F16, attn1) for i in range(RING_B)]
        rsum = [sb(f"rsum{i}", [P, TPB * 2], F32, attn1) for i in range(2)]
        on = [sb(f"on{i}", [P, TPB, 2, HEADW_B], F32, attn1) for i in range(2)]
        oT = [sb(f"oT{i}", [P, PAIRS_B, SEQ], F32, attn1) for i in range(2)]
        ysum = sb("ysum", [P, TPB, DIM], F32, attn1)
        wq_parts = [sb(f"wq_parts{p}", [P, WIDE], F32R, attn1) for p in range(2)]
        wkv_parts = [sb(f"wkv_parts{p}", [P, 2 * WIDE], F32R, attn1) for p in range(2)]
        attn1.close()
        ffn1 = ExitStack()
        xn3 = sb("xn3", [P, TILES, DIM], F32, ffn1)
        xT3 = sb("xT3", [P, TILES, P], F32, ffn1)
        lt = sb("lt", [P, TILES, EXPERTS + ER], F32, ffn1)
        sc = sb("sc", [P, TILES, EXPERTS], F32, ffn1)
        rest = sb("rest", [P, TILES, EXPERTS], F32, ffn1)
        cand = sb("cand", [P, TILES, EXPERTS], F32, ffn1)
        best = sb("best", [P, 2, TILES, EXPERTS], F32, ffn1)
        u16 = sb("u16", [P, TILES], F32, ffn1)
        tw = sb("tw", [P, TILES, ER], F32, ffn1)
        twT = sb("twT", [ER + 1, TILES * P], F32, ffn1)
        ffn1.close()
        qk_dram = nc.dram_tensor("qk_dram", [2, ROWT, (KROWS + MROWS) * GROUPS, TILES * P], BF16).ap()

        ld_x, ld_c, ld_w, ld_small = sem("ld_x"), sem("ld_c"), sem("ld_w"), sem("ld_small")
        out_stored = sem("out_stored")
        dve_self, act_self, pool_self = sem("dve_self"), sem("act_self"), sem("pool_self")
        consts_ready = sem("consts_ready")
        var_ready, std_ready, xn_ready = sem("var_ready"), sem("std_ready"), sem("xn_ready")
        job_full, job_out = sem("job_full"), sem("job_out")
        qk_split = sem("qk_split")
        qk_first, qk_rest = sem("qk_first"), sem("qk_rest")
        fill_ready, slot_clear = sem("fill_ready"), sem("slot_clear")
        v_cast, v_split = sem("v_cast"), sem("v_split")
        lam_sum, lam_exp, coef_ready = sem("lam_sum"), sem("lam_exp"), sem("coef_ready")
        aug_loaded = [sem(f"aug_loaded{i}") for i in range(SLOTS)]
        m_loaded = [[sem(f"m_loaded{i}_{h}") for h in range(2)] for i in range(SLOTS)]
        a_full, a_used = sem("a_full"), sem("a_used")
        b_full, exp_done = sem("b_full"), sem("exp_done")
        lo_pool, lo_dve = sem("lo_pool"), sem("lo_dve")
        pv_done, o_saved = sem("pv_done"), sem("o_saved")
        m_split, m_turned, m_copied = sem("m_split"), sem("m_turned"), sem("m_copied")
        ld_ffn, ld_experts = sem("ld_ffn"), sem("ld_experts")
        x1_ready = sem("x1_ready")
        ffn_consts = sem("ffn_consts")
        bT_full, bT_out = sem("bT_full"), sem("bT_out")
        xT_full, xT_out = sem("xT_full"), sem("xT_out")
        logits_full, logits_max, logits_exp = sem("logits_full"), sem("logits_max"), sem("logits_exp")
        mask_ready, rank_full, diag_ready = sem("mask_ready"), sem("rank_full"), sem("diag_ready")
        onehot_ready, onehot_used = sem("onehot_ready"), sem("onehot_used")
        row_full, row_out, onehotT_ready = sem("row_full"), sem("row_out"), sem("onehotT_ready")
        tok_full, tok_out = sem("tok_full"), sem("tok_out")
        h_full, h_biased, h_ready = sem("h_full"), sem("h_biased"), sem("h_ready")
        y_full, y_biased, yrow_full, yrow_out, y_split = sem("y_full"), sem("y_biased"), sem("yrow_full"), sem("yrow_out"), sem("y_split")
        moe_full, moe_used = sem("moe_full"), sem("moe_used")
        x2_ready = sem("x2_ready")
        ld_l1 = sem("ld_l1")
        ones1_ready = sem("ones1_ready")
        ctxT_full, ctxT_out = sem("ctxT_full"), sem("ctxT_out")
        batch_loaded = [sem(f"batch_loaded{i}") for i in range(2)]
        weights_split, tok_high, tok_split = sem("weights_split"), sem("tok_high"), sem("tok_split")
        proj_full, proj_high, proj_used = sem("proj_full"), sem("proj_high"), sem("proj_used")
        v1_mid, v1_split = sem("v1_mid"), sem("v1_split")
        s_full, s_exp, s_clip, s_low = sem("s_full"), sem("s_exp"), sem("s_clip"), sem("s_low")
        o_full, o_norm, oT_full, oT_out = sem("o_full"), sem("o_norm"), sem("oT_full"), sem("oT_out")
        out_full, out_used = sem("out_full"), sem("out_used")
        x3_ready = sem("x3_ready")
        ld_f1 = sem("ld_f1")
        w1T_full, w1T_out = sem("w1T_full"), sem("w1T_out")
        lt_full, lt_out = sem("lt_full"), sem("lt_out")
        sc_shifted, sc_exp, tw_ready = sem("sc_shifted"), sem("sc_exp"), sem("tw_ready")
        twT_full, twT_out, twT_ones = sem("twT_full"), sem("twT_out"), sem("twT_ones")
        lin_full, lin_used = sem("lin_full"), sem("lin_used")

        block = ctx.enter_context(nc.Block())

        JOBS = [("w", 0)] + [(what, c) for c in range(CHUNKS) for what in ("cT", "xT", "q", "k", "v")]
        job_at = {job: n for n, job in enumerate(JOBS)}

        def hi_of(k):
            return pexp[k % PRING][:].bitcast(BF16).rearrange("p r n (t two) -> p r n t two", two=2)[:, :, :, :, 1]

        def clip_hi_of(m):
            return pclip[m % RING_B][:].bitcast(BF16).rearrange("p n r (t two) -> p n r t two", two=2)[:, :, :, :, 1]

        def proj_bank(n):
            return ps[:, (5, 7)[n % 2], :]

        def qk_pieces(n, pair):
            bank, slot = proj_bank(n), pair % RING_QK
            rows = [slice(HEADW_B * r, HEADW_B * (r + 1)) for r in range(2)]
            return [([q[rows[r], r, :] for q in q_parts[slot]], bank[rows[r], 0:SEQ]) for r in range(2)] + \
                   [([k[:] for k in k_parts[slot]], bank[:, SEQ:2 * SEQ])]

        def v_piece(par, j, at):
            t, half = divmod(j, 2)
            return v1[par][:, t, 8 * half:8 * half + 8, at:at + HEADW_B]

        def by_head(bank):
            return bank.rearrange("p (h d) -> p h d", d=HEADW_B)

        def head_bank(k):
            return BANK_B[k % 2]

        @block.sync
        def _(sp):
            tok = lambda ap: ap.rearrange("b (t p) d -> p (b t) d", p=P)
            for c in range(CHUNKS):
                sp.dma_start(x[:, TPK * c:TPK * c + TPK, :], tok(I["x"])[:, TPK * c:TPK * c + TPK, :]).then_inc(ld_x, 16)
            for k, n in enumerate(("Wq", "Wk", "Wv")):
                sp.dma_start(w3[:, k, :], I["L0_xattn_" + n]).then_inc(ld_w, 16)
            sp.dma_start(cx[:], tok(I["ctx_1024"])).then_inc(ld_c, 16)
            for k, n in enumerate(("lambda_q1", "lambda_k1", "lambda_q2", "lambda_k2")):
                sp.dma_start(lam_in[:, k, :], I["L0_xattn_" + n].partition_broadcast(P)).then_inc(ld_small, 16)
            for k, n in enumerate(("g_xattn", "g_ffn")):
                sp.dma_start(gates[:, 2 * k:2 * k + 2], I[n].partition_broadcast(P)).then_inc(ld_small, 16)
            sp.dma_start(gate_w[:], I["L0_ffn_gate_w"]).then_inc(ld_ffn, 16)
            sp.dma_start(gate_b[:], I["L0_ffn_gate_b"].partition_broadcast(P)).then_inc(ld_ffn, 16)
            sp.dma_start(b1_in[:], I["L0_ffn_b1"].rearrange("e (c f) -> (e c) f", f=P)).then_inc(ld_ffn, 16)
            sp.dma_start(b2_in[:], I["L0_ffn_b2"]).then_inc(ld_ffn, 16)
            sp.dma_start(wq1[:], I["L1_xattn_Wq"]).then_inc(ld_l1, 16)
            sp.dma_start(wkv1[:], I["L1_xattn_Wkv"]).then_inc(ld_l1, 16)
            sp.dma_start(wo1[:], I["L1_xattn_Wo"].rearrange("(m p) d -> p m d", p=P)).then_inc(ld_l1, 16)
            for k, n in enumerate(("ln_l_w", "ln_l_b", "ln_c_w", "ln_c_b")):
                sp.dma_start(lnf[:, k:k + 1], I["L1_xattn_" + n].rearrange("(d o) -> d o", o=1)).then_inc(ld_l1, 16)
            sp.dma_start(bo1[:], I["L1_xattn_bo"].partition_broadcast(P)).then_inc(ld_l1, 16)
            sp.dma_start(wl_in[:], I["L1_ffn_W_lin"]).then_inc(ld_f1, 16)
            sp.dma_start(gw_in[:], I["L1_ffn_gate_w"]).then_inc(ld_f1, 16)
            sp.dma_start(gl[:, EXPERTS:].rearrange("p (e r) -> p e r", r=RANK),
                         I["L1_ffn_left"].rearrange("e d r -> d e r")).then_inc(ld_f1, 16)
            sp.dma_start(right_b[0:ER, :], I["L1_ffn_right"].rearrange("e r o -> (e r) o")).then_inc(ld_f1, 16)
            sp.dma_start(right_b[ER:ER + 1, :], I["L1_ffn_b_lin"].rearrange("(a d) -> a d", a=1)).then_inc(ld_f1, 16)
            sp.wait_ge(fill_ready, 1)
            for c in range(CHUNKS):
                for side in range(2):
                    sp.dma_start(qk_dram[side, :, KROWS * GROUPS:, BANK * c:BANK * c + BANK],
                                 mfill[:, side, :]).then_inc(qk_rest if c else qk_first, 16)

            def store_parts(cols, done, stored):
                for side, which in enumerate((Q_PARTS, K_PARTS)):
                    sp.wait_ge(qk_split, 2 * done - 1 + side)
                    for pair, part in enumerate(which):
                        rows = slice(pair * SUBW * GROUPS, (pair + 1) * SUBW * GROUPS)
                        sp.dma_start(qk_dram[side, :, rows, cols], parts[:, side, part, cols]).then_inc(stored, 16)

            store_parts(slice(0, BANK), 1, qk_first)
            sp.wait_ge(qk_first, 16 * 2 * (PAIRS + 1))
            sp.wait_ge(v_split, 1)

            def load_batch(b, s):
                for r in range(ROWT):
                    row = P // ROWT * r
                    for side, dst in enumerate((qaug[s][row:row + KROWS + MROWS, :, :],
                                                kaug[s][row:row + KROWS + MROWS, :, r, :])):
                        sp.dma_start(dst, qk_dram[side, r, :, bass.ds(b * SEQ, SEQ)].rearrange(
                            "(c g) t -> c g t", g=GROUPS)).then_inc(aug_loaded[s], 16)
                sp.dma_start(vbuf[s][:], vp[:, bass.ds(b * TPB, TPB), :, :]).then_inc(aug_loaded[s], 16)

            def m_rows(b, s, half):
                sp.wait_ge(m_copied, b * 2 + half + 1)
                for r in range(ROWT):
                    row = P // ROWT * r + KROWS
                    sp.dma_start(qaug[s][row:row + MROWS, HALF * half:HALF * half + HALF, :],
                                 mT[half][r * MROWS * HALF:(r + 1) * MROWS * HALF, :]).then_inc(m_loaded[s][half], 16)

            assert 2 * SEQ == BANK
            for b in range(2):
                sp.wait_ge(slot_clear, b + 1)
                load_batch(b, b)
            store_parts(slice(BANK, TILES * P), CHUNKS, qk_rest)
            m_rows(0, 0, 0)
            m_rows(0, 0, 1)
            sp.wait_ge(qk_rest, 16 * 2 * (PAIRS + CHUNKS - 1))
            sp.wait_ge(v_split, CHUNKS)
            sp.wait_ge(slot_clear, SLOTS)
            load_batch(2, 2)
            m_rows(1, 1, 0)
            with sp.Fori(0, (BATCH - 2) // SLOTS) as i:
                for j in range(1, SLOTS + 1):
                    b = i * SLOTS + j
                    m_rows(b, j % SLOTS, 1)
                    m_rows(b + 1, (j + 1) % SLOTS, 0)
                    sp.wait_ge(pv_done, b * B_TILES)
                    load_batch(b + 2 if j < SLOTS else i * 2 + 5, (j + 2) % SLOTS)
            m_rows(BATCH - 1, (BATCH - 1) % SLOTS, 1)

            sp.wait_ge(x1_ready, 1)
            sp.dma_start(w1[:], I["L0_ffn_w1"].rearrange("e d f -> d e f")).then_inc(ld_experts, 16)
            sp.dma_start(w2[:], I["L0_ffn_w2"].rearrange("e (c f) d -> f (e c) d", f=P)).then_inc(ld_experts, 16)

            def load_tokens(b, par):
                for side, src in enumerate((latT, cT)):
                    sp.dma_start(tok_b[par][:, side, :].rearrange("p (t n) -> p t n", n=P),
                                 src[:, bass.ds(b * TPB, TPB), :]).then_inc(batch_loaded[par], 16)

            sp.wait_ge(ctxT_out, CHUNKS)
            sp.wait_ge(xT_out, 2 * CHUNKS)
            load_tokens(0, 0)
            load_tokens(1, 1)
            with sp.Fori(0, (BATCH - 2) // 2) as i:
                for j in range(2):
                    sp.wait_ge(tok_split, i * 2 + (j + 1))
                    load_tokens(i * 2 + (j + 2), j)
            for c in range(CHUNKS):
                sp.wait_ge(lin_used, TPK * (c + 1))
                sp.dma_start(tok(out)[:, TPK * c:TPK * c + TPK, :], x[:, TPK * c:TPK * c + TPK, :]).then_inc(out_stored, 16)
            sp.wait_ge(out_stored, 16 * CHUNKS)

        @block.gpsimd
        def _(pool):
            c = Chain(pool, pool_self)
            c.link(nc.gpsimd.memset(ident[:], 0.0))
            c.link(nc.gpsimd.affine_select(out=ident[:], in_=ident[:], compare_op=ALU.not_equal, fill=1.0, base=0,
                                           pattern=[[-1, P]], channel_multiplier=1))
            nc.gpsimd.tensor_copy(identb[:], ident[:]).then_inc(consts_ready, 1)
            c.link(nc.gpsimd.memset(mfill[:, 0, :], 0.0))
            nc.gpsimd.memset(mfill[:, 1, :], 1.0).then_inc(fill_ready, 1)
            for s in range(SLOTS):
                nc.gpsimd.memset(qaug[s][:].bitcast(F32), 0.0)
                nc.gpsimd.memset(kaug[s][:].bitcast(F32), 0.0).then_inc(slot_clear, 1)
                if s == 0:
                    c.link(nc.gpsimd.memset(vp[:, :, :, VCOLS - 1:VCOLS], 1.0))
            for n in range(CHUNKS):
                pool.wait_ge(job_out, job_at[("v", n)] + 1)
                tiles = slice(TPK * n, TPK * n + TPK)
                heads = lambda ap: ap[:, tiles, :].rearrange("p t (h w) -> p (t h) w", w=HEADW_A)
                vpart = [vp[:, tiles, :, :].rearrange("p t h c -> p (t h) c")[:, :, HEADW_A * i:HEADW_A * (i + 1)] for i in range(VPARTS)]
                c.link(nc.gpsimd.tensor_copy(vpart[0], heads(v32)))
                c.link(nc.gpsimd.tensor_tensor(heads(vres), heads(v32), vpart[0], ALU.subtract))
                c.link(nc.gpsimd.tensor_copy(vpart[1], heads(vres)))
                nc.gpsimd.tensor_tensor(vpart[2], heads(vres), vpart[1], ALU.subtract).then_inc(v_split, 1)

            nc.gpsimd.iota(iota_e[:], [[0, TILES], [1, EXPERTS]], base=0, channel_multiplier=0, allow_small_or_imprecise_dtypes=True)
            nc.gpsimd.iota(place0[:], [[CAP, EXPERTS], [0, TILES]], base=0, channel_multiplier=0, allow_small_or_imprecise_dtypes=True)
            nc.gpsimd.iota(places[:], [[1, EROWS]], base=0, channel_multiplier=0, allow_small_or_imprecise_dtypes=True)
            nc.gpsimd.iota(place_p[:], [[P, ECH]], base=0, channel_multiplier=1, allow_small_or_imprecise_dtypes=True)
            nc.gpsimd.memset(onesh[:], 1.0)
            nc.gpsimd.memset(onesb[:], 1.0)
            c.link(nc.gpsimd.memset(keep_sum[:], 1.0))
            c.link(nc.gpsimd.memset(keep_sum[:, :, 0:1], 0.0))
            nc.gpsimd.affine_select(out=before[:], in_=onesb[:], compare_op=ALU.is_gt, fill=0.0, base=0,
                                    pattern=[[1, P]], channel_multiplier=-1).then_inc(ffn_consts, 1)

            def step(b, s, turn, first, last):
                for k in range(B_TILES):
                    if not lo_on_vector(k):
                        pool.wait_ge(exp_done, b * B_TILES + k + 1)
                        nc.gpsimd.tensor_tensor(plo[k % PRING][:], pexp[k % PRING][:], hi_of(k), ALU.subtract).then_inc(lo_pool, 1)

            batches(pool, step)
            pool.wait_ge(x1_ready, 1)
            pool.wait_ge(ld_l1, 16 * 8)
            for whole, part in ((wq1, wq_parts), (wkv1, wkv_parts)):
                c.link(nc.gpsimd.tensor_copy(part[0][:], whole[:]))
                last = nc.gpsimd.tensor_tensor(part[1][:], whole[:], part[0][:], ALU.subtract)
            last.then_inc(weights_split, 1)
            pool.wait_ge(x2_ready, 1)
            for parts_of in q_parts:
                for part in parts_of:
                    nc.gpsimd.memset(part[:].bitcast(F32), 0.0)
            for par in range(2):
                last = nc.gpsimd.memset(v1[par][:, :, :, HEADW_B:HEADC_B], 1.0)
            last.then_inc(ones1_ready, 1)

            def split_v(b, par, j):
                pool.wait_ge(v1_mid, b * JOBS_V + (j + 1))
                nc.gpsimd.tensor_tensor(v_piece(par, j, VLOW_B), by_head(v1res[j % 2][:]), v_piece(par, j, VMID_B),
                                        ALU.subtract).then_inc(v1_split, 1)

            for j in range(JOBS_V):
                split_v(0, 0, j)

            def step(b, par, first, last):
                for m in range(PAIRS_B):
                    pool.wait_ge(s_clip, b * PAIRS_B + (m + 1))
                    nc.gpsimd.tensor_tensor(pclo[m % RING_B][:], pclip[m % RING_B][:], clip_hi_of(m), ALU.subtract).then_inc(s_low, 1)
                    for what, j, ahead in jobs_with(m, last):
                        if what == "v":
                            split_v(b + ahead, 1 - par, j)

            batch_pairs(pool, step)
            pool.wait_ge(x3_ready, 1)
            nc.gpsimd.memset(twT[ER:ER + 1, :], 1.0).then_inc(twT_ones, 1)

        @block.tensor
        def _(pe):
            pe.wait_ge(consts_ready, 1)
            for n, (what, c) in enumerate(JOBS):
                bank = ps[:, n % 8, :]
                if n >= 8:
                    pe.wait_ge(job_out, n - 7)
                if what == "w":
                    pe.wait_ge(ld_w, 48)
                    for k in range(3):
                        mm = nc.tensor.transpose(bank[:, P * k:P * k + P], w3[:, k, :], ident[:])
                elif what in ("xT", "cT"):
                    if what == "xT":
                        pe.wait_ge(xn_ready, c + 1)
                    else:
                        pe.wait_ge(ld_c, 16)
                    src = xn if what == "xT" else cx
                    for t in range(TPK):
                        mm = nc.tensor.transpose(bank[:, P * t:P * t + P], src[:, TPK * c + t, :], ident[:])
                else:
                    need = {"q": ("xT", c), "k": ("cT", c), "v": ("cT", c)}[what]
                    pe.wait_ge(job_out, job_at[need] + 1)
                    if what == "v":
                        for t in range(TPK):
                            mm = nc.tensor.matmul(bank[:, P * t:P * t + P], cT[:, TPK * c + t, :], w3T[:, 2, :],
                                                  start=True, stop=True)
                    else:
                        src = (xT if what == "q" else cT)[:, TPK * c:TPK * c + TPK, :]
                        mm = nc.tensor.matmul(bank, w3T[:, 0 if what == "q" else 1, :], src, start=True, stop=True)
                mm.then_inc(job_full, 1)

            def score_a(b, s, a):
                g, r = a // ROWT, a % ROWT
                if not (isinstance(b, int) and b * A_TILES + a < 2):
                    pe.wait_ge(a_used, b * A_TILES + (a - 1))
                for t in range(TPB):
                    mm = nc.tensor.matmul(ps[:, BANK_A[a % 2], SEQ * t:SEQ * t + SEQ],
                                          qaug[s][:, g, P * t:P * t + P], kaug[s][:, g, r, :],
                                          start=True, stop=True)
                mm.then_inc(a_full, 1)

            def turn_max(b, half):
                pe.wait_ge(m_split, b * 2 + half + 1)
                if not (isinstance(b, int) and b * 2 + half < 1):
                    pe.wait_ge(m_copied, b * 2 + half)
                for t in range(TPB):
                    mm = nc.tensor.transpose(
                        ps[0:ROWT * MROWS * HALF, BANK_M, 0:SEQ // 2].bitcast(BF16)[:, P * t:P * t + P],
                        mpart[half][:, t, :, :, :], identb[:])
                mm.then_inc(m_turned, 1)

            def score_b(b, s, turn, k):
                g = k // 2
                if k == 0:
                    pe.wait_ge(aug_loaded[s], (turn + 1) * (16 * LOADS))
                    pe.wait_ge(m_loaded[s][0], (turn + 1) * (16 * ROWT))
                if k == B_TILES // 2:
                    pe.wait_ge(m_loaded[s][1], (turn + 1) * (16 * ROWT))
                if not (isinstance(b, int) and b * B_TILES + k < 2):
                    pe.wait_ge(exp_done, b * B_TILES + (k - 1))
                for t in range(TPB):
                    for r in range(2):
                        mm = nc.tensor.matmul(ps[:, head_bank(k) + r, SEQ * t:SEQ * t + SEQ],
                                              kaug[s][:, g, 2 * (k % 2) + r, P * t:P * t + P], qaug[s][:, g, :],
                                              start=True, stop=True)
                mm.then_inc(b_full, 1)

            def times_v(b, s, k):
                idx = b * B_TILES
                pe.wait_ge(exp_done, idx + (k + 1))
                g, q = k // 2, k // QUARTER
                dve_lo = sum(lo_on_vector(t) for t in range(k + 1))
                if lo_on_vector(k):
                    pe.wait_ge(lo_dve, b * LO_V + dve_lo)
                else:
                    pe.wait_ge(lo_pool, b * LO_G + (k + 1 - dve_lo))
                if k % QUARTER == 0 and not (isinstance(b, int) and b * 4 + q < 1):
                    pe.wait_ge(o_saved, b * 4 + q)
                for r in range(2):
                    h4 = 2 * (k % 2) + r
                    v = vbuf[s][:, :, (GROUPS * h4 + g) // 2, :]
                    for t in range(TPB):
                        at = ((t * ROWT + h4) * 2 + g % 2) * VCOLS
                        for nt in range(TPB):
                            for lo in range(2):
                                src = plo[k % PRING][:, r, nt, :] if lo else hi_of(k)[:, r, nt, :]
                                mm = nc.tensor.matmul(ps[:, BANK_O, at:at + VCOLS], src[:, P * t:P * t + P],
                                                      v[:, nt, :], start=nt == 0 and lo == 0,
                                                      stop=nt == TPB - 1 and lo == 1)
                mm.then_inc(pv_done, 1)

            def turn_x(src, n):
                for i in range(CHUNKS):
                    pe.wait_ge(xn_ready, CHUNKS * n + i + 1)
                    for t in range(TPK):
                        mm = nc.tensor.transpose(ps[:, i, P * t:P * t + P], src[:, TPK * i + t, :], ident[:])
                    mm.then_inc(xT_full, 1)

            pe.wait_ge(job_out, len(JOBS))
            pe.wait_ge(aug_loaded[0], 16 * LOADS)
            for a in range(A_TILES):
                score_a(0, 0, a)
                if a == A_TILES // 2 + 3:
                    turn_max(0, 0)
            turn_max(0, 1)

            def step(b, s, turn, first, last):
                for k in range(B_TILES):
                    if k == 1 and not first:
                        turn_max(b, 1)
                    score_b(b, s, turn, k)
                    if not last:
                        if k == 0:
                            pe.wait_ge(aug_loaded[(s + 1) % SLOTS], (turn + (s + 1) // SLOTS + 1) * (16 * LOADS))
                        score_a(b + 1, (s + 1) % SLOTS, 2 * k)
                        score_a(b + 1, (s + 1) % SLOTS, 2 * k + 1)
                        if k == B_TILES // 2 + 1:
                            turn_max(b + 1, 0)
                    if k >= LAG:
                        times_v(b, s, k - LAG)
                    elif not first:
                        times_v(b - 1, (s - 1) % SLOTS, B_TILES - LAG + k)

            batches(pe, step)
            for k in range(B_TILES - LAG, B_TILES):
                times_v(BATCH - 1, (BATCH - 1) % SLOTS, k)

            pe.wait_ge(ld_ffn, 16 * 4)
            pe.wait_ge(x1_ready, 1)
            nc.tensor.transpose(ps[:, 4, 0:EXPERTS * FCH], b1_in[:], ident[0:EXPERTS * FCH, 0:EXPERTS * FCH])
            nc.tensor.transpose(ps[:, 4, EXPERTS * FCH:EXPERTS * FCH + EXPERTS], b2_in[:],
                                ident[0:EXPERTS, 0:EXPERTS]).then_inc(bT_full, 1)
            turn_x(xn1, 1)
            pe.wait_ge(xT_out, CHUNKS)
            for t in range(TILES):
                mm = nc.tensor.matmul(ps[:, 5, EXPERTS * t:EXPERTS * t + EXPERTS], xT1[:, t, :], gate_w[:], start=True, stop=True)
            mm.then_inc(logits_full, 1)
            for i in range(CHUNKS):
                pe.wait_ge(xn_ready, CHUNKS * 2 + i + 1)
                for t in range(TPK):
                    mm = nc.tensor.transpose(ps[:, i, P * t:P * t + P], cx[:, TPK * i + t, :], ident[:])
                mm.then_inc(ctxT_full, 1)
            pe.wait_ge(mask_ready, 1)
            pe.wait_ge(ffn_consts, 1)
            nc.tensor.matmul(ps[:, 6, 0:EXPERTS * TILES], before[:], mask[:], start=True, stop=False)
            nc.tensor.matmul(ps[:, 6, 0:EXPERTS * TILES], onesb[:], prior[:], start=False, stop=True).then_inc(rank_full, 1)
            pe.wait_ge(diag_ready, 1)
            pe.wait_ge(ctxT_out, CHUNKS)
            for n in range(CHUNKS):
                nc.tensor.matmul(ps[:, n, :], onesh[:], diag[:, TPK * n:TPK * n + TPK, :], start=True, stop=True).then_inc(row_full, 1)
            for t in range(TILES):
                pe.wait_ge(onehot_ready, t + 1)
                if t == 0:
                    pe.wait_ge(bT_out, 1)
                for half in range(2):
                    mm = nc.tensor.matmul(ps[:, 4 + half, 0:EHALF], xn1[:, t, :], onehot[t % 4][:, EHALF * half:EHALF * half + EHALF],
                                          start=t == 0, stop=t == TILES - 1)
                mm.then_inc(onehot_used, 1)
            pe.wait_ge(tok_out, 1)
            pe.wait_ge(ld_experts, 16 * 2)
            pe.wait_ge(row_out, CHUNKS)
            for e in range(EXPERTS):
                if e >= 4:
                    pe.wait_ge(h_biased, e - 3)
                for f in range(FCH):
                    mm = nc.tensor.matmul(ps[:, e % 4, CAP * f:CAP * f + CAP], w1[:, e, P * f:P * f + P],
                                          tokT[:, CAP * e:CAP * e + CAP], start=True, stop=True)
                mm.then_inc(h_full, 1)
            for e in range(EXPERTS):
                pe.wait_ge(h_ready, e + 1)
                bank, at = 6 + e // 4, CAP * (e % 4)
                for f in range(FCH):
                    mm = nc.tensor.matmul(ps[:, bank, at:at + CAP], w2[:, FCH * e + f, :], hact[:, FCH * e + f, :],
                                          start=f == 0, stop=f == FCH - 1)
                if e % 4 == 3:
                    mm.then_inc(y_full, 1)
            pe.wait_ge(y_biased, 2)
            for j in range(ECH):
                mm = nc.tensor.transpose(ps[:, 4 + j // 4, P * (j % 4):P * (j % 4) + P], yT[:, P * j:P * j + P], ident[:])
            mm.then_inc(yrow_full, 1)
            pe.wait_ge(y_split, 1)
            pe.wait_ge(onehotT_ready, 1)
            for t in range(TILES):
                if t >= 4:
                    pe.wait_ge(moe_used, t - 3)
                for j in range(ECH):
                    for part in range(3):
                        mm = nc.tensor.matmul(ps[:, t % 4, 0:DIM], onehotT[:, j, P * t:P * t + P], ypart[:, part, j, :],
                                              start=j == 0 and part == 0, stop=j == ECH - 1 and part == 2)
                mm.then_inc(moe_full, 1)


            turn_x(xn2, 3)
            pe.wait_ge(ld_l1, 16 * 8)
            pe.wait_ge(xT_out, 2 * CHUNKS)
            pe.wait_ge(ctxT_out, CHUNKS)
            pe.wait_ge(ones1_ready, 1)

            def project(count, n, what, j, b, par):
                if not (isinstance(count, int) and count < 2):
                    pe.wait_ge(proj_used, count - 1)
                bank = proj_bank(n)
                products = list(enumerate(((0, 0), (0, 1), (1, 0))))
                if what == "qk":
                    for side, w in enumerate((wq_parts, wkv_parts)):
                        for i, (a, c) in products:
                            mm = nc.tensor.matmul(bank[:, SEQ * side:SEQ * side + SEQ], w[a][:, P * j:P * j + P],
                                                  tok_parts[par][c][:, side, :], start=i == 0, stop=i == 2)
                else:
                    t, half = divmod(j, 2)
                    at = WIDE + BANK * half
                    for i, (a, c) in products:
                        mm = nc.tensor.matmul(bank, tok_parts[par][a][:, 1, P * t:P * t + P], wkv_parts[c][:, at:at + BANK],
                                              start=i == 0, stop=i == 2)
                mm.then_inc(proj_full, 1)

            def scores(b, m, last):
                pe.wait_ge(proj_used, jobs_for_pair(b, m, last))
                if not (isinstance(b, int) and b * PAIRS_B + m < 2):
                    pe.wait_ge(s_exp, b * PAIRS_B + (m - 1))
                slot = m % RING_QK
                for t in range(TPB):
                    for i, (a, c) in enumerate(((0, 0), (0, 1), (1, 0))):
                        mm = nc.tensor.matmul(ps[:, 2 * (m % 2) + t, :], k_parts[slot][a][:, P * t:P * t + P],
                                              q_parts[slot][c][:], start=i == 0, stop=i == 2)
                mm.then_inc(s_full, 1)

            def apply_v(b, par, m):
                if m == 0:
                    pe.wait_ge(v1_split, (b + 1) * JOBS_V)
                pe.wait_ge(s_low, b * PAIRS_B + (m + 1))
                if not (isinstance(b, int) and b * PAIRS_B + m < 1):
                    pe.wait_ge(o_norm, b * PAIRS_B + m)
                for t in range(TPB):
                    for r in range(2):
                        at, v = (2 * t + r) * HEADC_B, v1[par][:, :, 2 * m + r, :]
                        whole, width = ps[:, 4, at:at + HEADC_B], ps[:, 4, at:at + HEADW_B]
                        for nt in range(TPB):
                            high, low = clip_hi_of(m)[:, nt, r, P * t:P * t + P], pclo[m % RING_B][:, nt, r, P * t:P * t + P]
                            nc.tensor.matmul(whole, high, v[:, nt, 0:HEADC_B], start=nt == 0, stop=False)
                            nc.tensor.matmul(width, high, v[:, nt, VMID_B:VLOW_B], start=False, stop=False)
                            nc.tensor.matmul(width, high, v[:, nt, VLOW_B:VCOLS_B], start=False, stop=False)
                            nc.tensor.matmul(width, low, v[:, nt, VMID_B:VLOW_B], start=False, stop=False)
                            mm = nc.tensor.matmul(whole, low, v[:, nt, 0:HEADC_B], start=False, stop=nt == TPB - 1)
                mm.then_inc(o_full, 1)

            def turn_o(b, par, m):
                pe.wait_ge(o_norm, b * PAIRS_B + (m + 1))
                if not (isinstance(b, int) and b * PAIRS_B + m < 1):
                    pe.wait_ge(oT_out, b * PAIRS_B + m)
                if m == 0 and not (isinstance(b, int) and b == 0):
                    pe.wait_ge(out_used, b)
                for t in range(TPB):
                    mm = nc.tensor.transpose(ps[:, 6, P * t:P * t + P],
                                             on[m % 2][:, t, :, :].rearrange("p r d -> p (r d)"), ident[:])
                mm.then_inc(oT_full, 1)

            def output(b, par):
                pe.wait_ge(oT_out, (b + 1) * PAIRS_B)
                for t in range(TPB):
                    for m in range(PAIRS_B):
                        mm = nc.tensor.matmul(ps[:, 6, P * t:P * t + P], oT[par][:, m, P * t:P * t + P], wo1[:, m, :],
                                              start=m == 0, stop=m == PAIRS_B - 1)
                mm.then_inc(out_full, 1)

            pe.wait_ge(weights_split, 1)
            pe.wait_ge(tok_split, 1)
            for n, (what, j) in enumerate(JOBS_FIRST):
                project(n, n, what, j, 0, 0)

            def earlier(do, b, par, m, lag, first):
                if m >= lag:
                    do(b, par, m - lag)
                elif not first:
                    do(b - 1, 1 - par, PAIRS_B - lag + m)

            def step(b, par, first, last):
                n = 0
                for m in range(PAIRS_B):
                    scores(b, m, last)
                    for what, j, ahead in jobs_with(m, last):
                        if what == "v" and j == 0:
                            pe.wait_ge(tok_split, b + 2)
                        project(job_count(b, 0, last) + n, n, what, j, b + ahead, par if ahead == 0 else 1 - par)
                        n += 1
                        if what == "qk":
                            if m == LAG_B + 1 and not first:
                                output(b - 1, 1 - par)
                            earlier(apply_v, b, par, m, LAG_B, first)
                    if not jobs_with(m, last):
                        earlier(apply_v, b, par, m, LAG_B, first)
                    earlier(turn_o, b, par, m, LAG_B + 1, first)

            batch_pairs(pe, step)
            last_b, par = BATCH - 1, (BATCH - 1) % 2
            for m in range(LAG_B + 1):
                if m < LAG_B:
                    apply_v(last_b, par, PAIRS_B - LAG_B + m)
                turn_o(last_b, par, PAIRS_B - LAG_B - 1 + m)
            output(last_b, par)

            pe.wait_ge(ld_f1, 16 * 5)
            pe.wait_ge(x3_ready, 1)
            nc.tensor.transpose(ps[:, 4, 0:P], wl_in[:], ident[:])
            nc.tensor.transpose(ps[:, 4, P:P + EXPERTS], gw_in[:], ident[0:EXPERTS, 0:EXPERTS]).then_inc(w1T_full, 1)
            turn_x(xn3, 4)
            pe.wait_ge(w1T_out, 1)
            pe.wait_ge(xT_out, 3 * CHUNKS)
            for t in range(TILES):
                mm = nc.tensor.matmul(ps[:, 5 + t // 8, (EXPERTS + ER) * (t % 8):(EXPERTS + ER) * (t % 8 + 1)], xT3[:, t, :], gl[:],
                                      start=True, stop=True)
            mm.then_inc(lt_full, 1)
            pe.wait_ge(tw_ready, 1)
            for n in range(CHUNKS):
                for t in range(TPK):
                    mm = nc.tensor.transpose(ps[0:ER, n, P * t:P * t + P], tw[:, TPK * n + t, :], ident[:])
                mm.then_inc(twT_full, 1)
            pe.wait_ge(twT_ones, 1)
            for t in range(TILES):
                pe.wait_ge(twT_out, t // TPK + 1)
                if t >= 4:
                    pe.wait_ge(lin_used, t - 3)
                bank = ps[:, 4 + t % 4, 0:DIM]
                nc.tensor.matmul(bank, xT3[:, t, :], wlT[:], start=True, stop=False)
                nc.tensor.matmul(bank, twT[:, P * t:P * t + P], right_b[:], start=False, stop=True).then_inc(lin_full, 1)

        @block.scalar
        def _(act):
            c = Chain(act, act_self)

            def job(what, n):
                act.wait_ge(job_full, job_at[(what, n)] + 1)
                return ps[:, job_at[(what, n)] % 8, :]

            def root(n, twice=False):
                act.wait_ge(var_ready, n + 1)
                if twice:
                    root_of = nc.scalar.activation(std[:], mv[:, :, 1], ACT.Sqrt, bias=eps[:, 1:2], scale=1 + EPS)
                else:
                    root_of = nc.scalar.activation(std[:], mv[:, :, 1], ACT.Sqrt, bias=eps[:, 0:1])
                root_of.then_inc(std_ready, 1)

            root(0)
            src = job("w", 0)
            for k in range(2):
                nc.scalar.activation(w3T[:, k, :].rearrange("p (r d g) -> p r g d", r=ROWT, g=GROUPS),
                                     src[:, P * k:P * k + P].rearrange("p (r g d) -> p r g d", r=ROWT, g=GROUPS), ACT.Copy)
            nc.scalar.activation(w3T[:, 2, :], src[:, 2 * P:3 * P], ACT.Copy).then_inc(job_out, 1)
            for what, n in JOBS[1:]:
                tiles, cols = slice(TPK * n, TPK * n + TPK), slice(BANK * n, BANK * n + BANK)
                dst = {"xT": xT[:, tiles, :], "cT": cT[:, tiles, :], "v": v32[:, tiles, :],
                       "q": qk32[:, 0, cols], "k": qk32[:, 1, cols]}[what]
                nc.scalar.activation(dst, job(what, n), ACT.Copy).then_inc(job_out, 1)
            act.wait_ge(lam_sum, 1)
            nc.scalar.activation(tg[:], gates[:], ACT.Tanh)
            nc.scalar.activation(lam_e[:], lam_s[:], ACT.Exp).then_inc(lam_exp, 1)

            def save_o(b, s, q):
                act.wait_ge(pv_done, b * B_TILES + (q + 1) * QUARTER)
                nc.scalar.activation(oraw[s][:, :, q, :],
                                     ps[:, BANK_O, 0:TPB * ROWT * 2 * VCOLS].rearrange("p (a c) -> p a c", c=2 * VCOLS),
                                     ACT.Copy).then_inc(o_saved, 1)

            def step(b, s, turn, first, last):
                for k in range(B_TILES):
                    act.wait_ge(b_full, b * B_TILES + (k + 1))
                    if not (isinstance(b, int) and b * B_TILES + k < PRING):
                        act.wait_ge(pv_done, b * B_TILES + (k + 1 - PRING))
                    bank = head_bank(k)
                    nc.scalar.activation(pexp[k % PRING][:], ps[:, bank:bank + 2, :].rearrange("p r (n t) -> p r n t", n=TPB),
                                         ACT.Exp, scale=SCALE_A).then_inc(exp_done, 1)
                    if k % QUARTER == 0:
                        q = k // QUARTER - 2
                        if q >= 0:
                            save_o(b, s, q)
                        elif not first:
                            save_o(b - 1, (s - 1) % SLOTS, q + 4)

            act.wait_ge(qk_first, 16 * 2 * (PAIRS + 1))
            act.wait_ge(qk_rest, 16 * 2 * (PAIRS + CHUNKS - 1))
            act.wait_ge(v_split, CHUNKS)
            batches(act, step)
            save_o(BATCH - 1, (BATCH - 1) % SLOTS, 2)
            save_o(BATCH - 1, (BATCH - 1) % SLOTS, 3)


            act.wait_ge(bT_full, 1)
            nc.scalar.activation(b1T[:], ps[:, 4, 0:EXPERTS * FCH], ACT.Copy)
            nc.scalar.activation(b2T[:], ps[:, 4, EXPERTS * FCH:EXPERTS * FCH + EXPERTS], ACT.Copy).then_inc(bT_out, 1)
            root(1)
            for n in range(CHUNKS):
                act.wait_ge(xT_full, n + 1)
                nc.scalar.activation(xT1[:, TPK * n:TPK * n + TPK, :], ps[:, n, :], ACT.Copy).then_inc(xT_out, 1)
            root(2)
            act.wait_ge(logits_max, 1)
            nc.scalar.activation(lg[:], lg[:], ACT.Exp).then_inc(logits_exp, 1)
            act.wait_ge(ld_l1, 16 * 8)
            for n in range(CHUNKS):
                act.wait_ge(ctxT_full, n + 1)
                nc.scalar.activation(cT[:, TPK * n:TPK * n + TPK, :], ps[:, n, :], ACT.Identity,
                                     bias=lnf[:, 3:4], scale=lnf[:, 2:3]).then_inc(ctxT_out, 1)
            for n in range(CHUNKS):
                act.wait_ge(row_full, n + 1)
                nc.scalar.activation(place_row[:, BANK * n:BANK * n + BANK], ps[:, n, :], ACT.Copy).then_inc(row_out, 1)
            act.wait_ge(onehot_used, TILES)
            for half in range(2):
                last = nc.scalar.activation(tokT[:, EHALF * half:EHALF * half + EHALF], ps[:, 4 + half, 0:EHALF], ACT.Copy)
            last.then_inc(tok_out, 1)
            for e in range(EXPERTS):
                act.wait_ge(h_biased, e + 1)
                nc.scalar.activation(hact[:, FCH * e:FCH * e + FCH, :], hpre[:, FCH * e:FCH * e + FCH, :],
                                     ACT.Gelu_apprx_tanh).then_inc(h_ready, 1)
            act.wait_ge(yrow_full, 1)
            nc.scalar.activation(yrow[:, 0:4, :], ps[:, 4, :], ACT.Copy)
            nc.scalar.activation(yrow[:, 4:ECH, :], ps[:, 5, 0:P], ACT.Copy).then_inc(yrow_out, 1)


            act.wait_ge(ld_l1, 16 * 8)
            root(3, twice=True)
            for n in range(CHUNKS):
                act.wait_ge(xT_full, CHUNKS + n + 1)
                nc.scalar.activation(latT[:, TPK * n:TPK * n + TPK, :], ps[:, n, :], ACT.Identity,
                                     bias=lnf[:, 1:2], scale=lnf[:, 0:1]).then_inc(xT_out, 1)
            def split_tokens(b, par):
                act.wait_ge(batch_loaded[par], (b - par) * 16 + 32)
                nc.scalar.activation(tok_parts[par][0][:], tok_b[par][:], ACT.Copy).then_inc(tok_high, 1)

            def copy_proj(count, n, what, j, par):
                act.wait_ge(proj_full, count + 1)
                if what == "qk":
                    for dst, src in qk_pieces(n, j):
                        last = nc.scalar.activation(dst[0], src, ACT.Copy)
                else:
                    last = nc.scalar.activation(v_piece(par, j, 0), by_head(proj_bank(n)), ACT.Copy)
                last.then_inc(proj_high, 1)

            def copy_oT(b, par, m):
                act.wait_ge(oT_full, b * PAIRS_B + (m + 1))
                nc.scalar.activation(oT[par][:, m, :], ps[:, 6, 0:SEQ], ACT.Copy).then_inc(oT_out, 1)

            act.wait_ge(ones1_ready, 1)
            split_tokens(0, 0)
            for n, (what, j) in enumerate(JOBS_FIRST):
                copy_proj(n, n, what, j, 0)

            def step(b, par, first, last):
                n = 0
                for m in range(PAIRS_B):
                    act.wait_ge(s_full, b * PAIRS_B + (m + 1))
                    if not (isinstance(b, int) and b * PAIRS_B + m < RING_B):
                        act.wait_ge(o_full, b * PAIRS_B + (m + 1 - RING_B))
                    nc.scalar.activation(pclip[m % RING_B][:], ps[:, 2 * (m % 2):2 * (m % 2) + 2, :].rearrange("p n (r t) -> p n r t", r=2),
                                         ACT.Exp, scale=SCALE_B).then_inc(s_exp, 1)
                    if m == 1 and not last:
                        split_tokens(b + 1, 1 - par)
                    for what, j, ahead in jobs_with(m, last):
                        copy_proj(job_count(b, 0, last) + n, n, what, j, 1 - par)
                        n += 1
                    if m >= LAG_B + 1:
                        copy_oT(b, par, m - LAG_B - 1)
                    elif not first:
                        copy_oT(b - 1, 1 - par, PAIRS_B - LAG_B - 1 + m)

            batch_pairs(act, step)
            for m in range(PAIRS_B - LAG_B - 1, PAIRS_B):
                copy_oT(BATCH - 1, (BATCH - 1) % 2, m)

            act.wait_ge(w1T_full, 1)
            nc.scalar.activation(wlT[:], ps[:, 4, 0:P], ACT.Copy)
            nc.scalar.activation(gl[:, 0:EXPERTS], ps[:, 4, P:P + EXPERTS], ACT.Copy).then_inc(w1T_out, 1)
            root(4)
            for n in range(CHUNKS):
                act.wait_ge(xT_full, 2 * CHUNKS + n + 1)
                nc.scalar.activation(xT3[:, TPK * n:TPK * n + TPK, :], ps[:, n, :], ACT.Copy).then_inc(xT_out, 1)
            act.wait_ge(sc_shifted, 1)
            nc.scalar.activation(sc[:], sc[:], ACT.Exp).then_inc(sc_exp, 1)
            for n in range(CHUNKS):
                act.wait_ge(twT_full, n + 1)
                nc.scalar.activation(twT[0:ER, BANK * n:BANK * n + BANK], ps[0:ER, n, :], ACT.Copy).then_inc(twT_out, 1)

        @block.vector
        def _(dve):
            c = Chain(dve, dve_self)
            nc.vector.memset(eps[:, 0:1], EPS)
            nc.vector.memset(eps[:, 1:2], EPS * EPS)

            def norm(n, src, dst):
                for t in range(TILES):
                    last = nc.vector.bn_stats(stat[:, t, :], src[:, t, :])
                c.link(last)
                for t in range(TILES):
                    last = nc.vector.bn_aggr(mv[:, t, :], stat[:, t, :])
                last.then_inc(var_ready, 1)
                dve.wait_ge(std_ready, n + 1)
                c.link(nc.vector.reciprocal(rstd[:], std[:]))
                for t in range(TILES):
                    last = nc.vector.tensor_scalar(dst[:, t, :], src[:, t, :], mv[:, t, 0:1], rstd[:, t:t + 1], ALU.subtract, ALU.mult)
                    if t % TPK == TPK - 1:
                        last.then_inc(xn_ready, 1)

            dve.wait_ge(ld_x, 16 * CHUNKS)
            norm(0, x, xn)
            dve.wait_ge(ld_small, 16 * 6)
            c.link(nc.vector.tensor_tensor(lam_pr[:], lam_in[:, 0:4:2, :], lam_in[:, 1:4:2, :], ALU.mult))
            nc.vector.tensor_reduce(lam_s[:], lam_pr[:], AX.X, ALU.add).then_inc(lam_sum, 1)

            for n in range(CHUNKS):
                cols = slice(BANK * n, BANK * n + BANK)
                for side, what in enumerate("qk"):
                    dve.wait_ge(job_out, job_at[(what, n)] + 1)
                    whole, r = qk32[:, side, cols], res[:, side, :]
                    c.link(nc.vector.tensor_copy(parts[:, side, 0, cols], whole))
                    c.link(nc.vector.tensor_tensor(r, whole, parts[:, side, 0, cols], ALU.subtract))
                    c.link(nc.vector.tensor_copy(parts[:, side, 1, cols], r))
                    nc.vector.tensor_tensor(parts[:, side, 2, cols], r, parts[:, side, 1, cols], ALU.subtract).then_inc(qk_split, 1)
            dve.wait_ge(lam_exp, 1)
            c.link(nc.vector.tensor_tensor(lam[:], lam_e[:, 0:1], lam_e[:, 1:2], ALU.subtract))
            c.link(nc.vector.tensor_scalar(lam[:], lam[:], LAMBDA_INIT, -1.0, ALU.add, ALU.mult))
            nc.vector.tensor_copy(coef[:, 0:1], tg[:, 0:1])
            c.link(nc.vector.tensor_tensor(coef[:, 1:2], lam[:], tg[:, 0:1], ALU.mult))

            def max_a(b, a):
                g, r = a // ROWT, a % ROWT
                dve.wait_ge(a_full, b * A_TILES + (a + 1))
                nc.vector.tensor_reduce(nmax[g // HALF][:, :, r, g % HALF],
                                        ps[:, BANK_A[a % 2], :].rearrange("p (t n) -> p t n", t=TPB),
                                        AX.X, ALU.max, negate=True).then_inc(a_used, 1)

            def split_max(b, half):
                dve.wait_ge(a_used, b * A_TILES + (half + 1) * (A_TILES // 2))
                for t in range(TPB):
                    last = nc.vector.tensor_copy(mpart[half][:, t, :, 0, :], nmax[half][:, t, :, :])
                c.link(last)
                for t in range(TPB):
                    last = nc.vector.tensor_tensor(mpart[half][:, t, :, 1, :], nmax[half][:, t, :, :],
                                                   mpart[half][:, t, :, 0, :], ALU.subtract)
                last.then_inc(m_split, 1)

            def copy_max(b, half):
                dve.wait_ge(m_turned, b * 2 + half + 1)
                nc.vector.tensor_copy(mT[half][:], ps[0:ROWT * MROWS * HALF, BANK_M, 0:SEQ // 2].bitcast(BF16)).then_inc(m_copied, 1)

            def combine(b, s):
                dve.wait_ge(o_saved, b * 4 + 4)
                raw = oraw[s][:].rearrange("p a q (two c) -> p (a q two) c", two=2)
                part = [raw[:, :, HEADW_A * i:HEADW_A * (i + 1)] for i in range(VPARTS)]
                o = ov[:].rearrange("p a two w -> p (a two) w")
                r = rs[:].rearrange("p a two -> p (a two)")
                c.link(nc.vector.tensor_tensor(o, part[1], part[2], ALU.add))
                c.link(nc.vector.tensor_tensor(o, o, part[0], ALU.add))
                c.link(nc.vector.reciprocal(r, raw[:, :, VCOLS - 1]))
                c.link(nc.vector.tensor_tensor(rs[:], rs[:], coef[:].unsqueeze(1).broadcast_to([P, TPB * ROWT * 4, 2]), ALU.mult))
                c.link(nc.vector.tensor_tensor(o, o, r.unsqueeze(2).broadcast_to([P, TPB * ROWT * 8, HEADW_A]), ALU.mult))
                c.link(nc.vector.tensor_tensor(ov[:, :, 0, :], ov[:, :, 0, :], ov[:, :, 1, :], ALU.add))
                xb = x[:, bass.ds(b * TPB, TPB), :].rearrange("p t (h w) -> p (t h) w", w=HEADW_A)
                c.link(nc.vector.tensor_tensor(xb, xb, ov[:, :, 0, :], ALU.add))

            for a in range(A_TILES):
                max_a(0, a)
                if a == A_TILES // 2 - 1:
                    split_max(0, 0)
                if a == A_TILES - 2:
                    copy_max(0, 0)
            split_max(0, 1)
            copy_max(0, 1)

            def step(b, s, turn, first, last):
                for k in range(B_TILES):
                    if k == 1 and not first:
                        copy_max(b, 1)
                    if not last:
                        max_a(b + 1, 2 * k)
                        max_a(b + 1, 2 * k + 1)
                        if k == B_TILES // 2 - 1:
                            split_max(b + 1, 0)
                        if k == B_TILES // 2 + 2:
                            copy_max(b + 1, 0)
                        if k == B_TILES - 1:
                            split_max(b + 1, 1)
                    if lo_on_vector(k):
                        dve.wait_ge(exp_done, b * B_TILES + (k + 1))
                        nc.vector.tensor_tensor(plo[k % PRING][:], pexp[k % PRING][:], hi_of(k), ALU.subtract).then_inc(lo_dve, 1)
                    if k == LAG + 3 and not first:
                        combine(b - 1, (s - 1) % SLOTS)

            batches(dve, step, c, COMBINE_LINKS + 2)
            combine(BATCH - 1, (BATCH - 1) % SLOTS)
            dve.wait_ge(dve_self, c.n)

            dve.wait_ge(aug_loaded[2], 3 * 16 * LOADS)
            nc.vector.tensor_copy(lam[:], lam[:]).then_inc(x1_ready, 1)
            norm(1, x, xn1)
            norm(2, cx, cx)
            wide = [P, TILES, EXPERTS]
            over_e = lambda ap: ap.unsqueeze(2).broadcast_to(wide)
            dve.wait_ge(logits_full, 1)
            dve.wait_ge(ld_ffn, 16 * 4)
            c.link(nc.vector.tensor_tensor(lg[:], ps[:, 5, 0:TILES * EXPERTS].rearrange("p (t e) -> p t e", e=EXPERTS),
                                           gate_b[:].unsqueeze(1).broadcast_to(wide), ALU.add))
            c.link(nc.vector.tensor_reduce(t16[:], lg[:], AX.X, ALU.max))
            nc.vector.tensor_tensor(lg[:], lg[:], over_e(t16[:]), ALU.subtract).then_inc(logits_max, 1)
            dve.wait_ge(logits_exp, 1)
            c.link(nc.vector.tensor_reduce(t16[:], lg[:], AX.X, ALU.add))
            c.link(nc.vector.reciprocal(t16[:], t16[:]))
            c.link(nc.vector.tensor_tensor(lg[:], lg[:], over_e(t16[:]), ALU.mult))
            c.link(nc.vector.tensor_reduce(gprob[:], lg[:], AX.X, ALU.max))
            c.link(nc.vector.tensor_tensor(ne[:], lg[:], over_e(gprob[:]), ALU.is_lt))
            dve.wait_ge(ffn_consts, 1)
            c.link(nc.vector.scalar_tensor_tensor(ne[:], ne[:], float(EXPERTS), iota_e[:], ALU.mult, ALU.add))
            c.link(nc.vector.tensor_reduce(t16[:], ne[:], AX.X, ALU.min))
            c.link(nc.vector.tensor_tensor(mask[:].rearrange("p e t -> p t e"), iota_e[:], over_e(t16[:]), ALU.is_equal))
            c.link(nc.vector.tensor_tensor_scan(upto[:].rearrange("p e t -> p (e t)"), keep_sum[:].rearrange("p e t -> p (e t)"),
                                                mask[:].rearrange("p e t -> p (e t)"), 0.0, ALU.mult, ALU.add))
            nc.vector.tensor_tensor(prior[:], upto[:], mask[:], ALU.subtract).then_inc(mask_ready, 1)
            dve.wait_ge(rank_full, 1)
            rank = ps[:, 6, 0:EXPERTS * TILES].rearrange("p (e t) -> p e t", e=EXPERTS)
            c.link(nc.vector.tensor_scalar(over[:], rank, float(CAP), float(EROWS), ALU.is_ge, ALU.mult))
            c.link(nc.vector.tensor_tensor(over[:], over[:], rank, ALU.add))
            c.link(nc.vector.tensor_tensor(over[:], over[:], place0[:], ALU.add))
            c.link(nc.vector.tensor_tensor(over[:], over[:], mask[:], ALU.mult))
            c.link(nc.vector.tensor_reduce(place[:], over[:].rearrange("p e t -> p t e"), AX.X, ALU.add))
            nc.vector.tensor_tensor(diag[:], ident[:].unsqueeze(1).broadcast_to([P, TILES, P]),
                                    place[:].unsqueeze(2).broadcast_to([P, TILES, P]), ALU.mult).then_inc(diag_ready, 1)
            for t in range(TILES):
                if t >= 4:
                    dve.wait_ge(onehot_used, t - 3)
                nc.vector.tensor_scalar(onehot[t % 4][:], places[:], place[:, t:t + 1], None, ALU.is_equal).then_inc(onehot_ready, 1)
            dve.wait_ge(row_out, CHUNKS)
            for j in range(ECH):
                last = nc.vector.tensor_scalar(onehotT[:, j, :], place_row[:], place_p[:, j:j + 1], None, ALU.is_equal)
            last.then_inc(onehotT_ready, 1)
            c.link(nc.vector.tensor_scalar(gprob[:], gprob[:], tg[:, 2:3], None, ALU.mult))
            dve.wait_ge(bT_out, 1)
            for e in range(EXPERTS):
                dve.wait_ge(h_full, e + 1)
                nc.vector.tensor_tensor(hpre[:, FCH * e:FCH * e + FCH, :], ps[:, e % 4, 0:FCH * CAP].rearrange("p (f c) -> p f c", f=FCH),
                                        b1T[:, FCH * e:FCH * e + FCH].unsqueeze(2).broadcast_to([P, FCH, CAP]), ALU.add).then_inc(h_biased, 1)
            for half in range(2):
                dve.wait_ge(y_full, half + 1)
                nc.vector.tensor_tensor(yT[:, EHALF * half:EHALF * half + EHALF].rearrange("p (e c) -> p e c", c=CAP),
                                        ps[:, 6 + half, 0:EHALF].rearrange("p (e c) -> p e c", c=CAP),
                                        b2T[:, 4 * half:4 * half + 4].unsqueeze(2).broadcast_to([P, 4, CAP]), ALU.add).then_inc(y_biased, 1)
            dve.wait_ge(yrow_out, 1)
            c.link(nc.vector.tensor_copy(ypart[:, 0], yrow[:]))
            c.link(nc.vector.tensor_tensor(yres[:], yrow[:], ypart[:, 0], ALU.subtract))
            c.link(nc.vector.tensor_copy(ypart[:, 1], yres[:]))
            nc.vector.tensor_tensor(ypart[:, 2], yres[:], ypart[:, 1], ALU.subtract).then_inc(y_split, 1)
            for t in range(TILES):
                dve.wait_ge(moe_full, t + 1)
                nc.vector.scalar_tensor_tensor(x[:, t, :], ps[:, t % 4, 0:DIM], gprob[:, t:t + 1], x[:, t, :], ALU.mult, ALU.add).then_inc(moe_used, 1)
            dve.wait_ge(moe_used, TILES)
            nc.vector.tensor_copy(lam[:], lam[:]).then_inc(x2_ready, 1)

            norm(3, x, xn2)
            low, high = exp(-CLIP), exp(CLIP)

            def split_tokens(b, par):
                dve.wait_ge(tok_high, b + 1)
                nc.vector.tensor_tensor(tok_parts[par][1][:], tok_b[par][:], tok_parts[par][0][:], ALU.subtract).then_inc(tok_split, 1)

            def copy_proj(count, n, what, j, b, par):
                dve.wait_ge(proj_high, count + 1)
                if what == "qk":
                    for dst, src in qk_pieces(n, j):
                        last = nc.vector.tensor_tensor(dst[1], src, dst[0], ALU.subtract)
                    last.then_inc(proj_used, 1)
                    return
                if not (isinstance(b, int) and b * JOBS_V + j < 2):
                    dve.wait_ge(v1_split, b * JOBS_V + (j - 1))
                rest = by_head(v1res[j % 2][:])
                nc.vector.tensor_tensor(rest, by_head(proj_bank(n)), v_piece(par, j, 0), ALU.subtract).then_inc(proj_used, 1)
                dve.wait_ge(proj_used, count + 1)
                nc.vector.tensor_copy(v_piece(par, j, VMID_B), rest).then_inc(v1_mid, 1)

            def norm_o(b, m):
                dve.wait_ge(o_full, b * PAIRS_B + (m + 1))
                src = ps[:, 4, 0:2 * TPB * HEADC_B].rearrange("p (a c) -> p a c", c=HEADC_B)
                c.link(nc.vector.reciprocal(rsum[m % 2][:], src[:, :, HEADW_B]))
                nc.vector.tensor_tensor(on[m % 2][:].rearrange("p t r d -> p (t r) d"), src[:, :, 0:HEADW_B],
                                        rsum[m % 2][:].unsqueeze(2).broadcast_to([P, 2 * TPB, HEADW_B]),
                                        ALU.mult).then_inc(o_norm, 1)

            def add_output(b):
                dve.wait_ge(out_full, b + 1)
                c.link(nc.vector.tensor_tensor(ysum[:], ps[:, 6, 0:SEQ].rearrange("p (t d) -> p t d", t=TPB),
                                               bo1[:].unsqueeze(1).broadcast_to([P, TPB, DIM]), ALU.add))
                xb = x[:, bass.ds(b * TPB, TPB), :]
                nc.vector.scalar_tensor_tensor(xb, ysum[:], tg[:, 1:2], xb, ALU.mult, ALU.add).then_inc(out_used, 1)

            dve.wait_ge(ones1_ready, 1)
            split_tokens(0, 0)
            for n, (what, j) in enumerate(JOBS_FIRST):
                copy_proj(n, n, what, j, 0, 0)

            def tail(b, par, m, first):
                if m >= LAG_B:
                    norm_o(b, m - LAG_B)
                elif not first:
                    norm_o(b - 1, PAIRS_B - LAG_B + m)
                if m == LAG_B + 1 and not first:
                    add_output(b - 1)

            def step(b, par, first, last):
                for m in range(PAIRS_B):
                    dve.wait_ge(s_exp, b * PAIRS_B + (m + 1))
                    nc.vector.tensor_scalar(pclip[m % RING_B][:], pclip[m % RING_B][:], low, high, ALU.max, ALU.min).then_inc(s_clip, 1)
                    if m == 1 and not last:
                        split_tokens(b + 1, 1 - par)
                    for i, (what, j, ahead) in enumerate(jobs_with(m, last)):
                        if i == 1:
                            tail(b, par, m, first)
                        copy_proj(job_count(b, m, last) + i, job_count(0, m, last) + i, what, j, b + ahead, 1 - par)
                    if len(jobs_with(m, last)) < 2:
                        tail(b, par, m, first)

            batch_pairs(dve, step, c, PAIRS_B + 1)
            norm_o(BATCH - 1, PAIRS_B - 2)
            norm_o(BATCH - 1, PAIRS_B - 1)
            add_output(BATCH - 1)
            dve.wait_ge(out_used, BATCH)
            nc.vector.tensor_copy(lam[:], lam[:]).then_inc(x3_ready, 1)

            norm(4, x, xn3)
            dve.wait_ge(lt_full, 1)
            for half in range(2):
                last = nc.vector.tensor_copy(lt[:, 8 * half:8 * half + 8, :],
                                             ps[:, 5 + half, 0:8 * (EXPERTS + ER)].rearrange("p (t n) -> p t n", t=8))
            c.link(last)
            logits = lt[:, :, 0:EXPERTS]
            c.link(nc.vector.tensor_reduce(u16[:], logits, AX.X, ALU.max))
            nc.vector.tensor_tensor(sc[:], logits, over_e(u16[:]), ALU.subtract).then_inc(sc_shifted, 1)
            dve.wait_ge(sc_exp, 1)
            c.link(nc.vector.tensor_reduce(u16[:], sc[:], AX.X, ALU.add))
            c.link(nc.vector.reciprocal(u16[:], u16[:]))
            c.link(nc.vector.tensor_tensor(sc[:], sc[:], over_e(u16[:]), ALU.mult))
            left = sc
            for n in range(2):
                c.link(nc.vector.tensor_reduce(u16[:], left[:], AX.X, ALU.max))
                c.link(nc.vector.tensor_tensor(cand[:], left[:], over_e(u16[:]), ALU.is_lt))
                c.link(nc.vector.scalar_tensor_tensor(cand[:], cand[:], float(EXPERTS), iota_e[:], ALU.mult, ALU.add))
                c.link(nc.vector.tensor_reduce(u16[:], cand[:], AX.X, ALU.min))
                c.link(nc.vector.tensor_tensor(best[:, n], iota_e[:], over_e(u16[:]), ALU.is_equal))
                if n == 0:
                    c.link(nc.vector.scalar_tensor_tensor(rest[:], best[:, 0], -2.0, sc[:], ALU.mult, ALU.add))
                    left = rest
            c.link(nc.vector.tensor_tensor(cand[:], best[:, 0], best[:, 1], ALU.add))
            c.link(nc.vector.tensor_tensor(cand[:], cand[:], sc[:], ALU.mult))
            nc.vector.tensor_tensor(tw[:].rearrange("p t (e r) -> p t e r", r=RANK),
                                    lt[:, :, EXPERTS:].rearrange("p t (e r) -> p t e r", r=RANK),
                                    cand[:].unsqueeze(3).broadcast_to([P, TILES, EXPERTS, RANK]), ALU.mult).then_inc(tw_ready, 1)
            for t in range(TILES):
                dve.wait_ge(lin_full, t + 1)
                nc.vector.scalar_tensor_tensor(x[:, t, :], ps[:, 4 + t % 4, 0:DIM], tg[:, 3:4], x[:, t, :], ALU.mult, ALU.add).then_inc(lin_used, 1)


INPUTS = ['x', 'ctx_1024', 'g_xattn', 'g_ffn', 'L0_xattn_Wq', 'L0_xattn_Wk', 'L0_xattn_Wv', 'L0_xattn_lambda_q1',
          'L0_xattn_lambda_q2', 'L0_xattn_lambda_k1', 'L0_xattn_lambda_k2', 'L0_ffn_gate_w', 'L0_ffn_gate_b',
          'L0_ffn_w1', 'L0_ffn_b1', 'L0_ffn_w2', 'L0_ffn_b2', 'L1_xattn_ln_l_w', 'L1_xattn_ln_l_b',
          'L1_xattn_ln_c_w', 'L1_xattn_ln_c_b', 'L1_xattn_Wq', 'L1_xattn_Wkv', 'L1_xattn_Wo', 'L1_xattn_bo',
          'L1_ffn_W_lin', 'L1_ffn_b_lin', 'L1_ffn_gate_w', 'L1_ffn_left', 'L1_ffn_right']


def kernel(**inputs):
    import numpy as np
    import concourse.bacc as bacc
    from concourse.bass_utils import run_bass_kernel_spmd

    nc = bacc.Bacc("TRN2", target_bir_lowering=False, num_devices=1)
    arrays, args = {}, {}
    for name in INPUTS:
        a = np.ascontiguousarray(inputs[name])
        arrays["in_" + name] = a
        args[name] = nc.dram_tensor("in_" + name, a.shape, mybir.dt.from_np(a.dtype), kind="ExternalInput").ap()
    out = nc.dram_tensor("out", (BATCH, SEQ, DIM), F32, kind="ExternalOutput").ap()
    build(nc, args, out)
    r = run_bass_kernel_spmd(nc, [arrays], core_ids=[0])
    return r.results[0]["out"]
```

```python
from contextlib import ExitStack
from math import exp

import concourse.bass as bass
from concourse import mybir

F32 = mybir.dt.float32
BF16 = mybir.dt.bfloat16
F16 = mybir.dt.float16
F32R = mybir.dt.float32r
ALU = mybir.AluOpType
ACT = mybir.ActivationFunctionType
AX = mybir.AxisListType

P = 128
BATCH, SEQ, DIM = 8, 256, 128
TILES = BATCH * SEQ // P
TPB = SEQ // P
BANK = 512
TPK = BANK // P
CHUNKS = TILES // TPK
EPS = 1e-5

SUBW, HEADS_A, HEADW_A = 4, 16, 8
ROWT, GROUPS = 4, 8
Q_PARTS = (0, 0, 0, 1, 1, 2)
K_PARTS = (0, 1, 2, 0, 1, 0)
PAIRS = len(Q_PARTS)
KROWS = PAIRS * SUBW
MROWS = 2
SLOTS = 3
VPARTS = 3
VCOLS = VPARTS * HEADW_A + 1
LAMBDA_INIT = 0.8
SCALE_A = SUBW ** -0.5
PRING = 8
LAG = 5
A_TILES = ROWT * GROUPS
B_TILES = 2 * GROUPS
QUARTER = 4
HALF = GROUPS // 2
LOADS = 2 * ROWT + 1
COMBINE_LINKS = 7
COMBINE_AT = 8

EXPERTS, CAP, FF = 8, 80, 512
FCH = FF // P
EROWS = EXPERTS * CAP
ECH = EROWS // P
EHALF = EROWS // 2


def lo_on_vector(b, k):
    if isinstance(b, int) and b == BATCH - 1:
        return k % 2 == 1
    return k % 4 == 0


LO_V = sum(lo_on_vector(0, t) for t in range(B_TILES))
LO_G = B_TILES - LO_V

WIDE, HEADS_B, HEADW_B = 1024, 16, 64
PAIRS_B = HEADS_B // 2
SCALE_B = HEADW_B ** -0.5
CLIP = 11.0
RING_B = 4
LAG_B = 2
HEADC_B = HEADW_B + 1
VMID_B, VLOW_B = HEADC_B, HEADC_B + HEADW_B
VCOLS_B = VLOW_B + HEADW_B
AHEAD_B = 2
JOBS_V = 4
V_AT = 2
RING_QK = 4
JOBS_FIRST = [("qk", 0)] + [("v", j) for j in range(JOBS_V)] + [("qk", 1)]


def jobs_with(m, last):
    jobs = [] if last and m + AHEAD_B >= PAIRS_B else [("qk", (m + AHEAD_B) % PAIRS_B, (m + AHEAD_B) // PAIRS_B)]
    if not last and 0 <= m - V_AT < JOBS_V:
        jobs.append(("v", m - V_AT, 1))
    return jobs


JOBS_B = sum(len(jobs_with(m, False)) for m in range(PAIRS_B))
assert JOBS_B % 2 == 0 and len(JOBS_FIRST) % 2 == 0


def job_count(b, m, last=False):
    return b * JOBS_B + (len(JOBS_FIRST) + sum(len(jobs_with(i, last)) for i in range(m)))


def jobs_for_pair(b, m, last=False):
    if m >= AHEAD_B:
        return job_count(b, m - AHEAD_B, last) + 1
    if isinstance(b, int) and b == 0:
        return JOBS_FIRST.index(("qk", m)) + 1
    return job_count(b - 1, PAIRS_B - AHEAD_B + m) + 1


RANK = 4
ER = EXPERTS * RANK


class Chain:

    def __init__(self, eng, sem):
        self.eng, self.sem, self.n, self.base = eng, sem, 0, 0

    def mark(self, ins):
        ins.then_inc(self.sem, 1)
        self.n += 1

    def follow(self):
        self.eng.wait_ge(self.sem, self.base + self.n)

    def link(self, ins):
        self.mark(ins)
        self.follow()


def batches(eng, step, chain=None, links=0):
    step(0, 0, 0, True, False)
    turns = (BATCH - 2) // SLOTS
    with eng.Fori(0, turns) as i:
        if chain:
            start, chain.base = chain.n, i * (SLOTS * links)
        for j in range(1, SLOTS + 1):
            step(i * SLOTS + j, j % SLOTS, i + j // SLOTS, False, False)
    if chain:
        assert chain.n - start == SLOTS * links
        chain.n, chain.base = start + turns * SLOTS * links, 0
    step(BATCH - 1, (BATCH - 1) % SLOTS, (BATCH - 1) // SLOTS, False, True)


def batch_pairs(eng, step, chain=None, links=0):
    step(0, 0, True, False)
    turns = (BATCH - 2) // 2
    with eng.Fori(0, turns) as i:
        if chain:
            start, chain.base = chain.n, i * (2 * links)
        for j in (1, 2):
            step(i * 2 + j, j % 2, False, False)
    if chain:
        assert chain.n - start == 2 * links
        chain.n, chain.base = start + turns * 2 * links, 0
    step(BATCH - 1, (BATCH - 1) % 2, False, True)


def build(nc, I, out):
    with ExitStack() as ctx:
        def sb(name, shape, dt=F32, scope=ctx):
            return scope.enter_context(nc.sbuf_tensor(name, shape, dt))

        def sem(name):
            return ctx.enter_context(nc.semaphore(name))

        ps = ctx.enter_context(nc.psum_tensor("ps", [P, 8, BANK], F32))
        BANK_A, BANK_B, BANK_O, BANK_M = (0, 1), (2, 4), 6, 7
        ROW_BANKS = (2, 3, 6, 7)

        ident = sb("ident", [P, P])
        identb = sb("identb", [P, P], BF16)
        x = sb("x", [P, TILES, DIM])
        cx = sb("cx", [P, TILES, DIM])
        eps = sb("eps", [P, 2])
        stat = sb("stat", [P, TILES, 6])
        stat_c = sb("stat_c", [P, TILES, 6])
        mv_c = sb("mv_c", [P, TILES, 2])
        std_c = sb("std_c", [P, TILES])
        rstd_c = sb("rstd_c", [P, TILES])
        mv = sb("mv", [P, TILES, 2])
        std = sb("std", [P, TILES])
        rstd = sb("rstd", [P, TILES])
        table_in = sb("table_in", [P, 1])
        cT = sb("cT", [P, TILES, P])
        w3 = sb("w3", [P, 3, DIM])
        w3T = sb("w3T", [P, 3, DIM])
        lam_in = sb("lam_in", [P, 4, SUBW])
        lam_pr = sb("lam_pr", [P, 2, SUBW])
        lam_s = sb("lam_s", [P, 2])
        lam_e = sb("lam_e", [P, 2])
        gates = sb("gates", [P, 4])
        tg = sb("tg", [P, 4])
        lam = sb("lam", [P, 1])
        coef = sb("coef", [P, 2])

        wq1 = sb("wq1", [P, WIDE])
        wkv1 = sb("wkv1", [P, 2 * WIDE])
        wo1 = sb("wo1", [P, PAIRS_B, DIM])
        lnf = sb("lnf", [P, 4])
        bo1 = sb("bo1", [P, DIM])
        wl_in, gw_in = sb("wl_in", [P, DIM]), sb("gw_in", [EXPERTS, DIM])
        wlT = sb("wlT", [P, DIM])
        gl = sb("gl", [P, EXPERTS + ER])
        right = sb("right", [P, TPK, DIM])
        blin = sb("blin", [P, DIM])
        gate_w, gate_b = sb("gate_w", [P, EXPERTS]), sb("gate_b", [P, EXPERTS])
        b1_in, b1T = sb("b1_in", [EXPERTS * FCH, P]), sb("b1T", [P, EXPERTS * FCH])
        b2_in, b2T = sb("b2_in", [EXPERTS, P]), sb("b2T", [P, EXPERTS])
        iota_e = sb("iota_e", [P, TILES, EXPERTS])
        place0 = sb("place0", [P, EXPERTS, TILES])
        keep_sum = sb("keep_sum", [P, EXPERTS, TILES])
        places = sb("places", [P, EROWS], F16)
        place_p = sb("place_p", [P, ECH])
        before = sb("before", [P, P], BF16)
        onesb = sb("onesb", [P, P], BF16)
        onesh = sb("onesh", [P, P], F16)
        attn0, ffn0 = ExitStack(), ExitStack()
        vp = sb("vp", [P, TILES, HEADS_A, VCOLS], BF16, attn0)
        qaug = [sb(f"qaug{i}", [P, GROUPS, SEQ], BF16, attn0) for i in range(SLOTS)]
        kaug = [sb(f"kaug{i}", [P, GROUPS, ROWT, SEQ], BF16, attn0) for i in range(SLOTS)]
        vbuf = [sb(f"vbuf{i}", [P, TPB, HEADS_A, VCOLS], BF16, attn0) for i in range(SLOTS)]
        nmax = [sb(f"nmax{i}", [P, TPB, ROWT, HALF], F32, attn0) for i in range(2)]
        mpart = [sb(f"mpart{i}", [P, TPB, ROWT, MROWS, HALF], BF16, attn0) for i in range(2)]
        mT = [sb(f"mT{i}", [ROWT * MROWS * HALF, SEQ], BF16, attn0) for i in range(2)]

        ov = sb("ov", [P, TPB * ROWT * 4, 2, HEADW_A], F32, attn0)
        rs = sb("rs", [P, TPB * ROWT * 4, 2], F32, attn0)

        early, loop_a = ExitStack(), ExitStack()
        xn = sb("xn", [P, TILES, DIM], F32, early)
        xT = sb("xT", [P, TILES, P], F32, early)
        qk32 = sb("qk32", [P, 2, TILES * P], F32, early)
        parts = sb("parts", [P, 2, 3, TILES * P], BF16, early)
        res = sb("res", [P, 2, BANK], F32, early)
        mfill = sb("mfill", [ROWT * MROWS * GROUPS, 2, BANK], BF16, early)
        v32 = sb("v32", [P, TILES, DIM], F32, early)
        vres = xn
        early.close()
        pexp = [sb(f"pexp{i}", [P, 2, TPB, SEQ], F32, loop_a) for i in range(PRING)]
        plo = [sb(f"plo{i}", [P, 2, TPB, SEQ], F16, loop_a) for i in range(PRING)]
        oraw = [sb(f"oraw{i}", [P, TPB * ROWT, 4, 2 * VCOLS], F32, loop_a) for i in range(SLOTS)]
        loop_a.close()
        attn0.close()
        w1 = sb("w1", [P, EXPERTS, FF], F32, ffn0)
        w2 = sb("w2", [P, EXPERTS * FCH, DIM], F32, ffn0)
        xn1 = sb("xn1", [P, TILES, DIM], F32, ffn0)
        xT1 = sb("xT1", [P, TILES, P], F32, ffn0)
        lg = sb("lg", [P, TILES, EXPERTS], F32, ffn0)
        ne = sb("ne", [P, TILES, EXPERTS], F32, ffn0)
        t16 = sb("t16", [P, TILES], F32, ffn0)
        gprob = sb("gprob", [P, TILES], F32, ffn0)
        mask = sb("mask", [P, EXPERTS, TILES], BF16, ffn0)
        upto = sb("upto", [P, EXPERTS, TILES], F32, ffn0)
        prior = sb("prior", [P, EXPERTS, TILES], BF16, ffn0)
        over = sb("over", [P, EXPERTS, TILES], F32, ffn0)
        place = sb("place", [P, TILES], F32, ffn0)
        onehot = [sb(f"onehot{i}", [P, EROWS], F32R, ffn0) for i in range(4)]
        diag = sb("diag", [P, TILES, P], F16, ffn0)
        place_row = sb("place_row", [P, TILES * P], F16, ffn0)
        onehotT = sb("onehotT", [P, ECH, TILES * P], BF16, ffn0)
        tokT = sb("tokT", [P, EROWS], F32, ffn0)
        xn1_high = sb("xn1_high", [P, TILES, DIM], F32R, ffn0)
        dispatch = ExitStack()
        xn1_low = sb("xn1_low", [P, TILES, DIM], F32R, dispatch)
        dispatch.close()
        hidden = sb("hidden", [P, EXPERTS * FCH, CAP], F32, ffn0)
        yT = sb("yT", [P, EROWS], F32, ffn0)
        yrow = sb("yrow", [P, ECH, P], F32, ffn0)
        ypart = sb("ypart", [P, 3, ECH, P], BF16, ffn0)
        yres = sb("yres", [P, ECH, P], F32, ffn0)
        ffn0.close()
        attn1 = ExitStack()
        xn2 = sb("xn2", [P, TILES, DIM], F32, attn1)
        latT = sb("latT", [P, TILES, P], F32, attn1)
        tok_b = [sb(f"tok_b{i}", [P, 2, SEQ], F32, attn1) for i in range(2)]
        tok_parts = [[sb(f"tok_parts{i}_{p}", [P, 2, SEQ], F32R, attn1) for p in range(2)] for i in range(2)]
        q_parts = [[sb(f"q_parts{i}_{p}", [P, 2, SEQ], F32R, attn1) for p in range(2)] for i in range(RING_QK)]
        k_parts = [[sb(f"k_parts{i}_{p}", [P, SEQ], F32R, attn1) for p in range(2)] for i in range(RING_QK)]
        v1 = [sb(f"v1_{i}", [P, TPB, HEADS_B, VCOLS_B], BF16, attn1) for i in range(2)]
        v1res = [sb(f"v1res{i}", [P, BANK], F32, attn1) for i in range(2)]
        pclip = [sb(f"pclip{i}", [P, TPB, 2, SEQ], F32, attn1) for i in range(RING_B)]
        pclo = [sb(f"pclo{i}", [P, TPB, 2, SEQ], F16, attn1) for i in range(RING_B)]
        rsum = [sb(f"rsum{i}", [P, TPB * 2], F32, attn1) for i in range(2)]
        on = [sb(f"on{i}", [P, TPB, 2, HEADW_B], F32, attn1) for i in range(2)]
        oT = [sb(f"oT{i}", [P, PAIRS_B, SEQ], F32, attn1) for i in range(2)]
        ysum = sb("ysum", [P, TPB, DIM], F32, attn1)
        wq_parts = [sb(f"wq_parts{p}", [P, WIDE], F32R, attn1) for p in range(2)]
        wkv_parts = [sb(f"wkv_parts{p}", [P, 2 * WIDE], F32R, attn1) for p in range(2)]
        attn1.close()
        ffn1 = ExitStack()
        xn3 = sb("xn3", [P, TILES, DIM], F32, ffn1)
        xT3 = sb("xT3", [P, TILES, P], F32, ffn1)
        lt = sb("lt", [P, TILES, EXPERTS + ER], F32, ffn1)
        sc = sb("sc", [P, TILES, EXPERTS], F32, ffn1)
        rest = sb("rest", [P, TILES, EXPERTS], F32, ffn1)
        cand = sb("cand", [P, TILES, EXPERTS], F32, ffn1)
        best = sb("best", [P, 2, TILES, EXPERTS], F32, ffn1)
        u16 = sb("u16", [P, TILES], F32, ffn1)
        tw = sb("tw", [P, TILES, ER], F32, ffn1)
        twT = sb("twT", [P, CHUNKS * P], F32, ffn1)
        base = sb("base", [P, TILES, DIM], F32, ffn1)
        ffn1.close()
        qk_dram = nc.dram_tensor("qk_dram", [2, ROWT, (KROWS + MROWS) * GROUPS, TILES * P], BF16).ap()

        ld_x, ld_c, ld_w, ld_small = sem("ld_x"), sem("ld_c"), sem("ld_w"), sem("ld_small")
        out_stored = sem("out_stored")
        dve_self, act_self, pool_self = sem("dve_self"), sem("act_self"), sem("pool_self")
        consts_ready = sem("consts_ready")
        var_ready, std_ready, xn_ready = sem("var_ready"), sem("std_ready"), sem("xn_ready")
        job_full, job_out = sem("job_full"), sem("job_out")
        qk_split = sem("qk_split")
        qk_first, qk_rest = sem("qk_first"), sem("qk_rest")
        fill_ready, slot_clear = sem("fill_ready"), sem("slot_clear")
        v_split = sem("v_split")
        lam_sum, lam_exp = sem("lam_sum"), sem("lam_exp")
        aug_loaded = [sem(f"aug_loaded{i}") for i in range(SLOTS)]
        m_loaded = [[sem(f"m_loaded{i}_{h}") for h in range(2)] for i in range(SLOTS)]
        a_full, a_used = sem("a_full"), sem("a_used")
        b_full, exp_done = sem("b_full"), sem("exp_done")
        lo_pool, lo_dve = sem("lo_pool"), sem("lo_dve")
        pv_done, o_saved = sem("pv_done"), sem("o_saved")
        m_split, m_turned, m_copied = sem("m_split"), sem("m_turned"), sem("m_copied")
        ld_ffn, ld_experts = sem("ld_ffn"), sem("ld_experts")
        ctx_var, ctx_std, cx_normed = sem("ctx_var"), sem("ctx_std"), sem("cx_normed")
        x1_ready, xn1_split = sem("x1_ready"), sem("xn1_split")
        ffn_consts = sem("ffn_consts")
        bT_full, bT_out = sem("bT_full"), sem("bT_out")
        xT_full, xT_out = sem("xT_full"), sem("xT_out")
        logits_full, logits_max, logits_exp = sem("logits_full"), sem("logits_max"), sem("logits_exp")
        mask_ready, rank_full = sem("mask_ready"), sem("rank_full")
        place_ready, diag_ready = sem("place_ready"), sem("diag_ready")
        onehot_ready, onehot_used = sem("onehot_ready"), sem("onehot_used")
        row_full, row_out, onehotT_ready = sem("row_full"), sem("row_out"), sem("onehotT_ready")
        tok_out = sem("tok_out")
        h_full, h_biased, h_ready = sem("h_full"), sem("h_biased"), sem("h_ready")
        y_full, y_biased, yrow_full, yrow_out, y_split = sem("y_full"), sem("y_biased"), sem("yrow_full"), sem("yrow_out"), sem("y_split")
        moe_full, moe_used = sem("moe_full"), sem("moe_used")
        ld_l1 = sem("ld_l1")
        ones1_ready = sem("ones1_ready")
        ctxT_full, ctxT_out = sem("ctxT_full"), sem("ctxT_out")
        batch_loaded = [sem(f"batch_loaded{i}") for i in range(2)]
        weights_split, tok_high, tok_split = sem("weights_split"), sem("tok_high"), sem("tok_split")
        proj_full, proj_high, proj_used = sem("proj_full"), sem("proj_high"), sem("proj_used")
        v1_mid, v1_split = sem("v1_mid"), sem("v1_split")
        s_full, s_exp, s_clip, s_low = sem("s_full"), sem("s_exp"), sem("s_clip"), sem("s_low")
        o_full, o_norm, oT_full, oT_out = sem("o_full"), sem("o_norm"), sem("oT_full"), sem("oT_out")
        out_full, out_used = sem("out_full"), sem("out_used")
        ld_f1, right_clear = sem("ld_f1"), sem("right_clear")
        w1T_full, w1T_out = sem("w1T_full"), sem("w1T_out")
        lt_full = sem("lt_full")
        sc_shifted, sc_exp, tw_ready = sem("sc_shifted"), sem("sc_exp"), sem("tw_ready")
        twT_full, twT_out = sem("twT_full"), sem("twT_out")
        base_full, base_out, base_added = sem("base_full"), sem("base_out"), sem("base_added")
        lin_full, lin_used = sem("lin_full"), sem("lin_used")

        block = ctx.enter_context(nc.Block())

        JOBS = [("w", 0)] + [(what, c) for c in range(CHUNKS) for what in ("cT", "xT", "q", "k", "v")]
        job_at = {job: n for n, job in enumerate(JOBS)}

        def hi_of(k):
            return pexp[k % PRING][:].bitcast(BF16).rearrange("p r n (t two) -> p r n t two", two=2)[:, :, :, :, 1]

        def clip_hi_of(m):
            return pclip[m % RING_B][:].bitcast(BF16).rearrange("p n r (t two) -> p n r t two", two=2)[:, :, :, :, 1]

        def proj_bank(n):
            return ps[:, (5, 7)[n % 2], :]

        def qk_pieces(n, pair):
            bank, slot = proj_bank(n), pair % RING_QK
            rows = [slice(HEADW_B * r, HEADW_B * (r + 1)) for r in range(2)]
            return [([q[rows[r], r, :] for q in q_parts[slot]], bank[rows[r], 0:SEQ]) for r in range(2)] + \
                   [([k[:] for k in k_parts[slot]], bank[:, SEQ:2 * SEQ])]

        def v_piece(par, j, at):
            t, half = divmod(j, 2)
            return v1[par][:, t, 8 * half:8 * half + 8, at:at + HEADW_B]

        def first_tokens(src):
            return src[:, 0:TPB, :].rearrange("p t n -> p (t n)")

        def by_head(bank):
            return bank.rearrange("p (h d) -> p h d", d=HEADW_B)

        def head_bank(k):
            return BANK_B[k % 2]

        @block.sync
        def _(sp):
            tok = lambda ap: ap.rearrange("b (t p) d -> p (b t) d", p=P)
            for c in range(CHUNKS):
                sp.dma_start(x[:, TPK * c:TPK * c + TPK, :], tok(I["x"])[:, TPK * c:TPK * c + TPK, :]).then_inc(ld_x, 16)
            for k, n in enumerate(("Wq", "Wk", "Wv")):
                sp.dma_start(w3[:, k, :], I["L0_xattn_" + n]).then_inc(ld_w, 16)
            sp.dma_start(cx[:], tok(I["ctx_1024"])).then_inc(ld_c, 16)
            for k, n in enumerate(("lambda_q1", "lambda_k1", "lambda_q2", "lambda_k2")):
                sp.dma_start(lam_in[:, k, :], I["L0_xattn_" + n].partition_broadcast(P)).then_inc(ld_small, 16)
            for k, n in enumerate(("g_xattn", "g_ffn")):
                sp.dma_start(gates[:, 2 * k:2 * k + 2], I[n].partition_broadcast(P)).then_inc(ld_small, 16)
            sp.dma_start(gate_w[:], I["L0_ffn_gate_w"]).then_inc(ld_ffn, 16)
            sp.dma_start(gate_b[:], I["L0_ffn_gate_b"].partition_broadcast(P)).then_inc(ld_ffn, 16)
            sp.dma_start(b1_in[:], I["L0_ffn_b1"].rearrange("e (c f) -> (e c) f", f=P)).then_inc(ld_ffn, 16)
            sp.dma_start(b2_in[:], I["L0_ffn_b2"]).then_inc(ld_ffn, 16)
            sp.dma_start(wq1[:], I["L1_xattn_Wq"]).then_inc(ld_l1, 16)
            sp.dma_start(wkv1[:], I["L1_xattn_Wkv"]).then_inc(ld_l1, 16)
            sp.dma_start(wo1[:], I["L1_xattn_Wo"].rearrange("(m p) d -> p m d", p=P)).then_inc(ld_l1, 16)
            for k, n in enumerate(("ln_l_w", "ln_l_b", "ln_c_w", "ln_c_b")):
                sp.dma_start(lnf[:, k:k + 1], I["L1_xattn_" + n].rearrange("(d o) -> d o", o=1)).then_inc(ld_l1, 16)
            sp.dma_start(bo1[:], I["L1_xattn_bo"].partition_broadcast(P)).then_inc(ld_l1, 16)
            sp.dma_start(wl_in[:], I["L1_ffn_W_lin"]).then_inc(ld_f1, 16)
            sp.dma_start(gw_in[:], I["L1_ffn_gate_w"]).then_inc(ld_f1, 16)
            sp.dma_start(gl[:, EXPERTS:].rearrange("p (e r) -> p e r", r=RANK),
                         I["L1_ffn_left"].rearrange("e d r -> d e r")).then_inc(ld_f1, 16)
            sp.wait_ge(right_clear, 1)
            for t in range(TPK):
                sp.dma_start(right[ER * t:ER * (t + 1), t, :], I["L1_ffn_right"].rearrange("e r o -> (e r) o")).then_inc(ld_f1, 16)
            sp.dma_start(blin[:], I["L1_ffn_b_lin"].partition_broadcast(P)).then_inc(ld_f1, 16)
            sp.wait_ge(fill_ready, 1)

            def store_fill(c, stored):
                for side in range(2):
                    sp.dma_start(qk_dram[side, :, KROWS * GROUPS:, BANK * c:BANK * c + BANK], mfill[:, side, :]).then_inc(stored, 16)

            store_fill(0, qk_first)

            def store_parts(cols, done, stored):
                for side, which in enumerate((Q_PARTS, K_PARTS)):
                    sp.wait_ge(qk_split, 2 * done - 1 + side)
                    for pair, part in enumerate(which):
                        rows = slice(pair * SUBW * GROUPS, (pair + 1) * SUBW * GROUPS)
                        sp.dma_start(qk_dram[side, :, rows, cols], parts[:, side, part, cols]).then_inc(stored, 16)

            store_parts(slice(0, BANK), 1, qk_first)
            sp.wait_ge(qk_first, 16 * 2 * (PAIRS + 1))
            sp.wait_ge(v_split, 1)

            def load_batch(b, s):
                for r in range(ROWT):
                    row = P // ROWT * r
                    for side, dst in enumerate((qaug[s][row:row + KROWS + MROWS, :, :],
                                                kaug[s][row:row + KROWS + MROWS, :, r, :])):
                        sp.dma_start(dst, qk_dram[side, r, :, bass.ds(b * SEQ, SEQ)].rearrange(
                            "(c g) t -> c g t", g=GROUPS)).then_inc(aug_loaded[s], 16)
                sp.dma_start(vbuf[s][:], vp[:, bass.ds(b * TPB, TPB), :, :]).then_inc(aug_loaded[s], 16)

            def m_rows(b, s, half):
                sp.wait_ge(m_copied, b * 2 + half + 1)
                for r in range(ROWT):
                    row = P // ROWT * r + KROWS
                    sp.dma_start(qaug[s][row:row + MROWS, HALF * half:HALF * half + HALF, :],
                                 mT[half][r * MROWS * HALF:(r + 1) * MROWS * HALF, :]).then_inc(m_loaded[s][half], 16)

            assert 2 * SEQ == BANK
            for b in range(2):
                sp.wait_ge(slot_clear, b + 1)
                load_batch(b, b)
            for c in range(1, CHUNKS):
                store_fill(c, qk_rest)
            store_parts(slice(BANK, TILES * P), CHUNKS, qk_rest)
            m_rows(0, 0, 0)
            m_rows(0, 0, 1)
            sp.wait_ge(qk_rest, 16 * 2 * (PAIRS + CHUNKS - 1))
            sp.wait_ge(v_split, CHUNKS)
            sp.wait_ge(slot_clear, SLOTS)
            load_batch(2, 2)
            m_rows(1, 1, 0)
            with sp.Fori(0, (BATCH - 2) // SLOTS) as i:
                for j in range(1, SLOTS + 1):
                    b = i * SLOTS + j
                    m_rows(b, j % SLOTS, 1)
                    sp.wait_ge(pv_done, b * B_TILES)
                    load_batch(b + 2 if j < SLOTS else i * 2 + 5, (j + 2) % SLOTS)
                    m_rows(b + 1, (j + 1) % SLOTS, 0)
            m_rows(BATCH - 1, (BATCH - 1) % SLOTS, 1)

            sp.wait_ge(x1_ready, 1)
            sp.dma_start(w1[:], I["L0_ffn_w1"].rearrange("e d f -> d e f")).then_inc(ld_experts, 16)
            sp.dma_start(w2[:], I["L0_ffn_w2"].rearrange("e (c f) d -> f (e c) d", f=P)).then_inc(ld_experts, 16)

            def load_tokens(b, par):
                for side, src in enumerate((latT, cT)):
                    sp.dma_start(tok_b[par][:, side, :].rearrange("p (t n) -> p t n", n=P),
                                 src[:, bass.ds(b * TPB, TPB), :]).then_inc(batch_loaded[par], 16)

            sp.wait_ge(ctxT_out, CHUNKS)
            sp.wait_ge(xT_out, 2 * CHUNKS)
            load_tokens(1, 1)
            with sp.Fori(0, (BATCH - 2) // 2) as i:
                for j in range(2):
                    sp.wait_ge(tok_split, i * 2 + (j + 1))
                    load_tokens(i * 2 + (j + 2), j)
            for c in range(CHUNKS):
                sp.wait_ge(lin_used, c + 1)
                sp.dma_start(tok(out)[:, TPK * c:TPK * c + TPK, :], x[:, TPK * c:TPK * c + TPK, :]).then_inc(out_stored, 16)
            sp.wait_ge(out_stored, 16 * CHUNKS)

        @block.gpsimd
        def _(pool):
            c = Chain(pool, pool_self)
            nc.gpsimd.memset(table_in[:], 1.0)
            c.link(nc.gpsimd.memset(ident[:], 0.0))
            c.link(nc.gpsimd.affine_select(out=ident[:], in_=ident[:], compare_op=ALU.not_equal, fill=1.0, base=0,
                                           pattern=[[-1, P]], channel_multiplier=1))
            nc.gpsimd.tensor_copy(identb[:], ident[:]).then_inc(consts_ready, 1)
            c.link(nc.gpsimd.memset(mfill[:, 0, :], 0.0))
            nc.gpsimd.memset(mfill[:, 1, :], 1.0).then_inc(fill_ready, 1)
            nc.gpsimd.memset(right[:], 0.0).then_inc(right_clear, 1)
            for s in range(SLOTS):
                nc.gpsimd.memset(qaug[s][:].bitcast(F32), 0.0)
                nc.gpsimd.memset(kaug[s][:].bitcast(F32), 0.0).then_inc(slot_clear, 1)
                if s == 0:
                    c.link(nc.gpsimd.memset(vp[:, :, :, VCOLS - 1:VCOLS], 1.0))
            for n in range(CHUNKS):
                pool.wait_ge(job_out, job_at[("v", n)] + 1)
                tiles = slice(TPK * n, TPK * n + TPK)
                heads = lambda ap: ap[:, tiles, :].rearrange("p t (h w) -> p (t h) w", w=HEADW_A)
                vpart = [vp[:, tiles, :, :].rearrange("p t h c -> p (t h) c")[:, :, HEADW_A * i:HEADW_A * (i + 1)] for i in range(VPARTS)]
                c.link(nc.gpsimd.tensor_copy(vpart[0], heads(v32)))
                c.link(nc.gpsimd.tensor_tensor(heads(vres), heads(v32), vpart[0], ALU.subtract))
                c.link(nc.gpsimd.tensor_copy(vpart[1], heads(vres)))
                nc.gpsimd.tensor_tensor(vpart[2], heads(vres), vpart[1], ALU.subtract).then_inc(v_split, 1)

            nc.gpsimd.iota(iota_e[:], [[0, TILES], [1, EXPERTS]], base=0, channel_multiplier=0, allow_small_or_imprecise_dtypes=True)
            nc.gpsimd.iota(place0[:], [[CAP, EXPERTS], [0, TILES]], base=0, channel_multiplier=0, allow_small_or_imprecise_dtypes=True)
            nc.gpsimd.iota(places[:], [[1, EROWS]], base=0, channel_multiplier=0, allow_small_or_imprecise_dtypes=True)
            nc.gpsimd.iota(place_p[:], [[P, ECH]], base=0, channel_multiplier=1, allow_small_or_imprecise_dtypes=True)
            nc.gpsimd.memset(onesh[:], 1.0)
            nc.gpsimd.memset(onesb[:], 1.0)
            c.link(nc.gpsimd.memset(keep_sum[:], 1.0))
            c.link(nc.gpsimd.memset(keep_sum[:, :, 0:1], 0.0))
            nc.gpsimd.affine_select(out=before[:], in_=onesb[:], compare_op=ALU.is_gt, fill=0.0, base=0,
                                    pattern=[[1, P]], channel_multiplier=-1).then_inc(ffn_consts, 1)

            def step(b, s, turn, first, last):
                for k in range(B_TILES):
                    if not lo_on_vector(b, k):
                        pool.wait_ge(exp_done, b * B_TILES + k + 1)
                        nc.gpsimd.tensor_tensor(plo[k % PRING][:], pexp[k % PRING][:], hi_of(k), ALU.subtract).then_inc(lo_pool, 1)

            batches(pool, step)
            pool.wait_ge(x1_ready, 1)
            pool.wait_ge(xn_ready, CHUNKS * 2)
            c.link(nc.gpsimd.tensor_copy(xn1_high[:], xn1[:]))
            nc.gpsimd.tensor_tensor(xn1_low[:], xn1[:], xn1_high[:], ALU.subtract).then_inc(xn1_split, 1)
            pool.wait_ge(ld_l1, 16 * 8)
            pool.wait_ge(place_ready, 1)
            nc.gpsimd.tensor_tensor(diag[:], ident[:].unsqueeze(1).broadcast_to([P, TILES, P]),
                                    place[:].unsqueeze(2).broadcast_to([P, TILES, P]), ALU.mult).then_inc(diag_ready, 1)
            for whole, part in ((wq1, wq_parts), (wkv1, wkv_parts)):
                c.link(nc.gpsimd.tensor_copy(part[0][:], whole[:]))
                last = nc.gpsimd.tensor_tensor(part[1][:], whole[:], part[0][:], ALU.subtract)
            last.then_inc(weights_split, 1)
            pool.wait_ge(moe_used, TILES)
            for parts_of in q_parts:
                for part in parts_of:
                    nc.gpsimd.memset(part[:].bitcast(F32), 0.0)
            for par in range(2):
                last = nc.gpsimd.memset(v1[par][:, :, :, HEADW_B:HEADC_B], 1.0)
            last.then_inc(ones1_ready, 1)

            def split_v(b, par, j):
                pool.wait_ge(v1_mid, b * JOBS_V + (j + 1))
                nc.gpsimd.tensor_tensor(v_piece(par, j, VLOW_B), by_head(v1res[j % 2][:]), v_piece(par, j, VMID_B),
                                        ALU.subtract).then_inc(v1_split, 1)

            for j in range(JOBS_V):
                split_v(0, 0, j)

            def step(b, par, first, last):
                for m in range(PAIRS_B):
                    pool.wait_ge(s_clip, b * PAIRS_B + (m + 1))
                    nc.gpsimd.tensor_tensor(pclo[m % RING_B][:], pclip[m % RING_B][:], clip_hi_of(m), ALU.subtract).then_inc(s_low, 1)
                    for what, j, ahead in jobs_with(m, last):
                        if what == "v":
                            split_v(b + ahead, 1 - par, j)

            batch_pairs(pool, step)
            pool.wait_ge(ld_f1, 16 * (4 + TPK))
            c.link(nc.gpsimd.tensor_scalar(blin[:], blin[:], tg[:, 3:4], None, ALU.mult))
            pool.wait_ge(xn_ready, CHUNKS * 4)
            c.link(nc.gpsimd.tensor_tensor(x[:], x[:], blin[:].unsqueeze(1).broadcast_to([P, TILES, DIM]), ALU.add))
            for n in range(CHUNKS):
                pool.wait_ge(base_out, n + 1)
                tiles = slice(TPK * n, TPK * n + TPK)
                nc.gpsimd.tensor_tensor(x[:, tiles, :], x[:, tiles, :], base[:, tiles, :], ALU.add).then_inc(base_added, 1)

        @block.tensor
        def _(pe):
            pe.wait_ge(consts_ready, 1)
            for n, (what, c) in enumerate(JOBS):
                bank = ps[:, n % 8, :]
                if n >= 8:
                    pe.wait_ge(job_out, n - 7)
                if what == "w":
                    pe.wait_ge(ld_w, 48)
                    for k in range(3):
                        mm = nc.tensor.transpose(bank[:, P * k:P * k + P], w3[:, k, :], ident[:])
                elif what in ("xT", "cT"):
                    if what == "xT":
                        pe.wait_ge(xn_ready, c + 1)
                    else:
                        pe.wait_ge(ld_c, 16)
                    src = xn if what == "xT" else cx
                    for t in range(TPK):
                        mm = nc.tensor.transpose(bank[:, P * t:P * t + P], src[:, TPK * c + t, :], ident[:])
                else:
                    need = {"q": ("xT", c), "k": ("cT", c), "v": ("cT", c)}[what]
                    pe.wait_ge(job_out, job_at[need] + 1)
                    if what == "v":
                        for t in range(TPK):
                            mm = nc.tensor.matmul(bank[:, P * t:P * t + P], cT[:, TPK * c + t, :], w3T[:, 2, :],
                                                  start=True, stop=True)
                    else:
                        src = (xT if what == "q" else cT)[:, TPK * c:TPK * c + TPK, :]
                        mm = nc.tensor.matmul(bank, w3T[:, 0 if what == "q" else 1, :], src, start=True, stop=True)
                mm.then_inc(job_full, 1)

            def score_a(b, s, a):
                g, r = a // ROWT, a % ROWT
                if not (isinstance(b, int) and b * A_TILES + a < 2):
                    pe.wait_ge(a_used, b * A_TILES + (a - 1))
                for t in range(TPB):
                    mm = nc.tensor.matmul(ps[:, BANK_A[a % 2], SEQ * t:SEQ * t + SEQ],
                                          qaug[s][:, g, P * t:P * t + P], kaug[s][:, g, r, :],
                                          start=True, stop=True)
                mm.then_inc(a_full, 1)

            def turn_max(b, half):
                pe.wait_ge(m_split, b * 2 + half + 1)
                if not (isinstance(b, int) and b * 2 + half < 1):
                    pe.wait_ge(m_copied, b * 2 + half)
                for t in range(TPB):
                    mm = nc.tensor.transpose(
                        ps[0:ROWT * MROWS * HALF, BANK_M, 0:SEQ // 2].bitcast(BF16)[:, P * t:P * t + P],
                        mpart[half][:, t, :, :, :], identb[:])
                mm.then_inc(m_turned, 1)

            def score_b(b, s, turn, k):
                g = k // 2
                if k == 0:
                    pe.wait_ge(aug_loaded[s], (turn + 1) * (16 * LOADS))
                    pe.wait_ge(m_loaded[s][0], (turn + 1) * (16 * ROWT))
                if k == B_TILES // 2:
                    pe.wait_ge(m_loaded[s][1], (turn + 1) * (16 * ROWT))
                if not (isinstance(b, int) and b * B_TILES + k < 2):
                    pe.wait_ge(exp_done, b * B_TILES + (k - 1))
                for t in range(TPB):
                    for r in range(2):
                        mm = nc.tensor.matmul(ps[:, head_bank(k) + r, SEQ * t:SEQ * t + SEQ],
                                              kaug[s][:, g, 2 * (k % 2) + r, P * t:P * t + P], qaug[s][:, g, :],
                                              start=True, stop=True)
                mm.then_inc(b_full, 1)

            def times_v(b, s, k):
                idx = b * B_TILES
                pe.wait_ge(exp_done, idx + (k + 1))
                g, q = k // 2, k // QUARTER
                dve_lo = sum(lo_on_vector(b, t) for t in range(k + 1))
                if lo_on_vector(b, k):
                    pe.wait_ge(lo_dve, b * LO_V + dve_lo)
                else:
                    pe.wait_ge(lo_pool, b * LO_G + (k + 1 - dve_lo))
                if k % QUARTER == 0 and not (isinstance(b, int) and b * 4 + q < 1):
                    pe.wait_ge(o_saved, b * 4 + q)
                for r in range(2):
                    h4 = 2 * (k % 2) + r
                    v = vbuf[s][:, :, (GROUPS * h4 + g) // 2, :]
                    for t in range(TPB):
                        at = ((t * ROWT + h4) * 2 + g % 2) * VCOLS
                        for nt in range(TPB):
                            for lo in range(2):
                                src = plo[k % PRING][:, r, nt, :] if lo else hi_of(k)[:, r, nt, :]
                                mm = nc.tensor.matmul(ps[:, BANK_O, at:at + VCOLS], src[:, P * t:P * t + P],
                                                      v[:, nt, :], start=nt == 0 and lo == 0,
                                                      stop=nt == TPB - 1 and lo == 1)
                mm.then_inc(pv_done, 1)

            def turn_x(src, n):
                for i in range(CHUNKS):
                    pe.wait_ge(xn_ready, CHUNKS * n + i + 1)
                    for t in range(TPK):
                        mm = nc.tensor.transpose(ps[:, i, P * t:P * t + P], src[:, TPK * i + t, :], ident[:])
                    mm.then_inc(xT_full, 1)

            pe.wait_ge(job_out, len(JOBS))
            pe.wait_ge(aug_loaded[0], 16 * LOADS)
            for a in range(A_TILES):
                score_a(0, 0, a)
                if a == A_TILES // 2 + 3:
                    turn_max(0, 0)
            turn_max(0, 1)

            def step(b, s, turn, first, last):
                for k in range(B_TILES):
                    if k == 1 and not first:
                        turn_max(b, 1)
                    score_b(b, s, turn, k)
                    if not last:
                        if k == 0:
                            pe.wait_ge(aug_loaded[(s + 1) % SLOTS], (turn + (s + 1) // SLOTS + 1) * (16 * LOADS))
                        score_a(b + 1, (s + 1) % SLOTS, 2 * k)
                        score_a(b + 1, (s + 1) % SLOTS, 2 * k + 1)
                        if k == B_TILES // 2 + 1:
                            turn_max(b + 1, 0)
                    if k >= LAG:
                        times_v(b, s, k - LAG)
                    elif not first:
                        times_v(b - 1, (s - 1) % SLOTS, B_TILES - LAG + k)

            batches(pe, step)
            for k in range(B_TILES - LAG, B_TILES):
                times_v(BATCH - 1, (BATCH - 1) % SLOTS, k)

            pe.wait_ge(ld_ffn, 16 * 4)
            pe.wait_ge(x1_ready, 1)
            nc.tensor.transpose(ps[:, 4, 0:EXPERTS * FCH], b1_in[:], ident[0:EXPERTS * FCH, 0:EXPERTS * FCH])
            nc.tensor.transpose(ps[:, 4, EXPERTS * FCH:EXPERTS * FCH + EXPERTS], b2_in[:],
                                ident[0:EXPERTS, 0:EXPERTS]).then_inc(bT_full, 1)
            turn_x(xn1, 1)
            pe.wait_ge(xT_out, CHUNKS)
            for t in range(TILES):
                mm = nc.tensor.matmul(ps[:, 5, EXPERTS * t:EXPERTS * t + EXPERTS], xT1[:, t, :], gate_w[:], start=True, stop=True)
            mm.then_inc(logits_full, 1)
            pe.wait_ge(mask_ready, 1)
            pe.wait_ge(ffn_consts, 1)
            nc.tensor.matmul(ps[:, 6, 0:EXPERTS * TILES], before[:], mask[:], start=True, stop=False)
            nc.tensor.matmul(ps[:, 6, 0:EXPERTS * TILES], onesb[:], prior[:], start=False, stop=True).then_inc(rank_full, 1)
            pe.wait_ge(xn1_split, 1)
            for t in range(TILES):
                pe.wait_ge(onehot_ready, t + 1)
                if t == 0:
                    pe.wait_ge(bT_out, 1)
                for part in (xn1_high, xn1_low):
                    for half in range(2):
                        mm = nc.tensor.matmul(ps[:, 4 + half, 0:EHALF], part[:, t, :], onehot[t % 4][:, EHALF * half:EHALF * half + EHALF],
                                              start=t == 0 and part is xn1_high, stop=t == TILES - 1 and part is xn1_low)
                mm.then_inc(onehot_used, 1)
            pe.wait_ge(diag_ready, 1)
            for n in range(CHUNKS):
                nc.tensor.matmul(ps[:, ROW_BANKS[n], :], onesh[:], diag[:, TPK * n:TPK * n + TPK, :], start=True, stop=True).then_inc(row_full, 1)
            pe.wait_ge(tok_out, 1)
            pe.wait_ge(ld_experts, 16 * 2)
            for e in range(EXPERTS):
                if e in ROW_BANKS:
                    pe.wait_ge(row_out, ROW_BANKS.index(e) + 1)
                if e >= 4:
                    pe.wait_ge(h_biased, e - 3)
                for f in range(FCH):
                    mm = nc.tensor.matmul(ps[:, e % 4, CAP * f:CAP * f + CAP], w1[:, e, P * f:P * f + P],
                                          tokT[:, CAP * e:CAP * e + CAP], start=True, stop=True)
                mm.then_inc(h_full, 1)
            pe.wait_ge(row_out, CHUNKS)
            for e in range(EXPERTS):
                pe.wait_ge(h_ready, e + 1)
                bank, at = 6 + e // 4, CAP * (e % 4)
                for f in range(FCH):
                    mm = nc.tensor.matmul(ps[:, bank, at:at + CAP], w2[:, FCH * e + f, :], hidden[:, FCH * e + f, :],
                                          start=f == 0, stop=f == FCH - 1)
                if e % 4 == 3:
                    mm.then_inc(y_full, 1)
            pe.wait_ge(y_biased, 2)
            for j in range(ECH):
                mm = nc.tensor.transpose(ps[:, 4 + j // 4, P * (j % 4):P * (j % 4) + P], yT[:, P * j:P * j + P], ident[:])
            mm.then_inc(yrow_full, 1)
            pe.wait_ge(yrow_out, 1)
            for i in range(CHUNKS):
                pe.wait_ge(cx_normed, i + 1)
                for t in range(TPK):
                    mm = nc.tensor.transpose(ps[:, 4 + i, P * t:P * t + P], cx[:, TPK * i + t, :], ident[:])
                mm.then_inc(ctxT_full, 1)
            pe.wait_ge(y_split, 1)
            pe.wait_ge(onehotT_ready, ECH)
            for t in range(TILES):
                if t >= 4:
                    pe.wait_ge(moe_used, t - 3)
                for j in range(ECH):
                    for part in range(3):
                        mm = nc.tensor.matmul(ps[:, t % 4, 0:DIM], onehotT[:, j, P * t:P * t + P], ypart[:, part, j, :],
                                              start=j == 0 and part == 0, stop=j == ECH - 1 and part == 2)
                mm.then_inc(moe_full, 1)

            turn_x(xn2, 2)
            pe.wait_ge(ld_l1, 16 * 8)
            pe.wait_ge(xT_out, 2 * CHUNKS)
            pe.wait_ge(ctxT_out, CHUNKS)
            pe.wait_ge(ones1_ready, 1)

            def project(count, n, what, j, b, par):
                if not (isinstance(count, int) and count < 2):
                    pe.wait_ge(proj_used, count - 1)
                bank = proj_bank(n)
                products = list(enumerate(((0, 0), (0, 1), (1, 0))))
                if what == "qk":
                    for side, w in enumerate((wq_parts, wkv_parts)):
                        for i, (a, c) in products:
                            mm = nc.tensor.matmul(bank[:, SEQ * side:SEQ * side + SEQ], w[a][:, P * j:P * j + P],
                                                  tok_parts[par][c][:, side, :], start=i == 0, stop=i == 2)
                else:
                    t, half = divmod(j, 2)
                    at = WIDE + BANK * half
                    for i, (a, c) in products:
                        mm = nc.tensor.matmul(bank, tok_parts[par][a][:, 1, P * t:P * t + P], wkv_parts[c][:, at:at + BANK],
                                              start=i == 0, stop=i == 2)
                mm.then_inc(proj_full, 1)

            def scores(b, m, last):
                pe.wait_ge(proj_used, jobs_for_pair(b, m, last))
                if not (isinstance(b, int) and b * PAIRS_B + m < 2):
                    pe.wait_ge(s_exp, b * PAIRS_B + (m - 1))
                slot = m % RING_QK
                for t in range(TPB):
                    for i, (a, c) in enumerate(((0, 0), (0, 1), (1, 0))):
                        mm = nc.tensor.matmul(ps[:, 2 * (m % 2) + t, :], k_parts[slot][a][:, P * t:P * t + P],
                                              q_parts[slot][c][:], start=i == 0, stop=i == 2)
                mm.then_inc(s_full, 1)

            def apply_v(b, par, m):
                if m == 0:
                    pe.wait_ge(v1_split, (b + 1) * JOBS_V)
                pe.wait_ge(s_low, b * PAIRS_B + (m + 1))
                if not (isinstance(b, int) and b * PAIRS_B + m < 1):
                    pe.wait_ge(o_norm, b * PAIRS_B + m)
                for t in range(TPB):
                    for r in range(2):
                        at, v = (2 * t + r) * HEADC_B, v1[par][:, :, 2 * m + r, :]
                        whole, width = ps[:, 4, at:at + HEADC_B], ps[:, 4, at:at + HEADW_B]
                        for nt in range(TPB):
                            high, low = clip_hi_of(m)[:, nt, r, P * t:P * t + P], pclo[m % RING_B][:, nt, r, P * t:P * t + P]
                            nc.tensor.matmul(whole, high, v[:, nt, 0:HEADC_B], start=nt == 0, stop=False)
                            nc.tensor.matmul(width, high, v[:, nt, VMID_B:VLOW_B], start=False, stop=False)
                            nc.tensor.matmul(width, high, v[:, nt, VLOW_B:VCOLS_B], start=False, stop=False)
                            nc.tensor.matmul(width, low, v[:, nt, VMID_B:VLOW_B], start=False, stop=False)
                            mm = nc.tensor.matmul(whole, low, v[:, nt, 0:HEADC_B], start=False, stop=nt == TPB - 1)
                mm.then_inc(o_full, 1)

            def turn_o(b, par, m):
                pe.wait_ge(o_norm, b * PAIRS_B + (m + 1))
                if not (isinstance(b, int) and b * PAIRS_B + m < 1):
                    pe.wait_ge(oT_out, b * PAIRS_B + m)
                if m == 0 and not (isinstance(b, int) and b == 0):
                    pe.wait_ge(out_used, b)
                for t in range(TPB):
                    mm = nc.tensor.transpose(ps[:, 6, P * t:P * t + P],
                                             on[m % 2][:, t, :, :].rearrange("p r d -> p (r d)"), ident[:])
                mm.then_inc(oT_full, 1)

            def output(b, par):
                pe.wait_ge(oT_out, (b + 1) * PAIRS_B)
                for t in range(TPB):
                    for m in range(PAIRS_B):
                        mm = nc.tensor.matmul(ps[:, 6, P * t:P * t + P], oT[par][:, m, P * t:P * t + P], wo1[:, m, :],
                                              start=m == 0, stop=m == PAIRS_B - 1)
                mm.then_inc(out_full, 1)

            pe.wait_ge(weights_split, 1)
            pe.wait_ge(tok_split, 1)
            for n, (what, j) in enumerate(JOBS_FIRST):
                project(n, n, what, j, 0, 0)

            def earlier(do, b, par, m, lag, first):
                if m >= lag:
                    do(b, par, m - lag)
                elif not first:
                    do(b - 1, 1 - par, PAIRS_B - lag + m)

            def step(b, par, first, last):
                n = 0
                for m in range(PAIRS_B):
                    scores(b, m, last)
                    for what, j, ahead in jobs_with(m, last):
                        if what == "v" and j == 0:
                            pe.wait_ge(tok_split, b + 2)
                        project(job_count(b, 0, last) + n, n, what, j, b + ahead, par if ahead == 0 else 1 - par)
                        n += 1
                        if what == "qk":
                            if m == LAG_B + 1 and not first:
                                output(b - 1, 1 - par)
                            earlier(apply_v, b, par, m, LAG_B, first)
                    if not jobs_with(m, last):
                        earlier(apply_v, b, par, m, LAG_B, first)
                    earlier(turn_o, b, par, m, LAG_B + 1, first)

            batch_pairs(pe, step)
            last_b, par = BATCH - 1, (BATCH - 1) % 2
            for m in range(LAG_B + 1):
                if m < LAG_B:
                    apply_v(last_b, par, PAIRS_B - LAG_B + m)
                turn_o(last_b, par, PAIRS_B - LAG_B - 1 + m)
            output(last_b, par)

            pe.wait_ge(ld_f1, 16 * (4 + TPK))
            pe.wait_ge(out_used, BATCH)
            nc.tensor.transpose(ps[:, 4, 0:P], wl_in[:], ident[:])
            nc.tensor.transpose(ps[:, 4, P:P + EXPERTS], gw_in[:], ident[0:EXPERTS, 0:EXPERTS]).then_inc(w1T_full, 1)
            turn_x(xn3, 3)
            pe.wait_ge(w1T_out, 1)
            pe.wait_ge(xT_out, 3 * CHUNKS)
            for t in range(TILES):
                mm = nc.tensor.matmul(ps[:, 5 + t // 8, (EXPERTS + ER) * (t % 8):(EXPERTS + ER) * (t % 8 + 1)], xT3[:, t, :], gl[:],
                                      start=True, stop=True)
            mm.then_inc(lt_full, 1)
            for n in range(CHUNKS):
                for t in range(TPK):
                    bank = ps[:, n, P * t:P * t + P]
                    mm = nc.tensor.matmul(bank, xT3[:, TPK * n + t, :], wlT[:], start=True, stop=True)
                mm.then_inc(base_full, 1)
            pe.wait_ge(tw_ready, 1)
            for n in range(CHUNKS):
                mm = nc.tensor.transpose(ps[:, 4, P * n:P * n + P], tw[:, TPK * n:TPK * n + TPK, :].rearrange("p t n -> p (t n)"), ident[:])
            mm.then_inc(twT_full, 1)
            pe.wait_ge(base_out, CHUNKS)
            pe.wait_ge(twT_out, 1)
            for n in range(CHUNKS):
                nc.tensor.matmul(ps[:, n, :], twT[:, P * n:P * n + P], right[:], start=True, stop=True).then_inc(lin_full, 1)

        @block.scalar
        def _(act):
            c = Chain(act, act_self)

            def job(what, n):
                act.wait_ge(job_full, job_at[(what, n)] + 1)
                return ps[:, job_at[(what, n)] % 8, :]

            def root(n, twice=False):
                act.wait_ge(var_ready, n + 1)
                if twice:
                    root_of = nc.scalar.activation(std[:], mv[:, :, 1], ACT.Sqrt, bias=eps[:, 1:2], scale=1 + EPS)
                else:
                    root_of = nc.scalar.activation(std[:], mv[:, :, 1], ACT.Sqrt, bias=eps[:, 0:1])
                root_of.then_inc(std_ready, 1)

            def load_table(func):
                if c.n:
                    c.follow()
                c.mark(nc.scalar.activation(table_in[:], table_in[:], func))

            root(0)
            src = job("w", 0)
            for k in range(2):
                nc.scalar.activation(w3T[:, k, :].rearrange("p (r d g) -> p r g d", r=ROWT, g=GROUPS),
                                     src[:, P * k:P * k + P].rearrange("p (r g d) -> p r g d", r=ROWT, g=GROUPS), ACT.Copy)
            nc.scalar.activation(w3T[:, 2, :], src[:, 2 * P:3 * P], ACT.Copy).then_inc(job_out, 1)
            for what, n in JOBS[1:]:
                tiles, cols = slice(TPK * n, TPK * n + TPK), slice(BANK * n, BANK * n + BANK)
                dst = {"xT": xT[:, tiles, :], "cT": cT[:, tiles, :], "v": v32[:, tiles, :],
                       "q": qk32[:, 0, cols], "k": qk32[:, 1, cols]}[what]
                nc.scalar.activation(dst, job(what, n), ACT.Copy).then_inc(job_out, 1)
            act.wait_ge(lam_sum, 1)
            nc.scalar.activation(tg[:], gates[:], ACT.Tanh)
            nc.scalar.activation(lam_e[:], lam_s[:], ACT.Exp).then_inc(lam_exp, 1)

            def copy_max(b, half):
                act.wait_ge(m_turned, b * 2 + half + 1)
                nc.scalar.activation(mT[half][:], ps[0:ROWT * MROWS * HALF, BANK_M, 0:SEQ // 2].bitcast(BF16), ACT.Copy).then_inc(m_copied, 1)

            def save_o(b, s, q):
                act.wait_ge(pv_done, b * B_TILES + (q + 1) * QUARTER)
                nc.scalar.activation(oraw[s][:, :, q, :],
                                     ps[:, BANK_O, 0:TPB * ROWT * 2 * VCOLS].rearrange("p (a c) -> p a c", c=2 * VCOLS),
                                     ACT.Copy).then_inc(o_saved, 1)

            def step(b, s, turn, first, last):
                for k in range(B_TILES):
                    act.wait_ge(b_full, b * B_TILES + (k + 1))
                    if not (isinstance(b, int) and b * B_TILES + k < PRING):
                        act.wait_ge(pv_done, b * B_TILES + (k + 1 - PRING))
                    bank = head_bank(k)
                    nc.scalar.activation(pexp[k % PRING][:], ps[:, bank:bank + 2, :].rearrange("p r (n t) -> p r n t", n=TPB),
                                         ACT.Exp, scale=SCALE_A).then_inc(exp_done, 1)
                    if k == 1 and not first:
                        copy_max(b, 1)
                    if k == B_TILES // 2 + 2 and not last:
                        copy_max(b + 1, 0)
                    if k % QUARTER == 0:
                        q = k // QUARTER - 2
                        if q >= 0:
                            save_o(b, s, q)
                        elif not first:
                            save_o(b - 1, (s - 1) % SLOTS, q + 4)

            act.wait_ge(qk_first, 16 * 2 * (PAIRS + 1))
            act.wait_ge(qk_rest, 16 * 2 * (PAIRS + CHUNKS - 1))
            act.wait_ge(v_split, CHUNKS)
            copy_max(0, 0)
            copy_max(0, 1)
            batches(act, step)
            save_o(BATCH - 1, (BATCH - 1) % SLOTS, 2)
            save_o(BATCH - 1, (BATCH - 1) % SLOTS, 3)

            load_table(ACT.Sqrt)
            act.wait_ge(bT_full, 1)
            nc.scalar.activation(b1T[:], ps[:, 4, 0:EXPERTS * FCH], ACT.Copy)
            nc.scalar.activation(b2T[:], ps[:, 4, EXPERTS * FCH:EXPERTS * FCH + EXPERTS], ACT.Copy).then_inc(bT_out, 1)
            root(1)
            for n in range(CHUNKS):
                act.wait_ge(xT_full, n + 1)
                nc.scalar.activation(xT1[:, TPK * n:TPK * n + TPK, :], ps[:, n, :], ACT.Copy).then_inc(xT_out, 1)
            act.wait_ge(ctx_var, 1)
            nc.scalar.activation(std_c[:], mv_c[:, :, 1], ACT.Sqrt, bias=eps[:, 0:1]).then_inc(ctx_std, 1)
            load_table(ACT.Exp)
            act.wait_ge(logits_max, 1)
            nc.scalar.activation(lg[:], lg[:], ACT.Exp).then_inc(logits_exp, 1)
            load_table(ACT.Gelu_apprx_tanh)
            act.wait_ge(onehot_used, TILES)
            for half in range(2):
                last = nc.scalar.activation(tokT[:, EHALF * half:EHALF * half + EHALF], ps[:, 4 + half, 0:EHALF], ACT.Copy)
            last.then_inc(tok_out, 1)
            for n in range(CHUNKS):
                act.wait_ge(row_full, n + 1)
                nc.scalar.activation(place_row[:, BANK * n:BANK * n + BANK], ps[:, ROW_BANKS[n], :], ACT.Copy).then_inc(row_out, 1)
            for e in range(EXPERTS):
                act.wait_ge(h_biased, e + 1)
                nc.scalar.activation(hidden[:, FCH * e:FCH * e + FCH, :], hidden[:, FCH * e:FCH * e + FCH, :],
                                     ACT.Gelu_apprx_tanh).then_inc(h_ready, 1)
            act.wait_ge(yrow_full, 1)
            nc.scalar.activation(yrow[:, 0:4, :], ps[:, 4, :], ACT.Copy)
            nc.scalar.activation(yrow[:, 4:ECH, :], ps[:, 5, 0:P], ACT.Copy).then_inc(yrow_out, 1)
            act.wait_ge(ld_l1, 16 * 8)
            for n in range(CHUNKS):
                act.wait_ge(ctxT_full, n + 1)
                nc.scalar.activation(cT[:, TPK * n:TPK * n + TPK, :], ps[:, 4 + n, :], ACT.Identity,
                                     bias=lnf[:, 3:4], scale=lnf[:, 2:3]).then_inc(ctxT_out, 1)
            load_table(ACT.Sqrt)

            act.wait_ge(ld_l1, 16 * 8)
            root(2, twice=True)
            for n in range(CHUNKS):
                act.wait_ge(xT_full, CHUNKS + n + 1)
                nc.scalar.activation(latT[:, TPK * n:TPK * n + TPK, :], ps[:, n, :], ACT.Identity,
                                     bias=lnf[:, 1:2], scale=lnf[:, 0:1]).then_inc(xT_out, 1)
            def split_tokens(b, par):
                if isinstance(b, int) and b == 0:
                    act.wait_ge(xT_out, CHUNKS + 1)
                    act.wait_ge(ctxT_out, 1)
                    for side, src in enumerate((latT, cT)):
                        last = nc.scalar.activation(tok_parts[par][0][:, side, :], first_tokens(src), ACT.Copy)
                    last.then_inc(tok_high, 1)
                    return
                act.wait_ge(batch_loaded[par], (b - par) * 16 + par * 32)
                nc.scalar.activation(tok_parts[par][0][:], tok_b[par][:], ACT.Copy).then_inc(tok_high, 1)

            def copy_proj(count, n, what, j, par):
                act.wait_ge(proj_full, count + 1)
                if what == "qk":
                    for dst, src in qk_pieces(n, j):
                        last = nc.scalar.activation(dst[0], src, ACT.Copy)
                else:
                    last = nc.scalar.activation(v_piece(par, j, 0), by_head(proj_bank(n)), ACT.Copy)
                last.then_inc(proj_high, 1)

            def copy_oT(b, par, m):
                act.wait_ge(oT_full, b * PAIRS_B + (m + 1))
                nc.scalar.activation(oT[par][:, m, :], ps[:, 6, 0:SEQ], ACT.Copy).then_inc(oT_out, 1)

            act.wait_ge(ones1_ready, 1)
            split_tokens(0, 0)
            for n, (what, j) in enumerate(JOBS_FIRST):
                copy_proj(n, n, what, j, 0)

            def step(b, par, first, last):
                n = 0
                for m in range(PAIRS_B):
                    act.wait_ge(s_full, b * PAIRS_B + (m + 1))
                    if not (isinstance(b, int) and b * PAIRS_B + m < RING_B):
                        act.wait_ge(o_full, b * PAIRS_B + (m + 1 - RING_B))
                    nc.scalar.activation(pclip[m % RING_B][:], ps[:, 2 * (m % 2):2 * (m % 2) + 2, :].rearrange("p n (r t) -> p n r t", r=2),
                                         ACT.Exp, scale=SCALE_B).then_inc(s_exp, 1)
                    if m == 1 and not last:
                        split_tokens(b + 1, 1 - par)
                    for what, j, ahead in jobs_with(m, last):
                        copy_proj(job_count(b, 0, last) + n, n, what, j, 1 - par)
                        n += 1
                    if m >= LAG_B + 1:
                        copy_oT(b, par, m - LAG_B - 1)
                    elif not first:
                        copy_oT(b - 1, 1 - par, PAIRS_B - LAG_B - 1 + m)

            batch_pairs(act, step)
            for m in range(PAIRS_B - LAG_B - 1, PAIRS_B):
                copy_oT(BATCH - 1, (BATCH - 1) % 2, m)
            load_table(ACT.Sqrt)

            act.wait_ge(w1T_full, 1)
            nc.scalar.activation(wlT[:], ps[:, 4, 0:P], ACT.Copy)
            nc.scalar.activation(gl[:, 0:EXPERTS], ps[:, 4, P:P + EXPERTS], ACT.Copy).then_inc(w1T_out, 1)
            root(3)
            for n in range(CHUNKS):
                act.wait_ge(xT_full, 2 * CHUNKS + n + 1)
                nc.scalar.activation(xT3[:, TPK * n:TPK * n + TPK, :], ps[:, n, :], ACT.Copy).then_inc(xT_out, 1)
            load_table(ACT.Exp)
            act.wait_ge(sc_shifted, 1)
            nc.scalar.activation(sc[:], sc[:], ACT.Exp).then_inc(sc_exp, 1)
            for n in range(CHUNKS):
                act.wait_ge(base_full, n + 1)
                nc.scalar.activation(base[:, TPK * n:TPK * n + TPK, :], ps[:, n, :], ACT.Copy, scale=tg[:, 3:4]).then_inc(base_out, 1)
            act.wait_ge(twT_full, 1)
            nc.scalar.activation(twT[:], ps[:, 4, :], ACT.Copy).then_inc(twT_out, 1)

        @block.vector
        def _(dve):
            c = Chain(dve, dve_self)
            nc.vector.memset(eps[:, 0:1], EPS)
            nc.vector.memset(eps[:, 1:2], EPS * EPS)

            def stats(src, tiles=range(TILES)):
                for t in tiles:
                    last = nc.vector.bn_stats(stat[:, t, :], src[:, t, :])
                return last

            def variances(last):
                c.link(last)
                for t in range(TILES):
                    last = nc.vector.bn_aggr(mv[:, t, :], stat[:, t, :])
                last.then_inc(var_ready, 1)

            def norm(n, src, dst):
                dve.wait_ge(std_ready, n + 1)
                c.link(nc.vector.reciprocal(rstd[:], std[:]))
                for t in range(TILES):
                    last = nc.vector.tensor_scalar(dst[:, t, :], src[:, t, :], mv[:, t, 0:1], rstd[:, t:t + 1], ALU.subtract, ALU.mult)
                    if t % TPK == TPK - 1:
                        last.then_inc(xn_ready, 1)

            dve.wait_ge(ld_x, 16 * CHUNKS)
            variances(stats(x))
            norm(0, x, xn)
            dve.wait_ge(ld_small, 16 * 6)
            c.link(nc.vector.tensor_tensor(lam_pr[:], lam_in[:, 0:4:2, :], lam_in[:, 1:4:2, :], ALU.mult))
            nc.vector.tensor_reduce(lam_s[:], lam_pr[:], AX.X, ALU.add).then_inc(lam_sum, 1)

            for n in range(CHUNKS):
                cols = slice(BANK * n, BANK * n + BANK)
                for side, what in enumerate("qk"):
                    dve.wait_ge(job_out, job_at[(what, n)] + 1)
                    whole, r = qk32[:, side, cols], res[:, side, :]
                    c.link(nc.vector.tensor_copy(parts[:, side, 0, cols], whole))
                    c.link(nc.vector.tensor_tensor(r, whole, parts[:, side, 0, cols], ALU.subtract))
                    c.link(nc.vector.tensor_copy(parts[:, side, 1, cols], r))
                    nc.vector.tensor_tensor(parts[:, side, 2, cols], r, parts[:, side, 1, cols], ALU.subtract).then_inc(qk_split, 1)
            dve.wait_ge(lam_exp, 1)
            c.link(nc.vector.tensor_tensor(lam[:], lam_e[:, 0:1], lam_e[:, 1:2], ALU.subtract))
            c.link(nc.vector.tensor_scalar(lam[:], lam[:], LAMBDA_INIT, -1.0, ALU.add, ALU.mult))
            nc.vector.tensor_copy(coef[:, 0:1], tg[:, 0:1])
            c.link(nc.vector.tensor_tensor(coef[:, 1:2], lam[:], tg[:, 0:1], ALU.mult))

            def max_a(b, a):
                g, r = a // ROWT, a % ROWT
                dve.wait_ge(a_full, b * A_TILES + (a + 1))
                nc.vector.tensor_reduce(nmax[g // HALF][:, :, r, g % HALF],
                                        ps[:, BANK_A[a % 2], :].rearrange("p (t n) -> p t n", t=TPB),
                                        AX.X, ALU.max, negate=True).then_inc(a_used, 1)

            def split_max(b, half):
                dve.wait_ge(a_used, b * A_TILES + (half + 1) * (A_TILES // 2))
                whole = nmax[half][:].rearrange("p t r g -> p (t r) g")
                part = mpart[half][:].rearrange("p t r m g -> p (t r) m g")
                c.link(nc.vector.tensor_copy(part[:, :, 0, :], whole))
                nc.vector.tensor_tensor(part[:, :, 1, :], whole, part[:, :, 0, :], ALU.subtract).then_inc(m_split, 1)

            def combine(b, s, n):
                raw = oraw[s][:].rearrange("p a q (two c) -> p (a q two) c", two=2)
                part = [raw[:, :, HEADW_A * i:HEADW_A * (i + 1)] for i in range(VPARTS)]
                o = ov[:].rearrange("p a two w -> p (a two) w")
                r = rs[:].rearrange("p a two -> p (a two)")
                xb = x[:, bass.ds(b * TPB, TPB), :].rearrange("p t (h w) -> p (t h) w", w=HEADW_A)
                if n == 0:
                    dve.wait_ge(o_saved, b * 4 + 4)
                c.follow()
                if n == 0:
                    c.mark(nc.vector.tensor_tensor(o, part[1], part[2], ALU.add))
                if n == 1:
                    c.mark(nc.vector.tensor_tensor(o, o, part[0], ALU.add))
                if n == 2:
                    c.mark(nc.vector.reciprocal(r, raw[:, :, VCOLS - 1]))
                if n == 3:
                    c.mark(nc.vector.tensor_tensor(rs[:], rs[:], coef[:].unsqueeze(1).broadcast_to([P, TPB * ROWT * 4, 2]), ALU.mult))
                if n == 4:
                    c.mark(nc.vector.tensor_tensor(o, o, r.unsqueeze(2).broadcast_to([P, TPB * ROWT * 8, HEADW_A]), ALU.mult))
                if n == 5:
                    c.mark(nc.vector.tensor_tensor(ov[:, :, 0, :], ov[:, :, 0, :], ov[:, :, 1, :], ALU.add))
                if n == 6:
                    c.mark(nc.vector.tensor_tensor(xb, xb, ov[:, :, 0, :], ALU.add))

            for a in range(A_TILES):
                max_a(0, a)
                if a == A_TILES // 2 - 1:
                    split_max(0, 0)
            split_max(0, 1)

            def step(b, s, turn, first, last):
                for k in range(B_TILES):
                    if not last:
                        max_a(b + 1, 2 * k)
                        max_a(b + 1, 2 * k + 1)
                        if k == B_TILES // 2 - 1:
                            split_max(b + 1, 0)
                        if k == B_TILES - 1:
                            split_max(b + 1, 1)
                    if lo_on_vector(b, k):
                        dve.wait_ge(exp_done, b * B_TILES + (k + 1))
                        nc.vector.tensor_tensor(plo[k % PRING][:], pexp[k % PRING][:], hi_of(k), ALU.subtract).then_inc(lo_dve, 1)
                    if 0 <= k - COMBINE_AT < COMBINE_LINKS and not first:
                        combine(b - 1, (s - 1) % SLOTS, k - COMBINE_AT)
                    if last and k < COMBINE_AT:
                        stats(x, range(TILES - 2 * TPB)[k::COMBINE_AT])
                    if last and k < B_TILES // 2:
                        for t in (2 * k, 2 * k + 1):
                            nc.vector.bn_stats(stat_c[:, t, :], cx[:, t, :])
                    if last and k == B_TILES - 1:
                        c.follow()
                        for t in range(TILES):
                            var = nc.vector.bn_aggr(mv_c[:, t, :], stat_c[:, t, :])
                        var.then_inc(ctx_var, 1)
                        stats(x, range(TILES - 2 * TPB, TILES - TPB))

            batches(dve, step, c, COMBINE_LINKS + 2)
            for n in range(COMBINE_LINKS):
                combine(BATCH - 1, (BATCH - 1) % SLOTS, n)
            dve.wait_ge(dve_self, c.n)

            dve.wait_ge(aug_loaded[2], 3 * 16 * LOADS)
            nc.vector.tensor_copy(lam[:], lam[:]).then_inc(x1_ready, 1)
            variances(stats(x, range(TILES - TPB, TILES)))
            norm(1, x, xn1)
            wide = [P, TILES, EXPERTS]
            over_e = lambda ap: ap.unsqueeze(2).broadcast_to(wide)
            dve.wait_ge(logits_full, 1)
            dve.wait_ge(ld_ffn, 16 * 4)
            c.link(nc.vector.tensor_tensor(lg[:], ps[:, 5, 0:TILES * EXPERTS].rearrange("p (t e) -> p t e", e=EXPERTS),
                                           gate_b[:].unsqueeze(1).broadcast_to(wide), ALU.add))
            c.link(nc.vector.tensor_reduce(t16[:], lg[:], AX.X, ALU.max))
            nc.vector.tensor_tensor(lg[:], lg[:], over_e(t16[:]), ALU.subtract).then_inc(logits_max, 1)
            dve.wait_ge(logits_exp, 1)
            c.link(nc.vector.tensor_reduce(t16[:], lg[:], AX.X, ALU.add))
            c.link(nc.vector.reciprocal(t16[:], t16[:]))
            c.link(nc.vector.tensor_tensor(lg[:], lg[:], over_e(t16[:]), ALU.mult))
            c.link(nc.vector.tensor_reduce(gprob[:], lg[:], AX.X, ALU.max))
            c.link(nc.vector.tensor_tensor(ne[:], lg[:], over_e(gprob[:]), ALU.is_lt))
            dve.wait_ge(ffn_consts, 1)
            c.link(nc.vector.scalar_tensor_tensor(ne[:], ne[:], float(EXPERTS), iota_e[:], ALU.mult, ALU.add))
            c.link(nc.vector.tensor_reduce(t16[:], ne[:], AX.X, ALU.min))
            c.link(nc.vector.tensor_tensor(mask[:].rearrange("p e t -> p t e"), iota_e[:], over_e(t16[:]), ALU.is_equal))
            c.link(nc.vector.tensor_tensor_scan(upto[:].rearrange("p e t -> p (e t)"), keep_sum[:].rearrange("p e t -> p (e t)"),
                                                mask[:].rearrange("p e t -> p (e t)"), 0.0, ALU.mult, ALU.add))
            nc.vector.tensor_tensor(prior[:], upto[:], mask[:], ALU.subtract).then_inc(mask_ready, 1)
            dve.wait_ge(rank_full, 1)
            rank = ps[:, 6, 0:EXPERTS * TILES].rearrange("p (e t) -> p e t", e=EXPERTS)
            c.link(nc.vector.tensor_scalar(over[:], rank, float(CAP), float(EROWS), ALU.is_ge, ALU.mult))
            c.link(nc.vector.tensor_tensor(over[:], over[:], rank, ALU.add))
            c.link(nc.vector.tensor_tensor(over[:], over[:], place0[:], ALU.add))
            c.link(nc.vector.tensor_tensor(over[:], over[:], mask[:], ALU.mult))
            nc.vector.tensor_reduce(place[:], over[:].rearrange("p e t -> p t e"), AX.X, ALU.add).then_inc(place_ready, 1)
            dve.wait_ge(place_ready, 1)
            for t in range(TILES):
                if t >= 4:
                    dve.wait_ge(onehot_used, t - 3)
                nc.vector.tensor_scalar(onehot[t % 4][:], places[:], place[:, t:t + 1], None, ALU.is_equal).then_inc(onehot_ready, 1)
            c.link(nc.vector.tensor_scalar(gprob[:], gprob[:], tg[:, 2:3], None, ALU.mult))
            dve.wait_ge(bT_out, 1)
            for e in range(EXPERTS):
                dve.wait_ge(h_full, e + 1)
                nc.vector.tensor_tensor(hidden[:, FCH * e:FCH * e + FCH, :], ps[:, e % 4, 0:FCH * CAP].rearrange("p (f c) -> p f c", f=FCH),
                                        b1T[:, FCH * e:FCH * e + FCH].unsqueeze(2).broadcast_to([P, FCH, CAP]), ALU.add).then_inc(h_biased, 1)
                if e == EXPERTS - ECH:
                    dve.wait_ge(row_out, CHUNKS)
                if e >= EXPERTS - ECH:
                    j = e - (EXPERTS - ECH)
                    nc.vector.tensor_scalar(onehotT[:, j, :], place_row[:], place_p[:, j:j + 1], None, ALU.is_equal).then_inc(onehotT_ready, 1)
            dve.wait_ge(ctx_std, 1)
            c.link(nc.vector.reciprocal(rstd_c[:], std_c[:]))
            for t in range(TILES):
                last = nc.vector.tensor_scalar(cx[:, t, :], cx[:, t, :], mv_c[:, t, 0:1], rstd_c[:, t:t + 1], ALU.subtract, ALU.mult)
                if t % TPK == TPK - 1:
                    last.then_inc(cx_normed, 1)
            for half in range(2):
                dve.wait_ge(y_full, half + 1)
                nc.vector.tensor_tensor(yT[:, EHALF * half:EHALF * half + EHALF].rearrange("p (e c) -> p e c", c=CAP),
                                        ps[:, 6 + half, 0:EHALF].rearrange("p (e c) -> p e c", c=CAP),
                                        b2T[:, 4 * half:4 * half + 4].unsqueeze(2).broadcast_to([P, 4, CAP]), ALU.add).then_inc(y_biased, 1)
            dve.wait_ge(yrow_out, 1)
            c.link(nc.vector.tensor_copy(ypart[:, 0], yrow[:]))
            c.link(nc.vector.tensor_tensor(yres[:], yrow[:], ypart[:, 0], ALU.subtract))
            c.link(nc.vector.tensor_copy(ypart[:, 1], yres[:]))
            nc.vector.tensor_tensor(ypart[:, 2], yres[:], ypart[:, 1], ALU.subtract).then_inc(y_split, 1)
            for t in range(TILES + 1):
                if t < TILES:
                    dve.wait_ge(moe_full, t + 1)
                    nc.vector.scalar_tensor_tensor(x[:, t, :], ps[:, t % 4, 0:DIM], gprob[:, t:t + 1], x[:, t, :], ALU.mult, ALU.add).then_inc(moe_used, 1)
                if t > 0:
                    dve.wait_ge(moe_used, t)
                    last = nc.vector.bn_stats(stat[:, t - 1, :], x[:, t - 1, :])

            variances(last)
            norm(2, x, xn2)
            low, high = exp(-CLIP), exp(CLIP)

            def split_tokens(b, par):
                dve.wait_ge(tok_high, b + 1)
                if isinstance(b, int) and b == 0:
                    for side, src in enumerate((latT, cT)):
                        last = nc.vector.tensor_tensor(tok_parts[par][1][:, side, :], first_tokens(src), tok_parts[par][0][:, side, :], ALU.subtract)
                    last.then_inc(tok_split, 1)
                    return
                nc.vector.tensor_tensor(tok_parts[par][1][:], tok_b[par][:], tok_parts[par][0][:], ALU.subtract).then_inc(tok_split, 1)

            def copy_proj(count, n, what, j, b, par):
                dve.wait_ge(proj_high, count + 1)
                if what == "qk":
                    for dst, src in qk_pieces(n, j):
                        last = nc.vector.tensor_tensor(dst[1], src, dst[0], ALU.subtract)
                    last.then_inc(proj_used, 1)
                    return
                if not (isinstance(b, int) and b * JOBS_V + j < 2):
                    dve.wait_ge(v1_split, b * JOBS_V + (j - 1))
                rest = by_head(v1res[j % 2][:])
                nc.vector.tensor_tensor(rest, by_head(proj_bank(n)), v_piece(par, j, 0), ALU.subtract).then_inc(proj_used, 1)
                dve.wait_ge(proj_used, count + 1)
                nc.vector.tensor_copy(v_piece(par, j, VMID_B), rest).then_inc(v1_mid, 1)

            def norm_o(b, m):
                dve.wait_ge(o_full, b * PAIRS_B + (m + 1))
                src = ps[:, 4, 0:2 * TPB * HEADC_B].rearrange("p (a c) -> p a c", c=HEADC_B)
                c.link(nc.vector.reciprocal(rsum[m % 2][:], src[:, :, HEADW_B]))
                nc.vector.tensor_tensor(on[m % 2][:].rearrange("p t r d -> p (t r) d"), src[:, :, 0:HEADW_B],
                                        rsum[m % 2][:].unsqueeze(2).broadcast_to([P, 2 * TPB, HEADW_B]),
                                        ALU.mult).then_inc(o_norm, 1)

            def add_output(b):
                dve.wait_ge(out_full, b + 1)
                c.link(nc.vector.tensor_tensor(ysum[:], ps[:, 6, 0:SEQ].rearrange("p (t d) -> p t d", t=TPB),
                                               bo1[:].unsqueeze(1).broadcast_to([P, TPB, DIM]), ALU.add))
                xb = x[:, bass.ds(b * TPB, TPB), :]
                nc.vector.scalar_tensor_tensor(xb, ysum[:], tg[:, 1:2], xb, ALU.mult, ALU.add).then_inc(out_used, 1)

            dve.wait_ge(ones1_ready, 1)
            split_tokens(0, 0)
            for n, (what, j) in enumerate(JOBS_FIRST):
                copy_proj(n, n, what, j, 0, 0)

            def tail(b, par, m, first):
                if m == LAG_B + 1 and not first:
                    add_output(b - 1)
                if m >= LAG_B:
                    norm_o(b, m - LAG_B)
                elif not first:
                    norm_o(b - 1, PAIRS_B - LAG_B + m)

            def step(b, par, first, last):
                for m in range(PAIRS_B):
                    dve.wait_ge(s_exp, b * PAIRS_B + (m + 1))
                    nc.vector.tensor_scalar(pclip[m % RING_B][:], pclip[m % RING_B][:], low, high, ALU.max, ALU.min).then_inc(s_clip, 1)
                    if m == 1 and not last:
                        split_tokens(b + 1, 1 - par)
                    for i, (what, j, ahead) in enumerate(jobs_with(m, last)):
                        if i == 1:
                            tail(b, par, m, first)
                        copy_proj(job_count(b, m, last) + i, job_count(0, m, last) + i, what, j, b + ahead, 1 - par)
                    if len(jobs_with(m, last)) < 2:
                        tail(b, par, m, first)
                    if last and m > LAG_B + 1:
                        dve.wait_ge(out_used, BATCH - 1)
                        stats(x, range(TILES - TPB)[m - LAG_B - 2::PAIRS_B - LAG_B - 2])

            batch_pairs(dve, step, c, PAIRS_B + 1)
            norm_o(BATCH - 1, PAIRS_B - 2)
            norm_o(BATCH - 1, PAIRS_B - 1)
            add_output(BATCH - 1)
            dve.wait_ge(out_used, BATCH)
            variances(stats(x, range(TILES - TPB, TILES)))

            norm(3, x, xn3)
            dve.wait_ge(lt_full, 1)
            for half in range(2):
                last = nc.vector.tensor_copy(lt[:, 8 * half:8 * half + 8, :],
                                             ps[:, 5 + half, 0:8 * (EXPERTS + ER)].rearrange("p (t n) -> p t n", t=8))
            c.link(last)
            logits = lt[:, :, 0:EXPERTS]
            c.link(nc.vector.tensor_reduce(u16[:], logits, AX.X, ALU.max))
            nc.vector.tensor_tensor(sc[:], logits, over_e(u16[:]), ALU.subtract).then_inc(sc_shifted, 1)
            dve.wait_ge(sc_exp, 1)
            c.link(nc.vector.tensor_reduce(u16[:], sc[:], AX.X, ALU.add))
            c.link(nc.vector.reciprocal(u16[:], u16[:]))
            c.link(nc.vector.tensor_tensor(sc[:], sc[:], over_e(u16[:]), ALU.mult))
            left = sc
            for n in range(2):
                c.link(nc.vector.tensor_reduce(u16[:], left[:], AX.X, ALU.max))
                c.link(nc.vector.tensor_tensor(cand[:], left[:], over_e(u16[:]), ALU.is_lt))
                c.link(nc.vector.scalar_tensor_tensor(cand[:], cand[:], float(EXPERTS), iota_e[:], ALU.mult, ALU.add))
                c.link(nc.vector.tensor_reduce(u16[:], cand[:], AX.X, ALU.min))
                c.link(nc.vector.tensor_tensor(best[:, n], iota_e[:], over_e(u16[:]), ALU.is_equal))
                if n == 0:
                    c.link(nc.vector.scalar_tensor_tensor(rest[:], best[:, 0], -2.0, sc[:], ALU.mult, ALU.add))
                    left = rest
            c.link(nc.vector.tensor_tensor(cand[:], best[:, 0], best[:, 1], ALU.add))
            c.link(nc.vector.tensor_tensor(cand[:], cand[:], sc[:], ALU.mult))
            nc.vector.tensor_tensor(tw[:].rearrange("p t (e r) -> p t e r", r=RANK),
                                    lt[:, :, EXPERTS:].rearrange("p t (e r) -> p t e r", r=RANK),
                                    cand[:].unsqueeze(3).broadcast_to([P, TILES, EXPERTS, RANK]), ALU.mult).then_inc(tw_ready, 1)
            for n in range(CHUNKS):
                tiles = slice(TPK * n, TPK * n + TPK)
                dve.wait_ge(base_added, n + 1)
                dve.wait_ge(lin_full, n + 1)
                nc.vector.scalar_tensor_tensor(x[:, tiles, :], ps[:, n, :].rearrange("p (t d) -> p t d", t=TPK), tg[:, 3:4], x[:, tiles, :],
                                               ALU.mult, ALU.add).then_inc(lin_used, 1)


INPUTS = ['x', 'ctx_1024', 'g_xattn', 'g_ffn', 'L0_xattn_Wq', 'L0_xattn_Wk', 'L0_xattn_Wv', 'L0_xattn_lambda_q1',
          'L0_xattn_lambda_q2', 'L0_xattn_lambda_k1', 'L0_xattn_lambda_k2', 'L0_ffn_gate_w', 'L0_ffn_gate_b',
          'L0_ffn_w1', 'L0_ffn_b1', 'L0_ffn_w2', 'L0_ffn_b2', 'L1_xattn_ln_l_w', 'L1_xattn_ln_l_b',
          'L1_xattn_ln_c_w', 'L1_xattn_ln_c_b', 'L1_xattn_Wq', 'L1_xattn_Wkv', 'L1_xattn_Wo', 'L1_xattn_bo',
          'L1_ffn_W_lin', 'L1_ffn_b_lin', 'L1_ffn_gate_w', 'L1_ffn_left', 'L1_ffn_right']


def kernel(**inputs):
    import numpy as np
    import concourse.bacc as bacc
    from concourse.bass_utils import run_bass_kernel_spmd

    nc = bacc.Bacc("TRN2", target_bir_lowering=False, num_devices=1)
    arrays, args = {}, {}
    for name in INPUTS:
        a = np.ascontiguousarray(inputs[name])
        arrays["in_" + name] = a
        args[name] = nc.dram_tensor("in_" + name, a.shape, mybir.dt.from_np(a.dtype), kind="ExternalInput").ap()
    out = nc.dram_tensor("out", (BATCH, SEQ, DIM), F32, kind="ExternalOutput").ap()
    build(nc, args, out)
    r = run_bass_kernel_spmd(nc, [arrays], core_ids=[0])
    return r.results[0]["out"]
```
